# Optimizing a Trainium2 kernel written in Bass

```python
import numpy as np
import jax
import jax.numpy as jnp

def _softmax(x, axis=-1):
    return jax.nn.softmax(x, axis=axis)

def _gelu(x):
    return jax.nn.gelu(x, approximate=True)

def _silu(x):
    return jax.nn.silu(x)

def _sigmoid(x):
    return jax.nn.sigmoid(x)

def _layernorm(x, axis=-1, eps=1e-05):
    m = jnp.mean(x, axis=axis, keepdims=True)
    v = jnp.var(x, axis=axis, keepdims=True)
    return (x - m) / jnp.sqrt(v + eps)

def _scatter_add(tgt, idx, src, axis=0):
    return tgt.at[idx].add(src)

def _segment_sum(src, seg, n):
    return jax.ops.segment_sum(src, seg, n)
kernel_name = 'mk_seq_preln_d2_jaxref_r8_af146f'

def setup_inputs(seed: int=0):
    np.random.seed(seed)
    _w = jnp.asarray

    def _L0_attn_setup():
        import math
        import jax, jax.numpy as jnp
        import numpy as np
        NUM_BUCKETS = 32
        MAX_DISTANCE = 128
        HEADS = 16
        D_MODEL = 128
        SEQ = 128
        BATCH = 4
        SCALE = (D_MODEL // HEADS) ** (-0.5)

        def _rel_pos_bucket_causal(seq_len):
            pos = jnp.arange(seq_len)
            n = jnp.maximum(pos[:, None] - pos[None, :], 0)
            max_exact = NUM_BUCKETS // 2
            val_large = max_exact + (jnp.log(jnp.maximum(n, 1).astype(jnp.float32) / max_exact) / math.log(MAX_DISTANCE / max_exact) * (NUM_BUCKETS - max_exact)).astype(jnp.int32)
            val_large = jnp.minimum(val_large, NUM_BUCKETS - 1)
            return jnp.where(n < max_exact, n, val_large)
        key = jax.random.key(seed)
        ks = jax.random.split(key, 6)
        s = 0.02
        return {'x': jax.random.normal(ks[0], (BATCH, SEQ, D_MODEL), jnp.float32), 'Wq': jax.random.normal(ks[1], (D_MODEL, D_MODEL), jnp.float32) * s, 'bq': jnp.zeros((D_MODEL,), jnp.float32), 'Wk': jax.random.normal(ks[2], (D_MODEL, D_MODEL), jnp.float32) * s, 'bk': jnp.zeros((D_MODEL,), jnp.float32), 'Wv': jax.random.normal(ks[3], (D_MODEL, D_MODEL), jnp.float32) * s, 'bv': jnp.zeros((D_MODEL,), jnp.float32), 'Wo': jax.random.normal(ks[4], (D_MODEL, D_MODEL), jnp.float32) * s, 'bo': jnp.zeros((D_MODEL,), jnp.float32), 'rel_emb': jax.random.normal(ks[5], (NUM_BUCKETS, HEADS), jnp.float32) * s}
    _L0_attn_in = _L0_attn_setup()

    def _L0_ffn_setup():
        import jax, jax.numpy as jnp
        import numpy as np
        LATENT = 128
        LEAF_W = 64
        DEPTH = 4
        N_LEAVES = 2 ** DEPTH
        N_NODES = 2 ** DEPTH - 1
        B, S = (4, 256)

        def _fff_params(key, prefix):
            ks = jax.random.split(key, 4)
            d, h, l, n = (LATENT, LEAF_W, N_LEAVES, N_NODES)
            s_in = 1.0 / np.sqrt(d).astype(np.float32)
            s_h = 1.0 / np.sqrt(h).astype(np.float32)
            return {f'{prefix}_node_w': jax.random.normal(ks[0], (n, d), jnp.float32) * s_in, f'{prefix}_node_b': jax.random.normal(ks[1], (n,), jnp.float32) * s_in, f'{prefix}_w1': jax.random.normal(ks[2], (l, d, h), jnp.float32) * s_in, f'{prefix}_b1': jnp.zeros((l, h), jnp.float32), f'{prefix}_w2': jax.random.normal(ks[3], (l, h, d), jnp.float32) * s_h, f'{prefix}_b2': jnp.zeros((l, d), jnp.float32)}

        def _fff(x, node_w, node_b, w1, b1, w2, b2):
            Bx, Sx, D = x.shape
            xf = x.reshape(-1, D)
            N = xf.shape[0]
            cur = jnp.zeros((N,), jnp.int32)
            for _ in range(DEPTH):
                pw = node_w[cur]
                score = jnp.einsum('nd,nd->n', xf, pw) + node_b[cur]
                cur = 2 * cur + 1 + (score >= 0).astype(jnp.int32)
            leaf = cur - N_NODES
            sel = jax.nn.one_hot(leaf, N_LEAVES, dtype=xf.dtype)
            hidden_all = jax.nn.relu(jnp.einsum('nd,ldh->lnh', xf, w1) + b1[:, None, :])
            hidden = hidden_all * sel.T[:, :, None]
            out = jnp.einsum('lnh,lho->no', hidden, w2) + sel @ b2
            return out.reshape(Bx, Sx, D)
        key = jax.random.key(seed)
        kx, kq, kk, kv = jax.random.split(key, 4)
        inp = {'x': jax.random.normal(kx, (B, S, LATENT), jnp.float32)}
        inp.update(_fff_params(kq, 'q'))
        inp.update(_fff_params(kk, 'k'))
        inp.update(_fff_params(kv, 'v'))
        return inp
    _L0_ffn_in = _L0_ffn_setup()

    def _L1_attn_setup():
        import jax, jax.numpy as jnp
        import numpy as np
        import math
        DIM = 128
        HEADS = 16
        HEAD_DIM = DIM // HEADS
        B, N = (1, 512)
        key = jax.random.key(seed)
        k1, k2, k3, k4 = jax.random.split(key, 4)
        content = jax.random.normal(k1, (B, N, DIM), dtype=jnp.float32)
        Wq = jnp.eye(DIM, dtype=jnp.float32) + 0.02 * jax.random.normal(k2, (DIM, DIM), dtype=jnp.float32)
        Wk = jnp.eye(DIM, dtype=jnp.float32) + 0.02 * jax.random.normal(k3, (DIM, DIM), dtype=jnp.float32)
        Wv = jnp.eye(DIM, dtype=jnp.float32) + 0.02 * jax.random.normal(k4, (DIM, DIM), dtype=jnp.float32)
        return {'content': content, 'Wq': Wq, 'Wk': Wk, 'Wv': Wv}
    _L1_attn_in = _L1_attn_setup()

    def _L1_ffn_setup():
        import jax, jax.numpy as jnp
        import numpy as np
        DIM = 128

        def _reference_tuple_inner(x, W_r, W_k, W_v, mu_r, mu_k):
            B, T, C = x.shape
            x_prev = jnp.concatenate([jnp.zeros((B, 1, C), x.dtype), x[:, :-1, :]], axis=1)
            xr = mu_r * x + (1.0 - mu_r) * x_prev
            xk = mu_k * x + (1.0 - mu_k) * x_prev
            r = jax.nn.sigmoid(jnp.einsum('btc,dc->btd', xr, W_r))
            k = jnp.einsum('btc,dc->btd', xk, W_k)
            k_act = jnp.square(jax.nn.relu(k))
            out = r * jnp.einsum('btc,dc->btd', k_act, W_v)
            new_state = x[:, -1, :]
            return (out, new_state)
        key = jax.random.key(seed)
        ks = jax.random.split(key, 6)
        B, T, C = (8, 256, DIM)
        x = jax.random.normal(ks[0], (B, T, C), dtype=jnp.float32)
        s = 1.0 / np.sqrt(C)
        W_r = jax.random.uniform(ks[1], (C, C), jnp.float32, -s, s)
        W_k = jax.random.uniform(ks[2], (C, C), jnp.float32, -s, s)
        W_v = jax.random.uniform(ks[3], (C, C), jnp.float32, -s, s)
        mu_r = jax.random.uniform(ks[4], (C,), jnp.float32)
        mu_k = jax.random.uniform(ks[5], (C,), jnp.float32)
        return {'x': x, 'W_r': W_r, 'W_k': W_k, 'W_v': W_v, 'mu_r': mu_r, 'mu_k': mu_k}
    _L1_ffn_in = _L1_ffn_setup()
    _d = {'L0_attn_x': _L0_attn_in['x'], 'L0_attn_Wq': _L0_attn_in['Wq'], 'L0_attn_bq': _L0_attn_in['bq'], 'L0_attn_Wk': _L0_attn_in['Wk'], 'L0_attn_bk': _L0_attn_in['bk'], 'L0_attn_Wv': _L0_attn_in['Wv'], 'L0_attn_bv': _L0_attn_in['bv'], 'L0_attn_Wo': _L0_attn_in['Wo'], 'L0_attn_bo': _L0_attn_in['bo'], 'L0_attn_rel_emb': _L0_attn_in['rel_emb'], 'L0_ffn_q_node_w': _L0_ffn_in['q_node_w'], 'L0_ffn_q_node_b': _L0_ffn_in['q_node_b'], 'L0_ffn_q_w1': _L0_ffn_in['q_w1'], 'L0_ffn_q_b1': _L0_ffn_in['q_b1'], 'L0_ffn_q_w2': _L0_ffn_in['q_w2'], 'L0_ffn_q_b2': _L0_ffn_in['q_b2'], 'L0_ffn_k_node_w': _L0_ffn_in['k_node_w'], 'L0_ffn_k_node_b': _L0_ffn_in['k_node_b'], 'L0_ffn_k_w1': _L0_ffn_in['k_w1'], 'L0_ffn_k_b1': _L0_ffn_in['k_b1'], 'L0_ffn_k_w2': _L0_ffn_in['k_w2'], 'L0_ffn_k_b2': _L0_ffn_in['k_b2'], 'L0_ffn_v_node_w': _L0_ffn_in['v_node_w'], 'L0_ffn_v_node_b': _L0_ffn_in['v_node_b'], 'L0_ffn_v_w1': _L0_ffn_in['v_w1'], 'L0_ffn_v_b1': _L0_ffn_in['v_b1'], 'L0_ffn_v_w2': _L0_ffn_in['v_w2'], 'L0_ffn_v_b2': _L0_ffn_in['v_b2'], 'L1_attn_Wq': _L1_attn_in['Wq'], 'L1_attn_Wk': _L1_attn_in['Wk'], 'L1_attn_Wv': _L1_attn_in['Wv'], 'L1_ffn_W_r': _L1_ffn_in['W_r'], 'L1_ffn_W_k': _L1_ffn_in['W_k'], 'L1_ffn_W_v': _L1_ffn_in['W_v'], 'L1_ffn_mu_r': _L1_ffn_in['mu_r'], 'L1_ffn_mu_k': _L1_ffn_in['mu_k']}
    _x0 = _d['L0_attn_x']
    _d['L0_attn_x'] = jax.random.normal(jax.random.fold_in(jax.random.key(seed), 1), (4, 1024, 128), dtype=_x0.dtype)
    del _x0
    return _d

def reference(L0_attn_x, L0_attn_Wq, L0_attn_bq, L0_attn_Wk, L0_attn_bk, L0_attn_Wv, L0_attn_bv, L0_attn_Wo, L0_attn_bo, L0_attn_rel_emb, L0_ffn_q_node_w, L0_ffn_q_node_b, L0_ffn_q_w1, L0_ffn_q_b1, L0_ffn_q_w2, L0_ffn_q_b2, L0_ffn_k_node_w, L0_ffn_k_node_b, L0_ffn_k_w1, L0_ffn_k_b1, L0_ffn_k_w2, L0_ffn_k_b2, L0_ffn_v_node_w, L0_ffn_v_node_b, L0_ffn_v_w1, L0_ffn_v_b1, L0_ffn_v_w2, L0_ffn_v_b2, L1_attn_Wq, L1_attn_Wk, L1_attn_Wv, L1_ffn_W_r, L1_ffn_W_k, L1_ffn_W_v, L1_ffn_mu_r, L1_ffn_mu_k):

    def _L0_attn_ref(x, Wq, bq, Wk, bk, Wv, bv, Wo, bo, rel_emb):
        import math
        import jax, jax.numpy as jnp
        import numpy as np
        NUM_BUCKETS = 32
        MAX_DISTANCE = 128
        HEADS = 16
        D_MODEL = 128
        SEQ = 128
        BATCH = 4
        SCALE = (D_MODEL // HEADS) ** (-0.5)

        def _rel_pos_bucket_causal(seq_len):
            pos = jnp.arange(seq_len)
            n = jnp.maximum(pos[:, None] - pos[None, :], 0)
            max_exact = NUM_BUCKETS // 2
            val_large = max_exact + (jnp.log(jnp.maximum(n, 1).astype(jnp.float32) / max_exact) / math.log(MAX_DISTANCE / max_exact) * (NUM_BUCKETS - max_exact)).astype(jnp.int32)
            val_large = jnp.minimum(val_large, NUM_BUCKETS - 1)
            return jnp.where(n < max_exact, n, val_large)
        b, n, d = x.shape
        h, hd = (HEADS, d // HEADS)
        q = (x @ Wq.T + bq).reshape(b, n, h, hd).transpose(0, 2, 1, 3)
        k = (x @ Wk.T + bk).reshape(b, n, h, hd).transpose(0, 2, 1, 3)
        v = (x @ Wv.T + bv).reshape(b, n, h, hd).transpose(0, 2, 1, 3)
        sim = jnp.einsum('bhid,bhjd->bhij', q, k)
        rp_bucket = _rel_pos_bucket_causal(n)
        bias = rel_emb[rp_bucket]
        sim = sim + jnp.transpose(bias, (2, 0, 1)) * SCALE
        i = jnp.arange(n)
        causal = jnp.where(i[None, :] > i[:, None], -jnp.inf, 0.0).astype(sim.dtype)
        sim = sim + causal
        attn = jax.nn.softmax(sim, axis=-1)
        out = jnp.einsum('bhij,bhjd->bhid', attn, v)
        out = out.transpose(0, 2, 1, 3).reshape(b, n, d)
        return out @ Wo.T + bo

    def _L0_ffn_ref(x, q_node_w, q_node_b, q_w1, q_b1, q_w2, q_b2, k_node_w, k_node_b, k_w1, k_b1, k_w2, k_b2, v_node_w, v_node_b, v_w1, v_b1, v_w2, v_b2):
        import jax, jax.numpy as jnp
        import numpy as np
        LATENT = 128
        LEAF_W = 64
        DEPTH = 4
        N_LEAVES = 2 ** DEPTH
        N_NODES = 2 ** DEPTH - 1
        B, S = (4, 256)

        def _fff_params(key, prefix):
            ks = jax.random.split(key, 4)
            d, h, l, n = (LATENT, LEAF_W, N_LEAVES, N_NODES)
            s_in = 1.0 / np.sqrt(d).astype(np.float32)
            s_h = 1.0 / np.sqrt(h).astype(np.float32)
            return {f'{prefix}_node_w': jax.random.normal(ks[0], (n, d), jnp.float32) * s_in, f'{prefix}_node_b': jax.random.normal(ks[1], (n,), jnp.float32) * s_in, f'{prefix}_w1': jax.random.normal(ks[2], (l, d, h), jnp.float32) * s_in, f'{prefix}_b1': jnp.zeros((l, h), jnp.float32), f'{prefix}_w2': jax.random.normal(ks[3], (l, h, d), jnp.float32) * s_h, f'{prefix}_b2': jnp.zeros((l, d), jnp.float32)}

        def _fff(x, node_w, node_b, w1, b1, w2, b2):
            Bx, Sx, D = x.shape
            xf = x.reshape(-1, D)
            N = xf.shape[0]
            cur = jnp.zeros((N,), jnp.int32)
            for _ in range(DEPTH):
                pw = node_w[cur]
                score = jnp.einsum('nd,nd->n', xf, pw) + node_b[cur]
                cur = 2 * cur + 1 + (score >= 0).astype(jnp.int32)
            leaf = cur - N_NODES
            sel = jax.nn.one_hot(leaf, N_LEAVES, dtype=xf.dtype)
            hidden_all = jax.nn.relu(jnp.einsum('nd,ldh->lnh', xf, w1) + b1[:, None, :])
            hidden = hidden_all * sel.T[:, :, None]
            out = jnp.einsum('lnh,lho->no', hidden, w2) + sel @ b2
            return out.reshape(Bx, Sx, D)
        q = _fff(x, q_node_w, q_node_b, q_w1, q_b1, q_w2, q_b2)
        k = _fff(x, k_node_w, k_node_b, k_w1, k_b1, k_w2, k_b2)
        v = _fff(x, v_node_w, v_node_b, v_w1, v_b1, v_w2, v_b2)
        scale = 1.0 / np.sqrt(LATENT).astype(np.float32)
        attn = jax.nn.softmax(jnp.einsum('bqd,bkd->bqk', q, k) * scale, axis=-1)
        return jnp.einsum('bqk,bkd->bqd', attn, v)

    def _L1_attn_ref(content, Wq, Wk, Wv):
        import jax, jax.numpy as jnp
        import numpy as np
        import math
        DIM = 128
        HEADS = 16
        HEAD_DIM = DIM // HEADS
        B, N = (1, 512)
        b, n, d = content.shape
        Q = (content @ Wq).reshape(b, n, HEADS, HEAD_DIM)
        K = (content @ Wk).reshape(b, n, HEADS, HEAD_DIM)
        V = (content @ Wv).reshape(b, n, HEADS, HEAD_DIM)
        scores = jnp.einsum('bqhd,bkhd->bhqk', Q, K) / math.sqrt(HEAD_DIM)
        alpha = jax.nn.softmax(scores, axis=-1)
        causal = jnp.tril(jnp.ones((n, n), dtype=bool))
        alpha = jnp.where(causal, alpha, jnp.zeros((), dtype=alpha.dtype))
        Y = jnp.einsum('bhqk,bkhd->bqhd', alpha, V).reshape(b, n, d)
        return Y

    def _L1_ffn_ref(x, W_r, W_k, W_v, mu_r, mu_k):
        import jax, jax.numpy as jnp
        import numpy as np
        DIM = 128

        def _reference_tuple_inner(x, W_r, W_k, W_v, mu_r, mu_k):
            B, T, C = x.shape
            x_prev = jnp.concatenate([jnp.zeros((B, 1, C), x.dtype), x[:, :-1, :]], axis=1)
            xr = mu_r * x + (1.0 - mu_r) * x_prev
            xk = mu_k * x + (1.0 - mu_k) * x_prev
            r = jax.nn.sigmoid(jnp.einsum('btc,dc->btd', xr, W_r))
            k = jnp.einsum('btc,dc->btd', xk, W_k)
            k_act = jnp.square(jax.nn.relu(k))
            out = r * jnp.einsum('btc,dc->btd', k_act, W_v)
            new_state = x[:, -1, :]
            return (out, new_state)
        return _reference_tuple_inner(x, W_r, W_k, W_v, mu_r, mu_k)[0]
    x = L0_attn_x
    x = x + _L0_attn_ref(_layernorm(x, axis=-1), L0_attn_Wq, L0_attn_bq, L0_attn_Wk, L0_attn_bk, L0_attn_Wv, L0_attn_bv, L0_attn_Wo, L0_attn_bo, L0_attn_rel_emb)
    x = x + _L0_ffn_ref(_layernorm(x, axis=-1), L0_ffn_q_node_w, L0_ffn_q_node_b, L0_ffn_q_w1, L0_ffn_q_b1, L0_ffn_q_w2, L0_ffn_q_b2, L0_ffn_k_node_w, L0_ffn_k_node_b, L0_ffn_k_w1, L0_ffn_k_b1, L0_ffn_k_w2, L0_ffn_k_b2, L0_ffn_v_node_w, L0_ffn_v_node_b, L0_ffn_v_w1, L0_ffn_v_b1, L0_ffn_v_w2, L0_ffn_v_b2)
    x = x + _L1_attn_ref(_layernorm(x, axis=-1), L1_attn_Wq, L1_attn_Wk, L1_attn_Wv)
    x = x + _L1_ffn_ref(_layernorm(x, axis=-1), L1_ffn_W_r, L1_ffn_W_k, L1_ffn_W_v, L1_ffn_mu_r, L1_ffn_mu_k)
    return x

_drawn_inputs = setup_inputs


def setup_inputs(seed=0):
    import zlib

    import numpy as np

    out = dict(_drawn_inputs(seed))
    spreads = {'L0_attn_bq': (0.0, 0.8),
     'L0_attn_bk': (0.0, 0.8),
     'L0_attn_bv': (0.0, 0.1),
     'L0_attn_bo': (0.0, 0.1),
     'L0_ffn_q_b1': (0.0, 0.8),
     'L0_ffn_q_b2': (0.0, 0.8),
     'L0_ffn_k_b1': (0.0, 0.8),
     'L0_ffn_k_b2': (0.0, 0.8),
     'L0_ffn_v_b1': (0.0, 0.43),
     'L0_ffn_v_b2': (0.0, 0.1)}
    factors = {'L0_attn_Wq': 8.0,
     'L0_attn_Wk': 8.0,
     'L0_attn_Wv': 8.0,
     'L0_attn_rel_emb': 8.0,
     'L0_ffn_q_node_w': 4.807,
     'L0_ffn_q_node_b': 8.0,
     'L0_ffn_q_w1': 5.562,
     'L0_ffn_q_w2': 4.578,
     'L0_ffn_k_node_w': 4.636,
     'L0_ffn_k_node_b': 8.0,
     'L0_ffn_k_w1': 5.5,
     'L0_ffn_k_w2': 4.613,
     'L1_ffn_W_r': 4.015,
     'L1_ffn_mu_r': 8.0}
    for name, (base, spread) in spreads.items():
        noise = np.random.default_rng([zlib.crc32(name.encode()), seed]).standard_normal(out[name].shape)
        drawn = base * np.exp(spread * noise) if base else spread * noise
        out[name] = jnp.asarray(drawn.astype(out[name].dtype))
    for name, factor in factors.items():
        out[name] = (out[name] * factor).astype(out[name].dtype)
    return out
```

```python
from contextlib import ExitStack

import concourse.bass as bass
from concourse import mybir

ALU = mybir.AluOpType
ACT = mybir.ActivationFunctionType
AXX = mybir.AxisListType.X
F32 = mybir.dt.float32
BF16 = mybir.dt.bfloat16

P = 128
B = 4
T = 1024
D = 128
HEADS = 16
HD = D // HEADS
NT = B * T // P
TPB = T // P
CH = 512
TPC = CH // P
CPB = T // CH
NCH = B * T // CH
EPS = 1e-5
PARTS = 3
SROWS = PARTS * PARTS * HD
MROW = SROWS
HSZ = PARTS * HD * T
BUCKETS = 32
MAX_DIST = 128
NEAR = 2 * P
ERW = 3 * P
NEG = -1.0e30
HEAD_SCALE = HD ** -0.5
LEAVES = 16
NODES = 15
DEPTH = 4
LW = 64
FF = 3
HID = LEAVES * LW // P
SELROW = 64
VW = 32


class Mem:

    def __init__(self, nc, ctx, tag):
        self.nc, self.ctx, self.tag = nc, ctx, tag

    def sb(self, name, shape, dt=F32):
        return self.ctx.enter_context(self.nc.sbuf_tensor(f"{self.tag}_{name}", shape, dt))

    def ps(self, name, shape, dt=F32):
        return self.ctx.enter_context(self.nc.psum_tensor(f"{self.tag}_{name}", shape, dt))

    def sem(self, name):
        return self.ctx.enter_context(self.nc.semaphore(f"{self.tag}_{name}"))


class Steps:

    def __init__(self, eng, sem, base=0):
        self.eng, self.sem, self.base, self.n = eng, sem, base, 0

    def did(self, ins):
        self.n += 1
        return ins.then_inc(self.sem, 1)

    def settle(self):
        self.eng.wait_ge(self.sem, self.base + self.n)

    def settle_alone(self, passed):
        wait_alone(self.eng, self.sem, self.base + self.n, passed)


def wait_alone(eng, sem, value, passed):
    eng.wait_ge(sem, value)
    eng.sem_inc(passed, 1)


def load_weights(nc, m, g, ins):
    wnat = m.sb("wnat", [P, 7, D])
    nodes_nat = m.sb("nodes_nat", [FF * NODES, D])
    rel = m.sb("rel", [BUCKETS, HEADS])
    onehot = m.sb("onehot", [BUCKETS, ERW])
    erow = m.sb("erow", [HEADS, ERW])
    identf = g["identf"]
    ebrev = m.sb("ebrev", [P, HEADS, NEAR])
    flip = m.sb("flip", [P, P])
    b2f = m.sb("b2f", [P, FF, D])
    b2d = m.sb("b2d", [P, FF, D])
    psW = m.ps("psW", [P, 8, D])
    psN = m.ps("psN", [P, 512])
    psE = m.ps("psE", [P, 512])
    psF = [m.ps(f"psF{i}", [P, CH]) for i in range(2)]
    flipped, flip_taken = m.sem("flipped"), m.sem("flip_taken")
    loaded_x, loaded_w, loaded_misc = m.sem("loaded_x"), m.sem("loaded_w"), m.sem("loaded_misc")
    loaded_b2 = m.sem("loaded_b2")
    made, zeroed = m.sem("made"), m.sem("zeroed")
    transposed, bias_ready, erow_ready = m.sem("transposed"), m.sem("bias_ready"), m.sem("erow_ready")
    erow_stored, eb_loaded = m.sem("erow_stored"), m.sem("eb_loaded")
    copied, split = m.sem("copied"), m.sem("split")
    squares = ["L0_attn_Wq", "L0_attn_Wk", "L0_attn_Wv", "L0_attn_Wo", "L1_ffn_W_r", "L1_ffn_W_k", "L1_ffn_W_v"]

    def bcast(name, parts=P):
        a = ins[name]
        n = 1
        for s in a.shape:
            n *= s
        return bass.AP(a.tensor, 0, [[0, parts], [1, n]])

    def column(name):
        return ins[name].rearrange("(d o) -> d o", o=1)

    W_N = len(squares) + FF

    with nc.Block() as block:

        @block.sync
        def _(sp):
            for i, name in enumerate(squares):
                sp.dma_start(wnat[:, i, :], ins[name]).then_inc(loaded_w, 16)
            for f, n in enumerate("qkv"):
                sp.dma_start(nodes_nat[f * NODES:(f + 1) * NODES, :], ins[f"L0_ffn_{n}_node_w"]).then_inc(loaded_w, 16)
            sp.dma_start(rel[:, :], ins["L0_attn_rel_emb"]).then_inc(loaded_misc, 16)
            sp.dma_start(onehot[:, :], ins["bucket_onehot"]).then_inc(loaded_misc, 16)
            x_t = ins["L0_attn_x"].rearrange("b (t p) d -> p (b t) d", p=P)
            for b in range(B):
                sp.dma_start(g["x"][:, b * TPB:(b + 1) * TPB, :], x_t[:, b * TPB:(b + 1) * TPB, :]).then_inc(loaded_x, 16)
            for i, name in enumerate(["L1_attn_Wq", "L1_attn_Wk", "L1_attn_Wv"]):
                sp.dma_start(g["w_c"][:, i, :], ins[name]).then_inc(loaded_x, 16)
            sp.wait_ge(loaded_w, 16 * W_N)
            sp.wait_ge(loaded_x, 16 * (B + 3))
            sp.wait_ge(erow_ready, 2)
            sp.dma_start(g["erow_dram"], erow[:, :]).then_inc(erow_stored, 16)
            sp.wait_ge(erow_stored, 16)
            sp.dma_start(ebrev[:, :, :], bass.AP(g["erow_dram"].tensor, 0, [[1, P], [ERW, HEADS], [1, NEAR]])).then_inc(eb_loaded, 16)

        @block.scalar
        def _(act):
            n = 0
            with nc.allow_non_contiguous_dma(reason="columns of biases, once"):
                for i, name in enumerate(["L0_attn_bq", "L0_attn_bk"]):
                    act.dma_start(g["bias_qk"][:, i:i + 1], column(name)).then_inc(loaded_misc, 16)
                for i, name in enumerate(["L1_ffn_mu_r", "L1_ffn_mu_k"]):
                    act.dma_start(g["mu"][:, i:i + 1], column(name)).then_inc(loaded_misc, 16)
                for f, nm in enumerate("qkv"):
                    act.dma_start(g["b1"][:, f, :], ins[f"L0_ffn_{nm}_b1"].rearrange("(m l) h -> (l h) m", l=2)).then_inc(loaded_misc, 16)
            act.dma_start(g["bv"][:, :], bcast("L0_attn_bv")).then_inc(loaded_misc, 16)
            act.dma_start(g["bo"][:, :], bcast("L0_attn_bo")).then_inc(loaded_misc, 16)
            for f, nm in enumerate("qkv"):
                act.dma_start(g["node_b"][:, f * NODES:(f + 1) * NODES], bcast(f"L0_ffn_{nm}_node_b")).then_inc(loaded_misc, 16)
                act.dma_start(g["w1"][:, f, :].rearrange("d (l h) -> d l h", l=LEAVES), ins[f"L0_ffn_{nm}_w1"].rearrange("l d h -> d l h")).then_inc(loaded_misc, 16)
                act.dma_start(g["w2"][:, f, :, :], ins[f"L0_ffn_{nm}_w2"].rearrange("(m l) h o -> (l h) m o", l=2)).then_inc(loaded_misc, 16)
            act.wait_ge(zeroed, 1)
            for f, nm in enumerate("qkv"):
                r = SELROW + f * LEAVES
                act.dma_start(b2f[r:r + LEAVES, f, :], ins[f"L0_ffn_{nm}_b2"]).then_inc(loaded_b2, 16)
            act.wait_ge(bias_ready, 1)
            act.activation(erow[:, :], psE[0:HEADS, 0:ERW], ACT.Exp, scale=HEAD_SCALE).then_inc(erow_ready, 1)
            act.wait_ge(transposed, 1)
            act.activation(g["w_a"][:, :, :], psW[:, 0:4, :], ACT.Copy).then_inc(copied, 1)
            act.activation(g["w_d"][:, :, :], psW[:, 4:7, :], ACT.Copy).then_inc(copied, 1)
            act.activation(g["node_wT"][:, :], psN[:, 0:FF * NODES], ACT.Copy).then_inc(copied, 1)
            act.wait_ge(copied, 3)
            for i in range(HEADS // 2):
                act.wait_ge(flipped, i + 1)
                act.activation(g["ebias"][:, 2 * i:2 * i + 2, :].rearrange("p h q -> p (h q)"), psF[i % 2][:, :], ACT.Copy).then_inc(flip_taken, 1)
            act.wait_ge(flip_taken, HEADS // 2)
            act.wait_ge(loaded_misc, 16 * (2 + 7 + 2 + 3 * FF))

        @block.gpsimd
        def _(pool):
            st = Steps(pool, made)
            st.did(pool.memset(identf[:, :], 0.0))
            st.did(pool.memset(g["identb"][:, :], 0.0))
            st.did(pool.memset(flip[:, :], 0.0))
            st.did(pool.memset(g["tri"][:, :], 1.0))
            st.did(pool.memset(g["maskneg"][:, :], 0.0))
            st.did(pool.memset(g["masknegT"][:, :], 0.0))
            st.did(pool.memset(g["leafx"][:, :], -NEG))
            st.settle()
            for t in (identf, g["identb"]):
                st.did(pool.affine_select(out=t[:, :], in_=t[:, :], compare_op=ALU.not_equal, fill=1.0, base=0,
                                          pattern=[[-1, P]], channel_multiplier=1))
            st.did(pool.affine_select(out=flip[:, :], in_=flip[:, :], compare_op=ALU.not_equal, fill=1.0, base=1 - P,
                                      pattern=[[1, P]], channel_multiplier=1))
            st.did(pool.affine_select(out=g["tri"][:, :], in_=g["tri"][:, :], compare_op=ALU.is_ge, fill=0.0, base=0,
                                      pattern=[[1, NEAR]], channel_multiplier=-1))
            st.did(pool.affine_select(out=g["maskneg"][:, :], in_=g["maskneg"][:, :], compare_op=ALU.is_ge, fill=NEG, base=0,
                                      pattern=[[-1, P]], channel_multiplier=1))
            st.did(pool.affine_select(out=g["masknegT"][:, :], in_=g["masknegT"][:, :], compare_op=ALU.is_ge, fill=NEG, base=0,
                                      pattern=[[1, P]], channel_multiplier=-1))
            st.did(pool.affine_select(out=g["leafx"][:, :], in_=g["leafx"][:, :], compare_op=ALU.is_ge, fill=0.0, base=0,
                                      pattern=[[1, FF * LEAVES * LW]], channel_multiplier=-LW))
            st.settle()
            st.did(pool.affine_select(out=g["leafx"][:, :], in_=g["leafx"][:, :], compare_op=ALU.is_ge, fill=0.0, base=LW - 1,
                                      pattern=[[-1, FF * LEAVES * LW]], channel_multiplier=LW))
            st.settle()

        @block.vector
        def _(dve):
            dve.memset(b2f[:, :, :], 0.0).then_inc(zeroed, 1)
            st = Steps(dve, split)
            st.did(dve.memset(g["selT"][:, :], 0.0))
            dve.wait_ge(erow_ready, 1)
            dve.memset(erow[:, 0:P - 1], 0.0).then_inc(erow_ready, 1)
            dve.wait_ge(loaded_b2, 16 * FF)
            dve.wait_ge(zeroed, 1)
            for i in range(PARTS):
                src = b2f if i == 0 else b2d
                st.did(dve.tensor_copy(g["b2p"][:, i, :, :], src[:, :, :]))
                st.settle()
                if i < PARTS - 1:
                    st.did(dve.tensor_tensor(b2d[:, :, :], src[:, :, :], g["b2p"][:, i, :, :], ALU.subtract))
                    st.settle()

        @block.tensor
        def _(pe):
            pe.wait_ge(loaded_misc, 16 * (2 + 7 + 2 + 3 * FF))
            pe.matmul(psE[0:HEADS, 0:ERW], rel[:, :], onehot[:, :], start=True, stop=True).then_inc(bias_ready, 1)
            pe.wait_ge(made, 10)
            pe.wait_ge(loaded_w, 16 * W_N)
            for i in range(7):
                pe.transpose(psW[:, i, :], wnat[:, i, :], identf[:, :])
            pe.transpose(psN[:, 0:FF * NODES], nodes_nat[:, :], identf[0:FF * NODES, 0:FF * NODES]).then_inc(transposed, 1)
            pe.wait_ge(eb_loaded, 16)
            for i in range(HEADS // 2):
                if i >= 2:
                    pe.wait_ge(flip_taken, i - 1)
                pe.matmul(psF[i % 2][:, :], flip[:, :], ebrev[:, 2 * i:2 * i + 2, :].rearrange("p h q -> p (h q)"), start=True, stop=True).then_inc(flipped, 1)


def normalise(dve, st, g, c, u, s, b):
    x, stats, mv, var, rt, nr, xn = g["x"], s["stats"], s["mv"], s["var"], s["root"], s["newton"], s["xn"]
    for t in range(TPC):
        st.did(dve.bn_stats(stats[:, u, t, :], x[:, b * TPB + u * TPC + t, :]))
    st.settle_alone(s["passed"])
    for t in range(TPC):
        st.did(dve.bn_aggr(mv[:, u, t, :], stats[:, u, t, :]))
    st.settle()
    dve.tensor_scalar(var[:, u, :], mv[:, u, :, 1], EPS, None, ALU.add).then_inc(s["var_ready"], 1)
    dve.wait_ge(s["root_ready"], c + 1)
    r, t = nr[:, u, 0, :], nr[:, u, 1, :]
    st.did(dve.reciprocal(r, rt[:, u, :]))
    st.settle()
    st.did(dve.tensor_tensor(t, r, r, ALU.mult))
    st.settle()
    st.did(dve.tensor_tensor(t, t, var[:, u, :], ALU.mult))
    st.settle()
    st.did(dve.tensor_scalar(t, t, -0.5, 1.5, ALU.mult, ALU.add))
    st.settle()
    st.did(dve.tensor_tensor(r, r, t, ALU.mult))
    st.settle()
    for t in range(TPC):
        last = dve.tensor_scalar(xn[:, u, t, :], x[:, b * TPB + u * TPC + t, :], mv[:, u, t, 0:1], nr[:, u, 0, t:t + 1],
                                 ALU.subtract, ALU.mult)
    last.then_inc(s["xn_ready"], 1)


NORM_STEPS = 2 * TPC + 5


def norm_mem(m):
    return {"stats": m.sb("stats", [P, CPB, TPC, 6]), "mv": m.sb("mv", [P, CPB, TPC, 2]),
            "var": m.sb("var", [P, CPB, TPC]), "root": m.sb("root", [P, CPB, TPC]),
            "newton": m.sb("newton", [P, CPB, 2, TPC]), "xn": m.sb("xn", [P, CPB, TPC, D]),
            "var_ready": m.sem("var_ready"), "root_ready": m.sem("root_ready"), "xn_ready": m.sem("xn_ready"), "passed": m.sem("passed")}


def project_heads(nc, m, g, w, biased):
    s = norm_mem(m)
    xnT = m.sb("xnT", [P, CPB, CH])
    qk = m.sb("qk", [P, CPB, 2, CH])
    rest = m.sb("rest", [P, CPB, 2, CH])
    parts = m.sb("parts", [P, CPB, PARTS, 2, CH], BF16)
    psT = [m.ps(f"psT{u}", [P, CH]) for u in range(CPB)]
    psQK = m.ps("psQK", [P, 2, CH])
    psV = m.ps("psV", [P, TPC, D])
    dve_steps, transposed, xnT_ready = m.sem("dve_steps"), m.sem("transposed"), m.sem("xnT_ready")
    qkv_done, qk_ready, v_taken = m.sem("qkv_done"), m.sem("qk_ready"), m.sem("v_taken")
    hi_ready, rest_ready, mid_ready, lo_ready = m.sem("hi_ready"), m.sem("rest_ready"), m.sem("mid_ready"), m.sem("lo_ready")
    stored = [m.sem(f"stored{u}") for u in range(CPB)]
    STORES = 2 * PARTS

    with nc.Block() as block:

        @block.vector
        def _(dve):
            with dve.Fori(0, B) as b:
                st = Steps(dve, dve_steps, b * (CPB * NORM_STEPS))
                for u in range(CPB):
                    c = b * CPB + u
                    normalise(dve, st, g, c, u, s, b)
                    dve.wait_ge(qkv_done, c + 1)
                    vout = g["v_all"][:, :, b, u * TPC:(u + 1) * TPC, :].rearrange("p h t e -> p t h e")
                    vin = psV[:, :, :].rearrange("p t (h e) -> p t h e", h=HEADS)
                    for t in range(TPC):
                        if biased:
                            last = dve.tensor_tensor(vout[:, t], vin[:, t], g["bv"][:, :].rearrange("p (h e) -> p h e", h=HEADS), ALU.add)
                        else:
                            last = dve.tensor_copy(vout[:, t], vin[:, t])
                    last.then_inc(v_taken, 1)
                    dve.wait_ge(hi_ready, c + 1)
                    dve.tensor_tensor(rest[:, u], qk[:, u], parts[:, u, 0], ALU.subtract).then_inc(rest_ready, 1)
                    dve.wait_ge(mid_ready, c + 1)
                    dve.tensor_tensor(parts[:, u, 2], rest[:, u], parts[:, u, 1], ALU.subtract).then_inc(lo_ready, 1)
                assert st.n == CPB * NORM_STEPS

        @block.scalar
        def _(act):
            def chunk(b, u, first):
                c = b * CPB + u
                act.wait_ge(s["var_ready"], c + 1)
                act.activation(s["root"][:, u, :], s["var"][:, u, :], ACT.Sqrt).then_inc(s["root_ready"], 1)
                act.wait_ge(transposed, c + 1)
                act.activation(xnT[:, u, :], psT[u][:, :], ACT.Copy).then_inc(xnT_ready, 1)
                act.wait_ge(qkv_done, c + 1)
                for i in range(2):
                    if biased:
                        ins = act.activation(qk[:, u, i, :], psQK[:, i, :], ACT.Identity, bias=g["bias_qk"][:, i:i + 1])
                    else:
                        ins = act.activation(qk[:, u, i, :], psQK[:, i, :], ACT.Copy)
                ins.then_inc(qk_ready, 1)
                act.wait_ge(qk_ready, c + 1)
                if not first:
                    act.wait_ge(stored[u], b * (16 * STORES))
                act.activation(parts[:, u, 0], qk[:, u], ACT.Copy).then_inc(hi_ready, 1)
                act.wait_ge(rest_ready, c + 1)
                act.activation(parts[:, u, 1], rest[:, u], ACT.Copy).then_inc(mid_ready, 1)

            for u in range(CPB):
                chunk(0, u, True)
            with act.Fori(1, B) as b:
                for u in range(CPB):
                    chunk(b, u, False)

        @block.tensor
        def _(pe):
            def chunk(b, u, first):
                c = b * CPB + u
                pe.wait_ge(s["xn_ready"], c + 1)
                for t in range(TPC):
                    last = pe.transpose(psT[u][:, t * P:(t + 1) * P], s["xn"][:, u, t, :], g["identf"][:, :])
                last.then_inc(transposed, 1)
                pe.wait_ge(xnT_ready, c + 1)
                if not first:
                    pe.wait_ge(qk_ready, c)
                    pe.wait_ge(v_taken, c)
                for i in range(2):
                    pe.matmul(psQK[:, i, :], w[:, i, :], xnT[:, u, :], start=True, stop=True)
                for t in range(TPC):
                    last = pe.matmul(psV[:, t, :], xnT[:, u, t * P:(t + 1) * P], w[:, 2, :], start=True, stop=True)
                last.then_inc(qkv_done, 1)

            for u in range(CPB):
                chunk(0, u, u == 0)
            with pe.Fori(1, B) as b:
                for u in range(CPB):
                    chunk(b, u, False)

        @block.sync
        def _(sp):
            with sp.Fori(0, B) as b:
                for u in range(CPB):
                    sp.wait_ge(lo_ready, b * CPB + u + 1)
                    for i, dram in enumerate((g["q_dram"], g["k_dram"])):
                        for part in range(PARTS):
                            dst = bass.AP(dram.tensor, b * HSZ + part * HD * T + u * CH, [[B * HSZ, HEADS], [T, HD], [1, CH]])
                            sp.dma_start(dst, parts[:, u, part, i, :]).then_inc(stored[u], 16)
            for u in range(CPB):
                sp.wait_ge(stored[u], 16 * STORES * B)


def attend_heads(nc, m, g, causal):
    NG = HEADS * B
    LAG = 3
    if causal:
        halves = [[h for h in range(2) if (h + 1) * CH > kb * P] for kb in range(TPB)]
    else:
        halves = [[0, 1] for kb in range(TPB)]
    first_unit = [sum(len(x) for x in halves[:kb]) for kb in range(TPB + 1)]
    UNITS = first_unit[-1]
    assert UNITS % 2 == 0

    def columns(kb, h):
        lo = max(h * CH, kb * P) if causal else h * CH
        return lo, (h + 1) * CH

    def near(kb):
        if causal:
            return kb * P, min(T, kb * P + NEAR)
        return kb * P, (kb + 2 - kb % 2) * P

    qM = [m.sb(f"qM{p}", [P, T], BF16) for p in range(2)]
    kM = [m.sb(f"kM{p}", [P, T], BF16) for p in range(2)]
    qS = [m.sb(f"qS{p}", [P, T], BF16) for p in range(2)]
    kS = [m.sb(f"kS{p}", [P, T], BF16) for p in range(2)]
    probs = [m.sb(f"probs{p}", [P, TPB, T]) for p in range(2)]
    masked = [m.sb(f"masked{p}", [P, TPB, NEAR]) for p in range(2)] if not causal else None
    v_ones = [m.sb(f"v_ones{p}", [P, TPB, VW]) for p in range(2)]
    v_only = [m.sb(f"v_only{p}", [P, TPB, VW]) for p in range(2)] if not causal else None
    ones_only = m.sb("ones_only", [P, VW]) if not causal else None
    mx = m.sb("mx", [P, 2, TPB])
    nm = m.sb("nm", [P, 2, 2, TPB], BF16)
    mrow = [m.sb(f"mrow{p}", [2 * TPB, P], BF16) for p in range(2)]
    oT = [m.sb(f"oT{p}", [P, 2 * P]) for p in range(2)]
    psM = [m.ps(f"psM{i}", [P, T]) for i in range(2)]
    psS = [m.ps(f"psS{i}", [P, CH]) for i in range(2)]
    psO = m.ps("psO", [P, CH])
    psR = m.ps("psR", [P, CH])

    cleared, pool_ready = m.sem("cleared"), m.sem("pool_ready")
    m_loaded = [m.sem(f"m_loaded{p}") for p in range(2)]
    s_loaded = [m.sem(f"s_loaded{p}") for p in range(2)]
    r_loaded = [m.sem(f"r_loaded{p}") for p in range(2)]
    o_stored = [m.sem(f"o_stored{p}") for p in range(2)]
    maxima_done = m.sem("maxima_done")
    max_taken = m.sem("max_taken")
    nm_hi, nm_ready = m.sem("nm_hi"), m.sem("nm_ready")
    rows_done, rows_taken = m.sem("rows_done"), m.sem("rows_taken")
    scores_done = m.sem("scores_done")
    exp_done = m.sem("exp_done")
    near_done = m.sem("near_done")
    v_staged, passed = m.sem("v_staged"), m.sem("passed")
    pv_done, o_taken = m.sem("pv_done"), m.sem("o_taken")

    def program(eng, step):
        for u in range(B):
            step(u, u, u)
        with eng.Fori(1, HEADS - 1) as h:
            for u in range(B):
                step(h * B + u, u, None)
        for u in range(B):
            step(NG - B + u, u, NG - B + u)

    with nc.Block() as block:

        @block.sync
        def _(sp):
            sp.wait_ge(cleared, 1)

            def load_m(n, p):
                for i in range(2):
                    q = bass.AP(g["q_dram"].tensor, n * HSZ + i * HD * T, [[0, 2], [T, HD], [1, T]])
                    sp.dma_start(qM[p][i * 2 * HD:(i + 1) * 2 * HD, :], q).then_inc(m_loaded[p], 16)
                    k = bass.AP(g["k_dram"].tensor, n * HSZ, [[T, 2 * HD], [1, T]])
                    sp.dma_start(kM[p][i * 2 * HD:(i + 1) * 2 * HD, :], k).then_inc(m_loaded[p], 16)

            def load_s(n, p):
                for i in range(PARTS):
                    r = i * PARTS * HD
                    q = bass.AP(g["q_dram"].tensor, n * HSZ + i * HD * T, [[0, PARTS], [T, HD], [1, T]])
                    sp.dma_start(qS[p][r:r + PARTS * HD, :], q).then_inc(s_loaded[p], 16)
                    k = bass.AP(g["k_dram"].tensor, n * HSZ, [[T, PARTS * HD], [1, T]])
                    sp.dma_start(kS[p][r:r + PARTS * HD, :], k).then_inc(s_loaded[p], 16)

            def load_r(n, p):
                sp.wait_ge(rows_taken, n + 1)
                for i in range(2):
                    sp.dma_start(qS[p][MROW + i:MROW + i + 1, :], mrow[p][i * TPB:(i + 1) * TPB, :]).then_inc(r_loaded[p], 16)

            for n in range(2):
                load_m(n, n)
            load_s(0, 0)
            sp.wait_ge(maxima_done, TPB)
            load_m(2, 0)
            load_r(0, 0)

            def step(n, u, known):
                p = u % 2
                if known is None or known < NG - 1:
                    if known != 0:
                        sp.wait_ge(scores_done, n * UNITS)
                    load_s(n + 1, 1 - p)
                if known is None or known < NG - 3:
                    sp.wait_ge(maxima_done, (n + 2) * TPB)
                    load_m(n + 3, 1 - p)
                if known is None or known < NG - 1:
                    load_r(n + 1, 1 - p)
                if known != 0:
                    sp.wait_ge(o_taken, n)
                    sp.dma_start(store_at(n - 1), oT[1 - p][:, :]).then_inc(o_stored[1 - p], 16)

            def store_at(n):
                return bass.AP(g["o_dram"].tensor, n * (VW * T), [[2 * P, 4], [T, VW], [1, 2 * P]])

            program(sp, step)
            sp.wait_ge(o_taken, NG)
            sp.dma_start(store_at(NG - 1), oT[1][:, :]).then_inc(o_stored[1], 16)
            for p in range(2):
                sp.wait_ge(o_stored[p], 16 * NG // 2)

        @block.vector
        def _(dve):
            for p in range(2):
                dve.memset(qM[p][:, :].bitcast(F32), 0.0)
                dve.memset(kM[p][:, :].bitcast(F32), 0.0)
                dve.memset(qS[p][:, :].bitcast(F32), 0.0)
                last = dve.memset(kS[p][:, :], 1.0)
            last.then_inc(cleared, 1)

            def maxima(n, p, static):
                for qb in range(TPB):
                    dve.wait_ge(maxima_done, n * TPB + qb + 1)
                    w = (qb + 1) * P if causal else T
                    if qb == 0 and (static is None or static >= 2):
                        dve.wait_ge(nm_ready, n - 1)
                    dve.tensor_reduce(mx[:, p, qb:qb + 1], psM[qb % 2][:, 0:w], AXX, ALU.max).then_inc(max_taken, 1)
                dve.wait_ge(max_taken, (n + 1) * TPB)
                if static is None or static >= 2:
                    dve.wait_ge(rows_done, n - 1)
                dve.tensor_scalar(nm[:, p, 0, :], mx[:, p, :], -1.0, None, ALU.mult).then_inc(nm_hi, 1)
                dve.wait_ge(nm_hi, n + 1)
                dve.scalar_tensor_tensor(nm[:, p, 1, :], mx[:, p, :], -1.0, nm[:, p, 0, :], ALU.mult, ALU.subtract).then_inc(nm_ready, 1)

            for n in range(2):
                maxima(n, n, n)

            def step(n, u, known):
                if known is None or known < NG - 2:
                    maxima(n + 2, u % 2, None if known is None else known + 2)

            program(dve, step)

        @block.gpsimd
        def _(pool):
            for p in range(2):
                pool.memset(v_ones[p][:, :, :], 0.0)
                if not causal:
                    pool.memset(v_only[p][:, :, :], 0.0)
            if not causal:
                pool.memset(ones_only[:, :], 0.0)
            pool.memset(mrow[0][:, :], 0.0).then_inc(pool_ready, 1)
            pool.wait_ge(pool_ready, 1)
            if not causal:
                pool.memset(ones_only[:, HD:2 * HD], 1.0)
            pool.memset(v_ones[0][:, :, HD:2 * HD], 1.0)
            pool.memset(v_ones[1][:, :, HD:2 * HD], 1.0).then_inc(pool_ready, 1)

            def stage_v(n, p):
                src = g["v_all"][:, :, :, :, :].rearrange("p h b t e -> p (h b) t e")[:, n, :, :]
                ins = pool.tensor_copy(v_ones[p][:, :, 0:HD], src)
                if not causal:
                    ins = pool.tensor_copy(v_only[p][:, :, 0:HD], src)
                ins.then_inc(v_staged, 1)

            pool.wait_ge(pool_ready, 2)
            stage_v(0, 0)

            def step(n, u, known):
                p = u % 2
                for kb in range(TPB):
                    a, z = near(kb)
                    wait_alone(pool, exp_done, n * UNITS + first_unit[kb + 1], passed)
                    if causal:
                        pool.tensor_tensor(probs[p][:, kb, a:z], probs[p][:, kb, a:z], ebias_of(n, u, z - a), ALU.mult).then_inc(near_done, 1)
                    else:
                        if kb == 0 and (known is None or known >= 2):
                            pool.wait_ge(pv_done, n - 1)
                        pool.tensor_tensor(masked[p][:, kb, 0:z - a], probs[p][:, kb, a:z], g["tri"][:, 0:z - a], ALU.mult).then_inc(near_done, 1)
                    if kb == LAG and (known is None or known < NG - 1):
                        if known != 0:
                            pool.wait_ge(pv_done, n)
                        stage_v(n + 1, 1 - p)

            def ebias_of(n, u, w):
                return g["ebias"][:, n // B if isinstance(n, int) else (n - u) // B, 0:w]

            program(pool, step)

        @block.scalar
        def _(act):
            def take_rows(n, p, static):
                act.wait_ge(rows_done, n + 1)
                if static is None or static >= 2:
                    act.wait_ge(r_loaded[p], row_loads(n))
                act.activation(mrow[p][:, :], psR[0:2 * TPB, 0:P], ACT.Copy).then_inc(rows_taken, 1)

            def row_loads(n):
                return (n - n_parity[0]) * 16

            n_parity = [0]
            act.wait_ge(pool_ready, 1)
            take_rows(0, 0, 0)

            def take_o(n, p, static):
                act.wait_ge(pv_done, n + 1)
                if static is None or static >= 2:
                    act.wait_ge(o_stored[p], (n - p) * 8)
                act.activation(oT[p][:, :], psO[:, 0:2 * P], ACT.Copy).then_inc(o_taken, 1)

            def step(n, u, known):
                p = u % 2
                for kb in range(TPB):
                    for i, h in enumerate(halves[kb]):
                        a, z = columns(kb, h)
                        unit = first_unit[kb] + i
                        act.wait_ge(scores_done, n * UNITS + unit + 1)
                        if kb == 0 and i == 0 and (known is None or known >= 2):
                            act.wait_ge(pv_done, n - 1)
                        act.activation(probs[p][:, kb, a:z], psS[unit % 2][:, a - h * CH:z - h * CH], ACT.Exp,
                                       scale=1.0 if causal else HEAD_SCALE).then_inc(exp_done, 1)
                    if kb == 1 and (known is None or known < NG - 1):
                        n_parity[0] = 1 - p
                        take_rows(n + 1, 1 - p, None if known is None else known + 1)
                    if kb == 2 and known != 0:
                        take_o(n - 1, 1 - p, None if known is None else known - 1)

            program(act, step)
            take_o(NG - 1, 1, NG - 1)

        @block.tensor
        def _(pe):
            def max_scores(n, p, qb, static):
                if static is None or static > 0 or qb >= 2:
                    pe.wait_ge(max_taken, n * TPB + qb - 1)
                if qb == 0:
                    pe.wait_ge(m_loaded[p], (n - p) * 32 + 64)
                w = (qb + 1) * P if causal else T
                for h in range(-(-w // CH)):
                    a, z = h * CH, min((h + 1) * CH, w)
                    holds_diagonal = causal and z == w
                    last = pe.matmul(psM[qb % 2][:, a:z], qM[p][:, qb * P:(qb + 1) * P], kM[p][:, a:z], start=True, stop=not holds_diagonal)
                if causal:
                    last = pe.matmul(psM[qb % 2][:, w - P:w], g["identb"][:, :], g["maskneg"][:, :], start=False, stop=True)
                last.then_inc(maxima_done, 1)

            def max_rows(n, p, static):
                pe.wait_ge(nm_ready, n + 1)
                if static is None or static > 0:
                    pe.wait_ge(rows_taken, n)
                pe.matmul(psR[0:2 * TPB, 0:P], nm[:, p, :, :].rearrange("p s q -> p (s q)"), g["identb"][:, :], start=True, stop=True).then_inc(rows_done, 1)

            def scores(n, p, kb, static):
                if kb == 0:
                    pe.wait_ge(s_loaded[p], (n - p) * (3 * 16) + 6 * 16)
                    pe.wait_ge(r_loaded[p], (n - p) * 16 + 32)
                for i, h in enumerate(halves[kb]):
                    a, z = columns(kb, h)
                    unit = first_unit[kb] + i
                    if static is None or static > 0 or unit >= 2:
                        pe.wait_ge(exp_done, n * UNITS + unit - 1)
                    masks = causal and i == 0
                    last = pe.matmul(psS[unit % 2][:, a - h * CH:z - h * CH], kS[p][:, kb * P:(kb + 1) * P], qS[p][:, a:z], start=True, stop=not masks)
                    if masks:
                        last = pe.matmul(psS[unit % 2][:, a - h * CH:a - h * CH + P], g["identb"][:, :], g["masknegT"][:, :], start=False, stop=True)
                    last.then_inc(scores_done, 1)

            def values(n, p, kb, static):
                if kb == 0:
                    pe.wait_ge(v_staged, n + 1)
                    if static is None or static > 0:
                        pe.wait_ge(o_taken, n)
                if causal:
                    pe.wait_ge(near_done, n * TPB + kb + 1)
                    for c in range(4):
                        out = psO[c * VW:(c + 1) * VW, 0:2 * P]
                        pr = probs[p][:, kb, :].rearrange("p (q w) -> p q w", w=P)
                        if kb <= c:
                            last = pe.matmul(out.rearrange("p (q w) -> p q w", w=P), v_ones[p][:, kb, :], pr[:, c:TPB - c:TPB - 1 - 2 * c, :],
                                             start=kb == 0, stop=False, tile_position=(0, c * VW))
                        elif kb <= TPB - 1 - c:
                            b = TPB - 1 - c
                            last = pe.matmul(out[:, P:2 * P], v_ones[p][:, kb, :], pr[:, b, :],
                                             start=False, stop=kb == TPB - 1 - c, tile_position=(0, c * VW))
                    if kb == TPB - 1:
                        last.then_inc(pv_done, 1)
                    return
                pe.wait_ge(exp_done, n * UNITS + first_unit[kb + 1])
                for c in range(4):
                    pe.matmul(psO[c * VW:(c + 1) * VW, 0:2 * P], v_ones[p][:, kb, :] if kb < 2 * c else ones_only[:, :],
                              probs[p][:, kb, 2 * c * P:(2 * c + 2) * P], start=kb == 0, stop=False, tile_position=(0, c * VW))
                if kb == TPB - 1:
                    pe.wait_ge(near_done, (n + 1) * TPB)
                    for odd in range(2):
                        for c in range(4):
                            last = pe.matmul(psO[c * VW:(c + 1) * VW, odd * P:2 * P], v_only[p][:, 2 * c + odd, :],
                                             masked[p][:, 2 * c + odd, 0:(2 - odd) * P], start=False, stop=odd == 1, tile_position=(0, c * VW))
                    last.then_inc(pv_done, 1)

            pe.wait_ge(cleared, 1)
            for n in range(2):
                for qb in range(TPB):
                    max_scores(n, n, qb, n)
                if n == 0:
                    max_rows(0, 0, 0)

            def step(n, u, known):
                p = u % 2
                for kb in range(TPB):
                    scores(n, p, kb, known)
                    if known is None or known < NG - 2:
                        max_scores(n + 2, p, kb, None)
                    if kb == 1 and (known is None or known < NG - 1):
                        max_rows(n + 1, 1 - p, None)
                    if kb >= LAG:
                        values(n, p, kb - LAG, known)
                    elif known != 0:
                        values(n - 1, 1 - p, kb - LAG + TPB, None if known is None else known - 1)

            program(pe, step)
            for kb in range(TPB - LAG, TPB):
                values(NG - 1, 1, kb, NG - 1)


def route_and_add(nc, m, g):
    s = norm_mem(m)
    num = [m.sb(f"num{p}", [P, T]) for p in range(1)]
    den = [m.sb(f"den{p}", [P, T]) for p in range(1)]
    att = m.sb("att", [P, T])
    NN = FF * NODES
    bits = m.sb("bits", [P, TPC, NN])
    nbits = m.sb("nbits", [P, TPC, NN])
    way = [m.sb(f"way{i}", [P, TPC, FF, 2 ** (i + 1)]) for i in range(DEPTH - 1)]
    sel = m.sb("sel", [P, TPC, P])
    psY = [m.ps(f"psY{u}", [P, TPC, D]) for u in range(CPB)]
    psT = [m.ps(f"psT{u}", [P, CH]) for u in range(CPB)]
    psN = m.ps("psN", [P, TPC, NN])
    psL = m.ps("psL", [P, CH])
    o_loaded, att_ready = m.sem("o_loaded"), m.sem("att_ready")
    projected, transposed, xnT_ready = m.sem("projected"), m.sem("transposed"), m.sem("xnT_ready")
    noded, sel_ready, sel_turned, sel_taken = m.sem("noded"), m.sem("sel_ready"), m.sem("sel_turned"), m.sem("sel_taken")
    dve_steps = m.sem("dve_steps")
    ROUTE = 4 + DEPTH
    xnT_now = m.sb("xnT_now", [P, CPB, CH])
    EXTRA = 2
    N_STEPS = 2 + CPB * (NORM_STEPS + EXTRA + ROUTE)

    with nc.Block() as block:

        @block.sync
        def _(sp):
            def load(b, first):
                if not first:
                    sp.wait_ge(att_ready, b)
                sp.dma_start(num[0][:, :], bass.AP(g["o_dram"].tensor, b * (VW * T), [[B * VW * T, HEADS], [T, HD], [1, T]])).then_inc(o_loaded, 16)
                sp.dma_start(den[0][:, :], bass.AP(g["o_dram"].tensor, b * (VW * T) + HD * T, [[B * VW * T, HEADS], [T, HD], [1, T]])).then_inc(o_loaded, 16)

            load(0, True)
            with sp.Fori(1, B) as b:
                load(b, False)

        @block.vector
        def _(dve):
            def batch(b, first):
                st = Steps(dve, dve_steps, b * N_STEPS)
                dve.wait_ge(o_loaded, b * 32 + 32)
                st.did(dve.reciprocal(den[0][:, :], den[0][:, :]))
                st.settle()
                if not first:
                    dve.wait_ge(projected, b * CPB)
                for half in range(2):
                    view = lambda t: t[:, :].rearrange("p (c q w) -> p c q w", q=2, w=P)[:, :, half, :]
                    o4 = att[:, :].rearrange("p (q w) -> p q w", w=P)
                    if half == 0:
                        st.did(dve.tensor_tensor(o4[:, 0:4, :], view(num[0]), view(den[0]), ALU.mult))
                    else:
                        for c in range(4):
                            ins = dve.tensor_tensor(o4[:, TPB - 1 - c, :], view(num[0])[:, c, :], view(den[0])[:, c, :], ALU.mult)
                        ins.then_inc(att_ready, 1)
                for u in range(CPB):
                    c = b * CPB + u
                    dve.wait_ge(projected, c + 1)
                    xs = g["x"][:, b * TPB + u * TPC:b * TPB + (u + 1) * TPC, :] if isinstance(b, int) else g["x"][:, bass.ds(b * TPB + u * TPC, TPC), :]
                    st.did(dve.tensor_tensor(xs, psY[u][:, :, :], xs, ALU.add))
                    st.settle()
                    st.did(dve.tensor_tensor(xs, xs, g["bo"][:, :].unsqueeze(1).to_broadcast([P, TPC, D]), ALU.add))
                    st.settle_alone(s["passed"])
                    normalise(dve, st, g, c, u, s, b)
                    dve.wait_ge(noded, c + 1)
                    st.did(dve.tensor_tensor(bits[:, :, :], psN[:, :, :], g["node_b"][:, :].unsqueeze(1).to_broadcast([P, TPC, NN]), ALU.add))
                    st.settle()
                    st.did(dve.tensor_scalar(nbits[:, :, :], bits[:, :, :], 0.0, None, ALU.is_lt))
                    st.did(dve.tensor_scalar(bits[:, :, :], bits[:, :, :], 0.0, None, ALU.is_ge))
                    st.settle()
                    if not first or u:
                        dve.wait_ge(sel_turned, c)
                    st.did(dve.memset(sel[:, :, :], 0.0))
                    st.settle()
                    for d in range(DEPTH):
                        lo, w = 2 ** d - 1, 2 ** d
                        for tree in range(FF):
                            if d < DEPTH - 1:
                                out = way[d][:, :, tree, :].rearrange("p t (n s) -> p t n s", s=2)
                            else:
                                a = SELROW + tree * LEAVES
                                out = sel[:, :, a:a + LEAVES].rearrange("p t (n s) -> p t n s", s=2)
                            for side, bb in enumerate((nbits, bits)):
                                node = bb[:, :, tree * NODES + lo:tree * NODES + lo + w]
                                if d == 0:
                                    last = dve.tensor_copy(out[:, :, :, side], node)
                                else:
                                    last = dve.tensor_tensor(out[:, :, :, side], way[d - 1][:, :, tree, :], node, ALU.mult)
                        st.did(last)
                        st.settle()
                    dve.tensor_scalar(sel[:, :, 0:FF * LEAVES], sel[:, :, SELROW:SELROW + FF * LEAVES], -1.0, None, ALU.add).then_inc(sel_ready, 1)
                    n_used.append(st.n)

            n_used = []
            batch(0, True)
            assert n_used[-1] == N_STEPS, (n_used[-1], N_STEPS)
            with dve.Fori(1, B) as b:
                batch(b, False)

        @block.scalar
        def _(act):
            with act.Fori(0, B) as b:
                for u in range(CPB):
                    c = b * CPB + u
                    act.wait_ge(s["var_ready"], c + 1)
                    act.activation(s["root"][:, u, :], s["var"][:, u, :], ACT.Sqrt).then_inc(s["root_ready"], 1)
                    act.wait_ge(transposed, c + 1)
                    act.activation(xnT_now[:, u, :], psT[u][:, :], ACT.Copy).then_inc(xnT_ready, 1)
                    act.activation(g["xnT_all"][:, bass.ds(b * T + u * CH, CH)], psT[u][:, :], ACT.Copy).then_inc(xnT_ready, 1)
                    act.wait_ge(sel_turned, c + 1)
                    act.activation(g["selT"][:, bass.ds(b * T + u * CH, CH)], psL[:, :], ACT.Copy).then_inc(sel_taken, 1)

        @block.tensor
        def _(pe):
            def batch(b, first):
                pe.wait_ge(att_ready, b + 1)
                for u in range(CPB):
                    for t in range(TPC):
                        last = pe.matmul(psY[u][:, t, :], att[:, (u * TPC + t) * P:(u * TPC + t + 1) * P], g["w_a"][:, 3, :], start=True, stop=True)
                    last.then_inc(projected, 1)
                for u in range(CPB):
                    c = b * CPB + u
                    pe.wait_ge(s["xn_ready"], c + 1)
                    for t in range(TPC):
                        last = pe.transpose(psT[u][:, t * P:(t + 1) * P], s["xn"][:, u, t, :], g["identf"][:, :])
                    last.then_inc(transposed, 1)
                    pe.wait_ge(xnT_ready, 2 * c + 2)
                    for t in range(TPC):
                        last = pe.matmul(psN[:, t, :], xnT_now[:, u, t * P:(t + 1) * P], g["node_wT"][:, :], start=True, stop=True)
                    last.then_inc(noded, 1)
                    pe.wait_ge(sel_ready, c + 1)
                    if not first or u:
                        pe.wait_ge(sel_taken, c)
                    for t in range(TPC):
                        last = pe.transpose(psL[:, t * P:(t + 1) * P], sel[:, t, :], g["identf"][:, :])
                    last.then_inc(sel_turned, 1)

            batch(0, True)
            with pe.Fori(1, B) as b:
                batch(b, False)



def trees(nc, m, g):
    NH = 4
    hid = [m.sb(f"hid{i}", [P, CH]) for i in range(NH)]
    vT = m.sb("vT", [P, CH])
    psH = [m.ps(f"psH{i}", [P, CH]) for i in range(2)]
    psO = [m.ps(f"psO{i}", [P, CH]) for i in range(2)]
    psV = m.ps("psV", [P, CH])
    hidden_done, hid_ready, out_done, out_taken = m.sem("hidden_done"), m.sem("hid_ready"), m.sem("out_done"), m.sem("out_taken")
    v_turned, v_taken = m.sem("v_turned"), m.sem("v_taken")
    used = m.sem("used")
    LAG = 2

    with nc.Block() as block:

        def rounds(eng, body):
            for f in range(FF):
                if f == 0:
                    for u in range(CPB):
                        body(f, 0, u, u == 0)
                with eng.Fori(1 if f == 0 else 0, B) as b:
                    for u in range(CPB):
                        body(f, b, u, False)

        @block.tensor
        def _(pe):
            def body(f, b, u, first):
                c = b * CPB + u + f * NCH
                toks = bass.ds(b * T + u * CH, CH)
                for i in range(HID + LAG):
                    if i < HID:
                        n = c * HID + i
                        if not first or i >= 2:
                            pe.wait_ge(hid_ready, n - 1)
                        pe.matmul(psH[i % 2][:, :], g["w1"][:, f, i * P:(i + 1) * P], g["xnT_all"][:, toks], start=True, stop=False)
                        a = (f * LEAVES + 2 * i) * LW
                        pe.matmul(psH[i % 2][:, :], g["leafx"][:, a:a + P], g["selT"][:, toks], start=False, stop=True).then_inc(hidden_done, 1)
                    if i >= LAG:
                        j = i - LAG
                        pe.wait_ge(hid_ready, c * HID + j + 1)
                        if j == 0 and not (first or (isinstance(b, int) and b == 0 and f == 0)):
                            pe.wait_ge(out_taken, c - 1)
                        pe.matmul(psO[u][:, :], g["w2"][:, f, j, :], hid[j % NH][:, :], start=j == 0, stop=False).then_inc(used, 1)
                for part in range(PARTS):
                    last = pe.matmul(psO[u][:, :], g["b2p"][:, part, f, :], g["selT"][:, toks], start=False, stop=part == PARTS - 1)
                last.then_inc(out_done, 1)
                if f == FF - 1:
                    pe.wait_ge(out_taken, c + 1)
                    pe.wait_ge(v_taken, b * CPB + u + 1)
                    for t in range(TPC):
                        last = pe.transpose(psV[:, t * P:(t + 1) * P], vT[:, t * P:(t + 1) * P], g["identf"][:, :])
                    last.then_inc(v_turned, 1)

            rounds(pe, body)

        @block.scalar
        def _(act):
            def body(f, b, u, first):
                c = b * CPB + u + f * NCH
                for i in range(HID):
                    n = c * HID + i
                    act.wait_ge(hidden_done, n + 1)
                    if not first or i >= NH:
                        act.wait_ge(used, n - NH + 1)
                    act.activation(hid[i % NH][:, :], psH[i % 2][:, :], ACT.Relu, bias=g["b1"][:, f, i:i + 1]).then_inc(hid_ready, 1)

            rounds(act, body)

        @block.vector
        def _(dve):
            dve.sem_inc(v_taken, 1)

            def body(f, b, u, first):
                c = b * CPB + u + f * NCH
                dve.wait_ge(out_done, c + 1)
                if f < FF - 1:
                    dve.tensor_copy(g["qkT"][:, f, bass.ds(b * T + u * CH, CH)], psO[u][:, :]).then_inc(out_taken, 1)
                else:
                    dve.tensor_copy(vT[:, :], psO[u][:, :]).then_inc(out_taken, 1)
                    dve.wait_ge(v_turned, b * CPB + u + 1)
                    dve.tensor_copy(g["v_tok"][:, bass.ds(b * TPB + u * TPC, TPC), :], psV[:, :].rearrange("p (t d) -> p t d", t=TPC)).then_inc(v_taken, 1)

            rounds(dve, body)


def attend_wide(nc, m, g):
    SC = float(D) ** -0.5
    qs = m.sb("qs", [P, T])
    probs = [m.sb(f"probs{i}", [P, T]) for i in range(2)]
    turned = [m.sb(f"turned{i}", [P, T]) for i in range(2)]
    mx, nmx, den, rden = m.sb("mx", [P, 2]), m.sb("nmx", [P, 2]), m.sb("den", [P, 2]), m.sb("rden", [P, 2])
    psS = [m.ps(f"psS{i}", [P, T]) for i in range(2)]
    psT = m.ps("psT", [P, 2, CH])
    psY = m.ps("psY", [P, CH])
    q_staged, scored, max_taken, shift_ready = m.sem("q_staged"), m.sem("scored"), m.sem("max_taken"), m.sem("shift_ready")
    exp_done, flipped, valued, added, rden_ready = (m.sem(n) for n in ("exp_done", "flipped", "valued", "added", "rden_ready"))
    flip_taken = [m.sem(f"flip_taken{h}") for h in range(2)]

    def batches(eng, body):
        body(0, True)
        with eng.Fori(1, B) as b:
            body(b, False)

    with nc.Block() as block:

        @block.tensor
        def _(pe):
            def score(b, qb, first):
                n = b * TPB + qb
                if qb == 0:
                    pe.wait_ge(q_staged, b + 1)
                if not first or qb >= 2:
                    pe.wait_ge(exp_done, n - 1)
                for h in range(2):
                    last = pe.matmul(psS[qb % 2][:, h * CH:(h + 1) * CH], qs[:, qb * P:(qb + 1) * P],
                                     g["qkT"][:, 1, bass.ds(b * T + h * CH, CH)], start=True, stop=True)
                last.then_inc(scored, 1)

            def value(b, qb, first):
                n = b * TPB + qb
                pe.wait_ge(exp_done, n + 1)
                for h in range(2):
                    if not first or qb:
                        pe.wait_ge(flip_taken[h], n)
                    for k in range(4):
                        kb = 4 * h + k
                        last = pe.transpose(psT[:, h, k * P:(k + 1) * P], probs[qb % 2][:, kb * P:(kb + 1) * P], g["identf"][:, :])
                    last.then_inc(flipped, 1)
                if not first or qb:
                    pe.wait_ge(added, n)
                for h in range(2):
                    pe.wait_ge(flip_taken[h], n + 1)
                    for k in range(4):
                        kb = 4 * h + k
                        last = pe.matmul(psY[:, 0:D], turned[qb % 2][:, kb * P:(kb + 1) * P], g["v_tok"][:, b * TPB + kb, :],
                                         start=kb == 0, stop=kb == TPB - 1)
                last.then_inc(valued, 1)

            def body(b, first):
                for qb in range(TPB + 1):
                    if qb < TPB:
                        score(b, qb, first)
                    if qb:
                        value(b, qb - 1, first)

            batches(pe, body)

        @block.gpsimd
        def _(pool):
            def body(b, first):
                if not first:
                    pool.wait_ge(scored, b * TPB)
                pool.tensor_copy(qs[:, :], g["qkT"][:, 0, bass.ds(b * T, T)]).then_inc(q_staged, 1)

            batches(pool, body)

        @block.vector
        def _(dve):
            def body(b, first):
                def shift(qb):
                    n = b * TPB + qb
                    p = qb % 2
                    dve.wait_ge(scored, n + 1)
                    dve.tensor_reduce(mx[:, p:p + 1], psS[p][:, :], AXX, ALU.max).then_inc(max_taken, 1)
                    dve.wait_ge(max_taken, n + 1)
                    if not first or qb >= 2:
                        dve.wait_ge(exp_done, n - 1)
                    dve.tensor_scalar(nmx[:, p:p + 1], mx[:, p:p + 1], -SC, None, ALU.mult).then_inc(shift_ready, 1)

                def finish(qb):
                    n = b * TPB + qb
                    p = qb % 2
                    dve.wait_ge(flipped, 2 * n + 2)
                    dve.tensor_copy(turned[p][:, CH:T], psT[:, 1, :]).then_inc(flip_taken[1], 1)
                    if not first or qb >= 1:
                        dve.wait_ge(added, n)
                    dve.reciprocal(rden[:, p:p + 1], den[:, p:p + 1]).then_inc(rden_ready, 1)
                    dve.wait_ge(rden_ready, n + 1)
                    dve.wait_ge(valued, n + 1)
                    dve.scalar_tensor_tensor(g["x"][:, b * TPB + qb, :], psY[:, 0:D], rden[:, p:p + 1], g["x"][:, b * TPB + qb, :],
                                             ALU.mult, ALU.add).then_inc(added, 1)

                for qb in range(TPB + 1):
                    if qb < TPB:
                        shift(qb)
                    if qb:
                        finish(qb - 1)

            batches(dve, body)

        @block.scalar
        def _(act):
            def body(b, first):
                for qb in range(TPB + 1):
                    if qb < TPB:
                        n = b * TPB + qb
                        p = qb % 2
                        act.wait_ge(shift_ready, n + 1)
                        if not first or qb >= 2:
                            act.wait_ge(flipped, 2 * n - 2)
                            act.wait_ge(rden_ready, n - 1)
                        act.activation(probs[p][:, :], psS[p][:, :], ACT.Exp, bias=nmx[:, p:p + 1], scale=SC,
                                       accum_out=den[:, p:p + 1]).then_inc(exp_done, 1)
                    if qb:
                        n = b * TPB + qb - 1
                        p = (qb - 1) % 2
                        act.wait_ge(flipped, 2 * n + 1)
                        if not first or qb > 2:
                            act.wait_ge(valued, n - 1)
                        act.activation(turned[p][:, 0:CH], psT[:, 0, :], ACT.Copy).then_inc(flip_taken[0], 1)

            batches(act, body)


def finish_layers(nc, m, g, out):
    s = norm_mem(m)
    num, den = m.sb("num", [P, T]), m.sb("den", [P, T])
    att = m.sb("att", [P, T])
    xT = m.sb("xT", [P, T + 1])
    omm = m.sb("omm", [P, 2])
    prev = m.sb("prev", [P, CPB, 2, CH])
    mix = m.sb("mix", [P, CPB, 2, CH])
    kact = m.sb("kact", [P, CPB, CH])
    gate = m.sb("gate", [P, CPB, CH])
    res = m.sb("res", [P, CPB, TPC, D])
    psA = [m.ps(f"psA{u}", [P, TPC, D]) for u in range(CPB)]
    psT = [m.ps(f"psT{u}", [P, CH]) for u in range(CPB)]
    psK = m.ps("psK", [P, CH])
    psR = m.ps("psR", [P, CH])
    psV = m.ps("psV", [P, CH])
    names = ["o_loaded", "att_ready", "att_turned", "transposed", "xT_ready", "mu_ready", "prev_ready", "mix_ready",
             "keys_done", "relu_done", "kact_ready", "gates_done", "gate_ready", "wide_done", "out_ready", "dve_steps"]
    (o_loaded, att_ready, att_turned, transposed, xT_ready, mu_ready, prev_ready, mix_ready,
     keys_done, relu_done, kact_ready, gates_done, gate_ready, wide_done, out_ready, dve_steps) = (m.sem(n) for n in names)
    out_stored = [m.sem(f"out_stored{u}") for u in range(CPB)]
    N_STEPS = 1 + CPB * (1 + NORM_STEPS + 1)

    def batches(eng, body):
        body(0, True)
        with eng.Fori(1, B) as b:
            body(b, False)

    with nc.Block() as block:

        @block.sync
        def _(sp):
            out_t = out.rearrange("b (t p) d -> b p t d", p=P)

            def body(b, first):
                if not first:
                    sp.wait_ge(att_ready, b)
                for dst, r in ((num, 0), (den, HD)):
                    sp.dma_start(dst[:, :], bass.AP(g["o_dram"].tensor, b * (VW * T) + r * T, [[B * VW * T, HEADS], [T, HD], [1, T]])).then_inc(o_loaded, 16)
                for u in range(CPB):
                    sp.wait_ge(out_ready, b * CPB + u + 1)
                    dst = bass.AP(out.tensor, b * (T * D) + u * CH * D, [[D, P], [P * D, TPC], [1, D]])
                    sp.dma_start(dst, res[:, u, :, :]).then_inc(out_stored[u], 16)

            batches(sp, body)
            for u in range(CPB):
                sp.wait_ge(out_stored[u], 16 * B)

        @block.vector
        def _(dve):
            dve.memset(xT[:, 0:1], 0.0).then_inc(mu_ready, 1)
            dve.tensor_scalar(omm[:, :], g["mu"][:, :], -1.0, 1.0, ALU.mult, ALU.add).then_inc(mu_ready, 1)
            dve.wait_ge(mu_ready, 2)

            def body(b, first):
                st = Steps(dve, dve_steps, b * N_STEPS)
                dve.wait_ge(o_loaded, b * 32 + 32)
                st.did(dve.reciprocal(den[:, :], den[:, :]))
                st.settle()
                if not first:
                    dve.wait_ge(att_turned, b * CPB)
                dve.tensor_tensor(att[:, :], num[:, :], den[:, :], ALU.mult).then_inc(att_ready, 1)
                for u in range(CPB):
                    c = b * CPB + u
                    dve.wait_ge(att_turned, c + 1)
                    xs = g["x"][:, bass.ds(b * TPB + u * TPC, TPC), :]
                    st.did(dve.tensor_tensor(xs, psA[u][:, :, :], xs, ALU.add))
                    st.settle_alone(s["passed"])
                    normalise(dve, st, g, c, u, s, b)
                    dve.wait_ge(xT_ready, c + 1)
                    if not first:
                        dve.wait_ge(wide_done, c - 1)
                    for i in range(2):
                        last = dve.tensor_scalar(prev[:, u, i, :], xT[:, u * CH:u * CH + CH], omm[:, i:i + 1], None, ALU.mult)
                    last.then_inc(prev_ready, 1)
                    dve.wait_ge(prev_ready, c + 1)
                    for i in range(2):
                        last = dve.scalar_tensor_tensor(mix[:, u, i, :], xT[:, u * CH + 1:u * CH + CH + 1], g["mu"][:, i:i + 1], prev[:, u, i, :], ALU.mult, ALU.add)
                    last.then_inc(mix_ready, 1)
                    dve.wait_ge(relu_done, c + 1)
                    dve.tensor_tensor(kact[:, u, :], kact[:, u, :], kact[:, u, :], ALU.mult).then_inc(kact_ready, 1)
                    dve.wait_ge(gate_ready, c + 1)
                    dve.wait_ge(wide_done, c + 1)
                    if not first:
                        dve.wait_ge(out_stored[u], b * 16)
                    r2 = res[:, u, :, :].rearrange("p t d -> p (t d)")
                    st.did(dve.tensor_tensor(r2, psV[:, :], gate[:, u, :], ALU.mult))
                    st.settle()
                    dve.tensor_tensor(res[:, u, :, :], res[:, u, :, :], xs, ALU.add).then_inc(out_ready, 1)
                n_used.append(st.n)

            n_used = []
            batches(dve, body)
            assert n_used[0] == N_STEPS, (n_used[0], N_STEPS)

        @block.scalar
        def _(act):
            def body(b, first):
                for u in range(CPB):
                    c = b * CPB + u
                    act.wait_ge(s["var_ready"], c + 1)
                    act.activation(s["root"][:, u, :], s["var"][:, u, :], ACT.Sqrt).then_inc(s["root_ready"], 1)
                    act.wait_ge(transposed, c + 1)
                    if not first or u:
                        act.wait_ge(mix_ready, c)
                    act.activation(xT[:, 1 + u * CH:1 + (u + 1) * CH], psT[u][:, :], ACT.Copy).then_inc(xT_ready, 1)
                    act.wait_ge(keys_done, c + 1)
                    act.activation(kact[:, u, :], psK[:, :], ACT.Relu).then_inc(relu_done, 1)
                    act.wait_ge(gates_done, c + 1)
                    act.activation(gate[:, u, :], psR[:, :], ACT.Sigmoid).then_inc(gate_ready, 1)

            batches(act, body)

        @block.tensor
        def _(pe):
            def body(b, first):
                pe.wait_ge(att_ready, b + 1)
                for u in range(CPB):
                    for t in range(TPC):
                        last = pe.transpose(psA[u][:, t, :], att[:, (u * TPC + t) * P:(u * TPC + t + 1) * P], g["identf"][:, :])
                    last.then_inc(att_turned, 1)
                for u in range(CPB):
                    c = b * CPB + u
                    pe.wait_ge(s["xn_ready"], c + 1)
                    for t in range(TPC):
                        last = pe.transpose(psT[u][:, t * P:(t + 1) * P], s["xn"][:, u, t, :], g["identf"][:, :])
                    last.then_inc(transposed, 1)
                    pe.wait_ge(mix_ready, c + 1)
                    pe.matmul(psK[:, :], g["w_d"][:, 1, :], mix[:, u, 1, :], start=True, stop=True).then_inc(keys_done, 1)
                    for t in range(TPC):
                        last = pe.matmul(psR[:, t * P:(t + 1) * P], mix[:, u, 0, t * P:(t + 1) * P], g["w_d"][:, 0, :], start=True, stop=True)
                    last.then_inc(gates_done, 1)
                    pe.wait_ge(kact_ready, c + 1)
                    if not first or u:
                        pe.wait_ge(out_ready, c)
                    for t in range(TPC):
                        last = pe.matmul(psV[:, t * P:(t + 1) * P], kact[:, u, t * P:(t + 1) * P], g["w_d"][:, 2, :], start=True, stop=True)
                    last.then_inc(wide_done, 1)

            batches(pe, body)


def build(nc, ins, out, phases=99):
    ctx = ExitStack()
    with ctx:
        gm = Mem(nc, ctx, "g")
        g = {
            "x": gm.sb("x", [P, NT, D]),
            "identf": gm.sb("identf", [P, P]), "identb": gm.sb("identb", [P, P], BF16),
            "w_a": gm.sb("w_a", [P, 4, D]), "w_c": gm.sb("w_c", [P, 3, D]), "w_d": gm.sb("w_d", [P, 3, D]),
            "node_wT": gm.sb("node_wT", [P, FF * NODES]), "node_b": gm.sb("node_b", [P, FF * NODES]),
            "bias_qk": gm.sb("bias_qk", [P, 2]), "bv": gm.sb("bv", [P, D]), "bo": gm.sb("bo", [P, D]),
            "mu": gm.sb("mu", [P, 2]), "b1": gm.sb("b1", [P, FF, HID]),
            "tri": gm.sb("tri", [P, NEAR]), "maskneg": gm.sb("maskneg", [P, P], BF16),
            "masknegT": gm.sb("masknegT", [P, P], BF16),
            "q_dram": nc.dram_tensor("q_parts", [HEADS, B, PARTS, HD, T], BF16, kind="Internal").ap(),
            "k_dram": nc.dram_tensor("k_parts", [HEADS, B, PARTS, HD, T], BF16, kind="Internal").ap(),
            "o_dram": nc.dram_tensor("head_outputs", [HEADS, B, VW, T], F32, kind="Internal").ap(),
            "erow_dram": nc.dram_tensor("bias_rows", [HEADS, ERW], F32, kind="Internal").ap(),
        }

        def phase(tag, f, *args):
            with ExitStack() as own:
                f(nc, Mem(nc, own, tag), g, *args)

        g["w1"], g["w2"] = gm.sb("w1", [P, FF, LEAVES * LW]), gm.sb("w2", [P, FF, HID, D])
        g["b2p"] = gm.sb("b2p", [P, PARTS, FF, D], BF16)
        g["leafx"] = gm.sb("leafx", [P, FF * LEAVES * LW], BF16)
        g["selT"] = gm.sb("selT", [P, B * T], BF16)

        with ExitStack() as one:
            m1 = Mem(nc, one, "one")
            g["ebias"] = m1.sb("ebias", [P, HEADS, NEAR])
            g["v_all"] = m1.sb("v_all", [P, HEADS, B, TPB, HD])
            phase("setup", load_weights, ins)
            phase("proj1", project_heads, g["w_a"], True)
            phase("heads1", attend_heads, True)
        if phases < 3:
            return
        with ExitStack() as two:
            m2 = Mem(nc, two, "two")
            g["xnT_all"] = m2.sb("xnT_all", [P, B * T])
            g["qkT"], g["v_tok"] = m2.sb("qkT", [P, 2, B * T]), m2.sb("v_tok", [P, NT, D])
            phase("route", route_and_add)
            phase("trees", trees)
            phase("wide", attend_wide)
        with ExitStack() as three:
            g["v_all"] = Mem(nc, three, "three").sb("v_all", [P, HEADS, B, TPB, HD])
            phase("proj3", project_heads, g["w_c"], False)
            phase("heads3", attend_heads, False)
        phase("finish", finish_layers, out)


def bucket_onehot():
    import numpy as np

    n = np.arange(P + NEAR) - (P - 1)
    near = np.maximum(n, 0)
    exact = BUCKETS // 2
    ratio = np.log(np.maximum(near, 1).astype(np.float32) / np.float32(exact)) / np.float32(np.log(MAX_DIST / exact))
    large = np.minimum(exact + (ratio * np.float32(BUCKETS - exact)).astype(np.int32), BUCKETS - 1)
    bucket = np.where(near < exact, near, large)
    table = (np.arange(BUCKETS)[:, None] == bucket[None, :]).astype(np.float32)
    table[BUCKETS - 1] -= 1.0
    return table


_INS = ['L0_attn_x', 'L0_attn_Wq', 'L0_attn_bq', 'L0_attn_Wk', 'L0_attn_bk', 'L0_attn_Wv', 'L0_attn_bv', 'L0_attn_Wo',
        'L0_attn_bo', 'L0_attn_rel_emb', 'L0_ffn_q_node_w', 'L0_ffn_q_node_b', 'L0_ffn_q_w1', 'L0_ffn_q_b1',
        'L0_ffn_q_w2', 'L0_ffn_q_b2', 'L0_ffn_k_node_w', 'L0_ffn_k_node_b', 'L0_ffn_k_w1', 'L0_ffn_k_b1',
        'L0_ffn_k_w2', 'L0_ffn_k_b2', 'L0_ffn_v_node_w', 'L0_ffn_v_node_b', 'L0_ffn_v_w1', 'L0_ffn_v_b1',
        'L0_ffn_v_w2', 'L0_ffn_v_b2', 'L1_attn_Wq', 'L1_attn_Wk', 'L1_attn_Wv', 'L1_ffn_W_r', 'L1_ffn_W_k',
        'L1_ffn_W_v', 'L1_ffn_mu_r', 'L1_ffn_mu_k']


def kernel(**inputs):
    import numpy as _np
    import concourse.bacc as _bacc
    from concourse import mybir as _mybir
    from concourse.bass_utils import run_bass_kernel_spmd as _run

    nc = _bacc.Bacc("TRN2", target_bir_lowering=False, num_devices=1)
    arrays, ins = {}, {}
    for name in [*_INS, "bucket_onehot"]:
        a = bucket_onehot() if name == "bucket_onehot" else _np.ascontiguousarray(inputs[name])
        arrays[f"in_{name}"] = a
        ins[name] = nc.dram_tensor(f"in_{name}", a.shape, _mybir.dt.from_np(a.dtype), kind="ExternalInput").ap()
    out = nc.dram_tensor("out_x", (B, T, D), F32, kind="ExternalOutput").ap()
    build(nc, ins, out)
    r = _run(nc, [arrays], core_ids=[0])
    return r.results[0]["out_x"]
```

```python
from contextlib import ExitStack

import concourse.bass as bass
from concourse import mybir

ALU = mybir.AluOpType
ACT = mybir.ActivationFunctionType
AXX = mybir.AxisListType.X
F32 = mybir.dt.float32
BF16 = mybir.dt.bfloat16

P = 128
B = 4
T = 1024
D = 128
HEADS = 16
HD = D // HEADS
NT = B * T // P
TPB = T // P
CH = 512
TPC = CH // P
CPB = T // CH
NCH = B * T // CH
EPS = 1e-5
PARTS = 3
SROWS = PARTS * PARTS * HD
MROW = 96
HSZ = PARTS * HD * T
BUCKETS = 32
MAX_DIST = 128
NEAR = 2 * P
ERW = 3 * P
NEG = -1.0e30
HEAD_SCALE = HD ** -0.5
LEAVES = 16
NODES = 15
DEPTH = 4
LW = 64
FF = 3
HID = LEAVES * LW // P
SELROW = 64
VW = 32


class Mem:

    def __init__(self, nc, ctx, tag):
        self.nc, self.ctx, self.tag = nc, ctx, tag

    def sb(self, name, shape, dt=F32):
        return self.ctx.enter_context(self.nc.sbuf_tensor(f"{self.tag}_{name}", shape, dt))

    def ps(self, name, shape, dt=F32):
        return self.ctx.enter_context(self.nc.psum_tensor(f"{self.tag}_{name}", shape, dt))

    def sem(self, name):
        return self.nc.alloc_semaphore(name=f"{self.tag}_{name}")


class Steps:

    def __init__(self, eng, sem, base=0):
        self.eng, self.sem, self.base, self.n = eng, sem, base, 0

    def did(self, ins):
        self.n += 1
        return ins.then_inc(self.sem, 1)

    def settle(self):
        self.eng.wait_ge(self.sem, self.base + self.n)

    def settle_alone(self, passed):
        wait_alone(self.eng, self.sem, self.base + self.n, passed)


def wait_alone(eng, sem, value, passed):
    eng.wait_ge(sem, value)
    eng.sem_inc(passed, 1)


def load_weights(nc, m, g, ins):
    wnat = m.sb("wnat", [P, 7, D])
    nodes_nat = m.sb("nodes_nat", [FF * NODES, D])
    rel = m.sb("rel", [BUCKETS, HEADS])
    onehot = m.sb("onehot", [BUCKETS, ERW])
    erow = m.sb("erow", [HEADS, ERW])
    identf = g["identf"]
    ebrev = m.sb("ebrev", [P, HEADS, NEAR])
    flip = m.sb("flip", [P, P])
    b2f = m.sb("b2f", [P, FF, D])
    b2d = m.sb("b2d", [P, FF, D])
    psW = m.ps("psW", [P, 8, D])
    psN = m.ps("psN", [P, 512])
    psE = m.ps("psE", [P, 512])
    psF = [m.ps(f"psF{i}", [P, CH]) for i in range(2)]
    flipped, flip_taken = m.sem("flipped"), m.sem("flip_taken")
    loaded_x, loaded_w, loaded_misc = m.sem("loaded_x"), m.sem("loaded_w"), m.sem("loaded_misc")
    loaded_b2 = m.sem("loaded_b2")
    made, zeroed = m.sem("made"), m.sem("zeroed")
    transposed, bias_ready, erow_ready = m.sem("transposed"), m.sem("bias_ready"), m.sem("erow_ready")
    erow_stored, eb_loaded = m.sem("erow_stored"), m.sem("eb_loaded")
    copied, split = m.sem("copied"), m.sem("split")
    squares = ["L0_attn_Wq", "L0_attn_Wk", "L0_attn_Wv", "L0_attn_Wo", "L1_ffn_W_r", "L1_ffn_W_k", "L1_ffn_W_v"]

    def bcast(name, parts=P):
        a = ins[name]
        n = 1
        for s in a.shape:
            n *= s
        return bass.AP(a.tensor, 0, [[0, parts], [1, n]])

    def column(name):
        return ins[name].rearrange("(d o) -> d o", o=1)

    W_N = len(squares) + FF

    with nc.Block() as block:

        @block.sync
        def _(sp):
            for i, name in enumerate(squares):
                sp.dma_start(wnat[:, i, :], ins[name]).then_inc(loaded_w, 16)
            for f, n in enumerate("qkv"):
                sp.dma_start(nodes_nat[f * NODES:(f + 1) * NODES, :], ins[f"L0_ffn_{n}_node_w"]).then_inc(loaded_w, 16)
            sp.dma_start(rel[:, :], ins["L0_attn_rel_emb"]).then_inc(loaded_misc, 16)
            sp.dma_start(onehot[:, :], ins["bucket_onehot"]).then_inc(loaded_misc, 16)
            x_t = ins["L0_attn_x"].rearrange("b (t p) d -> p (b t) d", p=P)
            for b in range(B):
                sp.dma_start(g["x"][:, b * TPB:(b + 1) * TPB, :], x_t[:, b * TPB:(b + 1) * TPB, :]).then_inc(loaded_x, 16)
            for i, name in enumerate(["L1_attn_Wq", "L1_attn_Wk", "L1_attn_Wv"]):
                sp.dma_start(g["w_c"][:, i, :], ins[name]).then_inc(loaded_x, 16)
            sp.wait_ge(loaded_w, 16 * W_N)
            sp.wait_ge(loaded_x, 16 * (B + 3))
            sp.wait_ge(erow_ready, 2)
            sp.dma_start(g["erow_dram"], erow[:, :]).then_inc(erow_stored, 16)
            sp.wait_ge(erow_stored, 16)
            sp.dma_start(ebrev[:, :, :], bass.AP(g["erow_dram"].tensor, 0, [[1, P], [ERW, HEADS], [1, NEAR]])).then_inc(eb_loaded, 16)

        @block.scalar
        def _(act):
            n = 0
            with nc.allow_non_contiguous_dma(reason="columns of biases, once"):
                for i, name in enumerate(["L0_attn_bq", "L0_attn_bk"]):
                    act.dma_start(g["bias_qk"][:, i:i + 1], column(name)).then_inc(loaded_misc, 16)
                for i, name in enumerate(["L1_ffn_mu_r", "L1_ffn_mu_k"]):
                    act.dma_start(g["mu"][:, i:i + 1], column(name)).then_inc(loaded_misc, 16)
                for f, nm in enumerate("qkv"):
                    act.dma_start(g["b1"][:, f, :], ins[f"L0_ffn_{nm}_b1"].rearrange("(m l) h -> (l h) m", l=2)).then_inc(loaded_misc, 16)
            act.dma_start(g["bv"][:, :], bcast("L0_attn_bv")).then_inc(loaded_misc, 16)
            act.dma_start(g["bo"][:, :], bcast("L0_attn_bo")).then_inc(loaded_misc, 16)
            for f, nm in enumerate("qkv"):
                act.dma_start(g["node_b"][:, f * NODES:(f + 1) * NODES], bcast(f"L0_ffn_{nm}_node_b")).then_inc(loaded_misc, 16)
                act.dma_start(g["w1"][:, f, :].rearrange("d (l h) -> d l h", l=LEAVES), ins[f"L0_ffn_{nm}_w1"].rearrange("l d h -> d l h")).then_inc(loaded_misc, 16)
                act.dma_start(g["w2"][:, f, :, :], ins[f"L0_ffn_{nm}_w2"].rearrange("(m l) h o -> (l h) m o", l=2)).then_inc(loaded_misc, 16)
            act.wait_ge(zeroed, 1)
            for f, nm in enumerate("qkv"):
                r = SELROW + f * LEAVES
                act.dma_start(b2f[r:r + LEAVES, f, :], ins[f"L0_ffn_{nm}_b2"]).then_inc(loaded_b2, 16)
            act.wait_ge(bias_ready, 1)
            act.activation(erow[:, :], psE[0:HEADS, 0:ERW], ACT.Exp, scale=HEAD_SCALE).then_inc(erow_ready, 1)
            act.wait_ge(transposed, 1)
            act.activation(g["w_a"][:, :, :], psW[:, 0:4, :], ACT.Copy).then_inc(copied, 1)
            act.activation(g["w_d"][:, :, :], psW[:, 4:7, :], ACT.Copy).then_inc(copied, 1)
            act.activation(g["node_wT"][:, :], psN[:, 0:FF * NODES], ACT.Copy).then_inc(copied, 1)
            act.wait_ge(copied, 3)
            for i in range(HEADS // 2):
                act.wait_ge(flipped, i + 1)
                act.activation(g["ebias"][:, 2 * i:2 * i + 2, :].rearrange("p h q -> p (h q)"), psF[i % 2][:, :], ACT.Copy).then_inc(flip_taken, 1)
            act.wait_ge(flip_taken, HEADS // 2)
            act.wait_ge(loaded_misc, 16 * (2 + 7 + 2 + 3 * FF))

        @block.gpsimd
        def _(pool):
            st = Steps(pool, made)
            st.did(pool.memset(identf[:, :], 0.0))
            st.did(pool.memset(g["identb"][:, :], 0.0))
            st.did(pool.memset(flip[:, :], 0.0))
            st.did(pool.memset(g["tri"][:, :], 1.0))
            st.did(pool.memset(g["maskneg"][:, :], 0.0))
            st.did(pool.memset(g["masknegT"][:, :], 0.0))
            st.did(pool.memset(g["leafx"][:, :], -NEG))
            st.settle()
            for t in (identf, g["identb"]):
                st.did(pool.affine_select(out=t[:, :], in_=t[:, :], compare_op=ALU.not_equal, fill=1.0, base=0,
                                          pattern=[[-1, P]], channel_multiplier=1))
            st.did(pool.affine_select(out=flip[:, :], in_=flip[:, :], compare_op=ALU.not_equal, fill=1.0, base=1 - P,
                                      pattern=[[1, P]], channel_multiplier=1))
            st.did(pool.affine_select(out=g["tri"][:, :], in_=g["tri"][:, :], compare_op=ALU.is_ge, fill=0.0, base=0,
                                      pattern=[[1, NEAR]], channel_multiplier=-1))
            st.did(pool.affine_select(out=g["maskneg"][:, :], in_=g["maskneg"][:, :], compare_op=ALU.is_ge, fill=NEG, base=0,
                                      pattern=[[-1, P]], channel_multiplier=1))
            st.did(pool.affine_select(out=g["masknegT"][:, :], in_=g["masknegT"][:, :], compare_op=ALU.is_ge, fill=NEG, base=0,
                                      pattern=[[1, P]], channel_multiplier=-1))
            st.did(pool.affine_select(out=g["leafx"][:, :], in_=g["leafx"][:, :], compare_op=ALU.is_ge, fill=0.0, base=0,
                                      pattern=[[1, FF * LEAVES * LW]], channel_multiplier=-LW))
            st.settle()
            st.did(pool.affine_select(out=g["leafx"][:, :], in_=g["leafx"][:, :], compare_op=ALU.is_ge, fill=0.0, base=LW - 1,
                                      pattern=[[-1, FF * LEAVES * LW]], channel_multiplier=LW))
            st.settle()

        @block.vector
        def _(dve):
            dve.memset(b2f[:, :, :], 0.0).then_inc(zeroed, 1)
            st = Steps(dve, split)
            st.did(dve.memset(g["selT"][:, :], 0.0))
            dve.wait_ge(erow_ready, 1)
            dve.memset(erow[:, 0:P - 1], 0.0).then_inc(erow_ready, 1)
            dve.wait_ge(loaded_b2, 16 * FF)
            dve.wait_ge(zeroed, 1)
            for i in range(PARTS):
                src = b2f if i == 0 else b2d
                st.did(dve.tensor_copy(g["b2p"][:, i, :, :], src[:, :, :]))
                st.settle()
                if i < PARTS - 1:
                    st.did(dve.tensor_tensor(b2d[:, :, :], src[:, :, :], g["b2p"][:, i, :, :], ALU.subtract))
                    st.settle()

        @block.tensor
        def _(pe):
            pe.wait_ge(loaded_misc, 16 * (2 + 7 + 2 + 3 * FF))
            pe.matmul(psE[0:HEADS, 0:ERW], rel[:, :], onehot[:, :], start=True, stop=True).then_inc(bias_ready, 1)
            pe.wait_ge(made, 10)
            pe.wait_ge(loaded_w, 16 * W_N)
            for i in range(7):
                pe.transpose(psW[:, i, :], wnat[:, i, :], identf[:, :])
            pe.transpose(psN[:, 0:FF * NODES], nodes_nat[:, :], identf[0:FF * NODES, 0:FF * NODES]).then_inc(transposed, 1)
            pe.wait_ge(eb_loaded, 16)
            for i in range(HEADS // 2):
                if i >= 2:
                    pe.wait_ge(flip_taken, i - 1)
                pe.matmul(psF[i % 2][:, :], flip[:, :], ebrev[:, 2 * i:2 * i + 2, :].rearrange("p h q -> p (h q)"), start=True, stop=True).then_inc(flipped, 1)


def pipeline(eng, stages, count=NCH):
    most = max(lag for _, lag in stages)
    start = most + 2 + most % 2

    def step(n, u, static):
        for stage, lag in stages:
            if not static:
                stage(n - lag, (u - lag) % 2, False)
            elif 0 <= n - lag < count:
                stage(n - lag, (u - lag) % 2, n - lag < 2)

    for n in range(start):
        step(n, n % 2, True)
    if start < count:
        with eng.Fori(start // 2, count // 2) as pair:
            for u in range(2):
                step(pair * 2 + u, u, False)
    for n in range(count, count + most):
        step(n, n % 2, True)


class Norm:
    STATS, SCALE = TPC + TPC, 4

    def __init__(self, m, x):
        self.x = x
        self.stats, self.mv = m.sb("stats", [P, 2, TPC, 6]), m.sb("mv", [P, 2, TPC, 2])
        self.var, self.root = m.sb("var", [P, 2, TPC]), m.sb("root", [P, 2, TPC])
        self.newton, self.xn = m.sb("newton", [P, 2, 2, TPC]), m.sb("xn", [P, 2, TPC, D])
        self.stat_steps, self.scale_steps = m.sem("stat_steps"), m.sem("scale_steps")
        self.var_ready, self.root_ready, self.xn_ready = m.sem("var_ready"), m.sem("root_ready"), m.sem("xn_ready")
        self.passed = m.sem("passed")

    def statistics(self, dve, c, u):
        st = Steps(dve, self.stat_steps, c * self.STATS)
        for t in range(TPC):
            st.did(dve.bn_stats(self.stats[:, u, t, :], self.x[:, c * TPC + t, :]))
        st.settle_alone(self.passed)
        for t in range(TPC):
            st.did(dve.bn_aggr(self.mv[:, u, t, :], self.stats[:, u, t, :]))
        st.settle()
        dve.tensor_scalar(self.var[:, u, :], self.mv[:, u, :, 1], EPS, None, ALU.add).then_inc(self.var_ready, 1)

    def take_root(self, act, c, u):
        act.wait_ge(self.var_ready, c + 1)
        act.activation(self.root[:, u, :], self.var[:, u, :], ACT.Sqrt).then_inc(self.root_ready, 1)

    def scale(self, dve, c, u, transposed, early):
        st = Steps(dve, self.scale_steps, c * self.SCALE)
        r, t = self.newton[:, u, 0, :], self.newton[:, u, 1, :]
        dve.wait_ge(self.root_ready, c + 1)
        st.did(dve.reciprocal(r, self.root[:, u, :]))
        st.settle()
        st.did(dve.scalar_tensor_tensor(t, r, -0.5, r, ALU.mult, ALU.mult))
        st.settle()
        st.did(dve.tensor_tensor(t, t, self.var[:, u, :], ALU.mult))
        st.settle()
        st.did(dve.scalar_tensor_tensor(r, t, 1.5, r, ALU.add, ALU.mult))
        st.settle()
        if not early:
            dve.wait_ge(transposed, c - 1)
        for t in range(TPC):
            last = dve.tensor_scalar(self.xn[:, u, t, :], self.x[:, c * TPC + t, :], self.mv[:, u, t, 0:1],
                                     self.newton[:, u, 0, t:t + 1], ALU.subtract, ALU.mult)
        last.then_inc(self.xn_ready, 1)


def project_heads(nc, m, g, w, biased):
    norm = Norm(m, g["x"])
    xnT = m.sb("xnT", [P, 2, CH])
    qk = m.sb("qk", [P, 2, 2, CH])
    rest = m.sb("rest", [P, 2, 2, CH])
    parts = [m.sb(f"parts{u}", [P, 2, PARTS, CH], BF16) for u in range(2)]
    psT = [m.ps(f"psT{u}", [P, CH]) for u in range(2)]
    psQK = [m.ps(f"psQK{u}", [P, 2, CH]) for u in range(2)]
    psV = [m.ps(f"psV{u}", [P, TPC, D]) for u in range(2)]
    transposed, xnT_ready = m.sem("transposed"), m.sem("xnT_ready")
    qkv_done, qk_ready, v_taken = m.sem("qkv_done"), m.sem("qk_ready"), m.sem("v_taken")
    hi_ready, rest_ready, mid_ready, lo_ready = m.sem("hi_ready"), m.sem("rest_ready"), m.sem("mid_ready"), m.sem("lo_ready")
    passed = m.sem("passed_split")
    stored = [m.sem(f"stored{u}") for u in range(2)]
    STORES = 2 * PARTS

    with nc.Block() as block:

        @block.vector
        def _(dve):
            def statistics(c, u, early):
                norm.statistics(dve, c, u)

            def scale(c, u, early):
                norm.scale(dve, c, u, transposed, early)

            def values(c, u, early):
                dve.wait_ge(qkv_done, c + 1)
                v_all = g["v_all"][:, :, :, :].rearrange("p h (c t) e -> p h c t e", t=TPC)
                for t in range(TPC):
                    vout = v_all[:, :, c, t, :]
                    vin = psV[u][:, t, :].rearrange("p (h e) -> p h e", h=HEADS)
                    if biased:
                        last = dve.tensor_tensor(vout, vin, g["bv"][:, :].rearrange("p (h e) -> p h e", h=HEADS), ALU.add)
                    else:
                        last = dve.tensor_copy(vout, vin)
                last.then_inc(v_taken, 1)

            def lows(c, u, early):
                dve.wait_ge(mid_ready, c + 1)
                dve.tensor_tensor(parts[u][:, :, 2, :], rest[:, u], parts[u][:, :, 1, :], ALU.subtract).then_inc(lo_ready, 1)

            pipeline(dve, [(scale, 1), (statistics, 0), (values, 3), (lows, 4)])

        @block.gpsimd
        def _(pool):
            def rests(c, u, early):
                wait_alone(pool, hi_ready, c + 1, passed)
                pool.tensor_tensor(rest[:, u], qk[:, u], parts[u][:, :, 0, :], ALU.subtract).then_inc(rest_ready, 1)

            pipeline(pool, [(rests, 3)])

        @block.scalar
        def _(act):
            def root(c, u, early):
                norm.take_root(act, c, u)

            def turned(c, u, early):
                act.wait_ge(transposed, c + 1)
                if not early:
                    act.wait_ge(qkv_done, c - 1)
                act.activation(xnT[:, u, :], psT[u][:, :], ACT.Copy).then_inc(xnT_ready, 1)

            def highs(c, u, early):
                act.wait_ge(qkv_done, c + 1)
                if not early:
                    act.wait_ge(rest_ready, c - 1)
                for i in range(2):
                    if biased:
                        ins = act.activation(qk[:, u, i, :], psQK[u][:, i, :], ACT.Identity, bias=g["bias_qk"][:, i:i + 1])
                    else:
                        ins = act.activation(qk[:, u, i, :], psQK[u][:, i, :], ACT.Copy)
                ins.then_inc(qk_ready, 1)
                act.wait_ge(qk_ready, c + 1)
                if not early:
                    act.wait_ge(stored[u], (c - u) * (8 * STORES))
                act.activation(parts[u][:, :, 0, :], qk[:, u], ACT.Copy).then_inc(hi_ready, 1)

            def mids(c, u, early):
                act.wait_ge(rest_ready, c + 1)
                act.activation(parts[u][:, :, 1, :], rest[:, u], ACT.Copy).then_inc(mid_ready, 1)

            pipeline(act, [(turned, 1), (root, 0), (highs, 3), (mids, 4)])

        @block.tensor
        def _(pe):
            def turn(c, u, early):
                pe.wait_ge(norm.xn_ready, c + 1)
                if not early:
                    pe.wait_ge(xnT_ready, c - 1)
                for t in range(TPC):
                    last = pe.transpose(psT[u][:, t * P:(t + 1) * P], norm.xn[:, u, t, :], g["identf"][:, :])
                last.then_inc(transposed, 1)

            def project(c, u, early):
                pe.wait_ge(xnT_ready, c + 1)
                if not early:
                    pe.wait_ge(qk_ready, c - 1)
                    pe.wait_ge(v_taken, c - 1)
                for i in range(2):
                    pe.matmul(psQK[u][:, i, :], w[:, i, :], xnT[:, u, :], start=True, stop=True)
                for t in range(TPC):
                    last = pe.matmul(psV[u][:, t, :], xnT[:, u, t * P:(t + 1) * P], w[:, 2, :], start=True, stop=True)
                last.then_inc(qkv_done, 1)

            pipeline(pe, [(turn, 1), (project, 2)])

        @block.sync
        def _(sp):
            def store(part, ready):
                def run(c, u, early):
                    sp.wait_ge(ready, c + 1)
                    at = (c - u) * (HSZ // 2) + u * CH
                    q = bass.AP(g["q_dram"].tensor, at + part * HD * T, [[B * HSZ, HEADS], [T, HD], [1, CH]])
                    sp.dma_start(q, parts[u][:, 0, part, :]).then_inc(stored[u], 16)
                    k = bass.AP(g["k_dram"].tensor, at + part * T, [[B * HSZ, HEADS], [PARTS * T, HD], [1, CH]])
                    sp.dma_start(k, parts[u][:, 1, part, :]).then_inc(stored[u], 16)
                return run

            pipeline(sp, [(store(0, hi_ready), 0), (store(1, mid_ready), 1), (store(2, lo_ready), 1)])
            for u in range(2):
                sp.wait_ge(stored[u], 16 * STORES * NCH // 2)


def attend_heads(nc, m, g, causal):
    NG = HEADS * B
    LAG = 3
    if causal:
        halves = [[h for h in range(2) if (h + 1) * CH > kb * P] for kb in range(TPB)]
    else:
        halves = [[0, 1] for kb in range(TPB)]
    first_unit = [sum(len(x) for x in halves[:kb]) for kb in range(TPB + 1)]
    UNITS = first_unit[-1]
    assert UNITS % 2 == 0

    def columns(kb, h):
        lo = max(h * CH, kb * P) if causal else h * CH
        return lo, (h + 1) * CH

    def near(kb):
        if causal:
            return kb * P, min(T, kb * P + NEAR)
        return kb * P, (kb + 2 - kb % 2) * P

    qS = [m.sb(f"qS{u}", [P, T], BF16) for u in range(B)]
    kS = [m.sb(f"kS{u}", [P, T], BF16) for u in range(B)]
    probs = [m.sb(f"probs{p}", [P, TPB, T]) for p in range(2)]
    masked = [m.sb(f"masked{p}", [P, TPB, NEAR]) for p in range(2)] if not causal else None
    v_ones = [m.sb(f"v_ones{p}", [P, TPB, VW]) for p in range(2)]
    v_only = [m.sb(f"v_only{p}", [P, TPB, VW]) for p in range(2)] if not causal else None
    ones_only = m.sb("ones_only", [P, VW]) if not causal else None
    mx = m.sb("mx", [P, 2, TPB])
    nm = m.sb("nm", [P, 2, 2, TPB], BF16)
    mrow = [m.sb(f"mrow{p}", [2 * TPB, P], BF16) for p in range(2)]
    oT = [m.sb(f"oT{p}", [P, 2 * P]) for p in range(2)]
    psM = [m.ps(f"psM{i}", [P, T]) for i in range(2)]
    psS = [m.ps(f"psS{i}", [P, CH]) for i in range(2)]
    psO = m.ps("psO", [P, CH])
    psR = m.ps("psR", [P, CH])

    cleared, pool_ready = m.sem("cleared"), m.sem("pool_ready")
    s_loaded = [m.sem(f"s_loaded{u}") for u in range(B)]
    r_loaded = [m.sem(f"r_loaded{u}") for u in range(B)]
    o_stored = [m.sem(f"o_stored{p}") for p in range(2)]
    maxima_done = m.sem("maxima_done")
    max_taken = m.sem("max_taken")
    nm_hi, nm_ready = m.sem("nm_hi"), m.sem("nm_ready")
    rows_done, rows_taken = m.sem("rows_done"), m.sem("rows_taken")
    scores_done = m.sem("scores_done")
    exp_done = m.sem("exp_done")
    near_done = m.sem("near_done")
    v_staged, passed = m.sem("v_staged"), m.sem("passed")
    pv_done, o_taken = m.sem("pv_done"), m.sem("o_taken")

    def program(eng, step):
        for u in range(B):
            step(u, u, u)
        with eng.Fori(1, HEADS - 1) as h:
            for u in range(B):
                step(h * B + u, u, None)
        for u in range(B):
            step(NG - B + u, u, NG - B + u)

    with nc.Block() as block:

        @block.sync
        def _(sp):
            sp.wait_ge(cleared, 1)

            def load_s(n, u):
                q = bass.AP(g["q_dram"].tensor, n * HSZ, [[T, PARTS * HD], [0, PARTS], [1, T]])
                sp.dma_start(qS[u][0:SROWS, :], q).then_inc(s_loaded[u], 16)
                k = bass.AP(g["k_dram"].tensor, n * HSZ, [[0, PARTS], [T, HD * PARTS], [1, T]])
                sp.dma_start(kS[u][0:SROWS, :], k).then_inc(s_loaded[u], 16)

            def load_r(n, u):
                sp.wait_ge(rows_taken, n + 1)
                sp.dma_start(qS[u][MROW:MROW + 2, :].rearrange("s (q w) -> s q w", w=P), mrow[u % 2][:, :]).then_inc(r_loaded[u], 16)

            for n in range(3):
                load_s(n, n)
            load_r(0, 0)

            def step(n, u, known):
                if known is None or known < NG - 3:
                    if known != 0:
                        sp.wait_ge(scores_done, n * UNITS)
                    load_s(n + 3, (u + 3) % B)
                if known is None or known < NG - 1:
                    load_r(n + 1, (u + 1) % B)
                if known != 0:
                    sp.wait_ge(o_taken, n)
                    sp.dma_start(store_at(n - 1), oT[(u + 1) % 2][:, :]).then_inc(o_stored[(u + 1) % 2], 16)

            def store_at(n):
                return bass.AP(g["o_dram"].tensor, n * (VW * T), [[2 * P, 4], [T, VW], [1, 2 * P]])

            program(sp, step)
            sp.wait_ge(o_taken, NG)
            sp.dma_start(store_at(NG - 1), oT[1][:, :]).then_inc(o_stored[1], 16)
            for p in range(2):
                sp.wait_ge(o_stored[p], 16 * NG // 2)

        @block.vector
        def _(dve):
            for u in range(B):
                dve.memset(qS[u][:, :].bitcast(F32), 0.0)
                last = dve.memset(kS[u][:, :], 1.0)
            last.then_inc(cleared, 1)

            def maxima(n, p, static):
                for qb in range(TPB):
                    dve.wait_ge(maxima_done, n * TPB + qb + 1)
                    w = (qb + 1) * P if causal else T
                    if qb == 0 and (static is None or static >= 2):
                        dve.wait_ge(nm_ready, n - 1)
                    dve.tensor_reduce(mx[:, p, qb:qb + 1], psM[qb % 2][:, 0:w], AXX, ALU.max).then_inc(max_taken, 1)
                dve.wait_ge(max_taken, (n + 1) * TPB)
                if static is None or static >= 2:
                    dve.wait_ge(rows_done, n - 1)
                dve.tensor_scalar(nm[:, p, 0, :], mx[:, p, :], -1.0, None, ALU.mult).then_inc(nm_hi, 1)
                dve.wait_ge(nm_hi, n + 1)
                dve.scalar_tensor_tensor(nm[:, p, 1, :], mx[:, p, :], -1.0, nm[:, p, 0, :], ALU.mult, ALU.subtract).then_inc(nm_ready, 1)

            for n in range(2):
                maxima(n, n, n)

            def step(n, u, known):
                if known is None or known < NG - 2:
                    maxima(n + 2, u % 2, None if known is None else known + 2)

            program(dve, step)

        @block.gpsimd
        def _(pool):
            for p in range(2):
                pool.memset(v_ones[p][:, :, :], 0.0)
                if not causal:
                    pool.memset(v_only[p][:, :, :], 0.0)
            if not causal:
                pool.memset(ones_only[:, :], 0.0)
            pool.memset(mrow[0][:, :], 0.0).then_inc(pool_ready, 1)
            pool.wait_ge(pool_ready, 1)
            if not causal:
                pool.memset(ones_only[:, HD:2 * HD], 1.0)
            pool.memset(v_ones[0][:, :, HD:2 * HD], 1.0)
            pool.memset(v_ones[1][:, :, HD:2 * HD], 1.0).then_inc(pool_ready, 1)

            def stage_v(n, p):
                src = g["v_all"][:, :, :, :].rearrange("p h (b t) e -> p (h b) t e", b=B)[:, n, :, :]
                ins = pool.tensor_copy(v_ones[p][:, :, 0:HD], src)
                if not causal:
                    ins = pool.tensor_copy(v_only[p][:, :, 0:HD], src)
                ins.then_inc(v_staged, 1)

            pool.wait_ge(pool_ready, 2)
            stage_v(0, 0)

            def step(n, u, known):
                p = u % 2
                for kb in range(TPB):
                    a, z = near(kb)
                    wait_alone(pool, exp_done, n * UNITS + first_unit[kb + 1], passed)
                    if causal:
                        pool.tensor_tensor(probs[p][:, kb, a:z], probs[p][:, kb, a:z], ebias_of(n, u, z - a), ALU.mult).then_inc(near_done, 1)
                    else:
                        if kb == 0 and (known is None or known >= 2):
                            pool.wait_ge(pv_done, n - 1)
                        pool.tensor_tensor(masked[p][:, kb, 0:z - a], probs[p][:, kb, a:z], g["tri"][:, 0:z - a], ALU.mult).then_inc(near_done, 1)
                    if kb == LAG and (known is None or known < NG - 1):
                        if known != 0:
                            pool.wait_ge(pv_done, n)
                        stage_v(n + 1, 1 - p)

            def ebias_of(n, u, w):
                return g["ebias"][:, n // B if isinstance(n, int) else (n - u) // B, 0:w]

            program(pool, step)

        @block.scalar
        def _(act):
            def take_rows(n, u, static):
                p = u % 2
                act.wait_ge(rows_done, n + 1)
                if static is None or static >= 2:
                    m2 = (u + 2) % B
                    act.wait_ge(r_loaded[m2], (n - 2 - m2 + B) * (16 // B))
                act.activation(mrow[p][:, :], psR[0:2 * TPB, 0:P], ACT.Copy).then_inc(rows_taken, 1)

            act.wait_ge(pool_ready, 1)
            take_rows(0, 0, 0)

            def take_o(n, p, static):
                act.wait_ge(pv_done, n + 1)
                if static is None or static >= 2:
                    act.wait_ge(o_stored[p], (n - p) * 8)
                act.activation(oT[p][:, :], psO[:, 0:2 * P], ACT.Copy).then_inc(o_taken, 1)

            def step(n, u, known):
                p = u % 2
                for kb in range(TPB):
                    for i, h in enumerate(halves[kb]):
                        a, z = columns(kb, h)
                        unit = first_unit[kb] + i
                        act.wait_ge(scores_done, n * UNITS + unit + 1)
                        if kb == 0 and i == 0 and (known is None or known >= 2):
                            act.wait_ge(pv_done, n - 1)
                        act.activation(probs[p][:, kb, a:z], psS[unit % 2][:, a - h * CH:z - h * CH], ACT.Exp,
                                       scale=1.0 if causal else HEAD_SCALE).then_inc(exp_done, 1)
                    if kb == 1 and (known is None or known < NG - 1):
                        take_rows(n + 1, (u + 1) % B, None if known is None else known + 1)
                    if kb == 2 and known != 0:
                        take_o(n - 1, 1 - p, None if known is None else known - 1)

            program(act, step)
            take_o(NG - 1, 1, NG - 1)

        @block.tensor
        def _(pe):
            def max_scores(n, u, qb, static):
                if static is None or static > 0 or qb >= 2:
                    pe.wait_ge(max_taken, n * TPB + qb - 1)
                if qb == 0:
                    pe.wait_ge(s_loaded[u], (n - u + B) * (32 // B))
                w = (qb + 1) * P if causal else T
                for h in range(-(-w // CH)):
                    a, z = h * CH, min((h + 1) * CH, w)
                    holds_diagonal = causal and z == w
                    last = pe.matmul(psM[qb % 2][:, a:z], qS[u][0:MROW, qb * P:(qb + 1) * P], kS[u][0:MROW, a:z], start=True, stop=not holds_diagonal)
                if causal:
                    last = pe.matmul(psM[qb % 2][:, w - P:w], g["identb"][:, :], g["maskneg"][:, :], start=False, stop=True)
                last.then_inc(maxima_done, 1)

            def max_rows(n, p, static):
                pe.wait_ge(nm_ready, n + 1)
                if static is None or static > 0:
                    pe.wait_ge(rows_taken, n)
                pe.matmul(psR[0:2 * TPB, 0:P], nm[:, p, :, :].rearrange("p s q -> p (s q)"), g["identb"][:, :], start=True, stop=True).then_inc(rows_done, 1)

            def scores(n, u, kb, static):
                if kb == 0:
                    pe.wait_ge(r_loaded[u], (n - u + B) * (16 // B))
                for i, h in enumerate(halves[kb]):
                    a, z = columns(kb, h)
                    unit = first_unit[kb] + i
                    if static is None or static > 0 or unit >= 2:
                        pe.wait_ge(exp_done, n * UNITS + unit - 1)
                    masks = causal and i == 0
                    last = pe.matmul(psS[unit % 2][:, a - h * CH:z - h * CH], kS[u][:, kb * P:(kb + 1) * P], qS[u][:, a:z], start=True, stop=not masks)
                    if masks:
                        last = pe.matmul(psS[unit % 2][:, a - h * CH:a - h * CH + P], g["identb"][:, :], g["masknegT"][:, :], start=False, stop=True)
                    last.then_inc(scores_done, 1)

            def values(n, p, kb, static):
                if kb == 0:
                    pe.wait_ge(v_staged, n + 1)
                    if static is None or static > 0:
                        pe.wait_ge(o_taken, n)
                if causal:
                    pe.wait_ge(near_done, n * TPB + kb + 1)
                    for c in range(4):
                        out = psO[c * VW:(c + 1) * VW, 0:2 * P]
                        pr = probs[p][:, kb, :].rearrange("p (q w) -> p q w", w=P)
                        if kb <= c:
                            last = pe.matmul(out.rearrange("p (q w) -> p q w", w=P), v_ones[p][:, kb, :], pr[:, c:TPB - c:TPB - 1 - 2 * c, :],
                                             start=kb == 0, stop=False, tile_position=(0, c * VW))
                        elif kb <= TPB - 1 - c:
                            b = TPB - 1 - c
                            last = pe.matmul(out[:, P:2 * P], v_ones[p][:, kb, :], pr[:, b, :],
                                             start=False, stop=kb == TPB - 1 - c, tile_position=(0, c * VW))
                    if kb == TPB - 1:
                        last.then_inc(pv_done, 1)
                    return
                pe.wait_ge(exp_done, n * UNITS + first_unit[kb + 1])
                for c in range(4):
                    pe.matmul(psO[c * VW:(c + 1) * VW, 0:2 * P], v_ones[p][:, kb, :] if kb < 2 * c else ones_only[:, :],
                              probs[p][:, kb, 2 * c * P:(2 * c + 2) * P], start=kb == 0, stop=False, tile_position=(0, c * VW))
                if kb == TPB - 1:
                    pe.wait_ge(near_done, (n + 1) * TPB)
                    for odd in range(2):
                        for c in range(4):
                            last = pe.matmul(psO[c * VW:(c + 1) * VW, odd * P:2 * P], v_only[p][:, 2 * c + odd, :],
                                             masked[p][:, 2 * c + odd, 0:(2 - odd) * P], start=False, stop=odd == 1, tile_position=(0, c * VW))
                    last.then_inc(pv_done, 1)

            pe.wait_ge(cleared, 1)
            for n in range(2):
                for qb in range(TPB):
                    max_scores(n, n, qb, n)
                if n == 0:
                    max_rows(0, 0, 0)

            def step(n, u, known):
                p = u % 2
                for kb in range(TPB):
                    scores(n, u, kb, known)
                    if known is None or known < NG - 2:
                        max_scores(n + 2, (u + 2) % B, kb, None)
                    if kb == 1 and (known is None or known < NG - 1):
                        max_rows(n + 1, 1 - p, None)
                    if kb >= LAG:
                        values(n, p, kb - LAG, known)
                    elif known != 0:
                        values(n - 1, 1 - p, kb - LAG + TPB, None if known is None else known - 1)

            program(pe, step)
            for kb in range(TPB - LAG, TPB):
                values(NG - 1, 1, kb, NG - 1)


class Gather:

    def __init__(self, nc, m, g):
        self.g = g
        self.den = m.sb("den", [P, B * T * HEADS // P])
        self.rden = m.sb("rden", [P, B * T * HEADS // P])
        self.num = [m.sb(f"num{i}", [P, T]) for i in range(2)]
        self.inv = [m.sb(f"inv{i}", [P, T]) for i in range(2)]
        self.den_loaded, self.rden_ready, self.rden_stored = m.sem("den_loaded"), m.sem("rden_ready"), m.sem("rden_stored")
        self.loaded = [m.sem(f"heads_loaded{i}") for i in range(B)]
        self.att_ready = m.sem("att_ready")

    def reciprocals(self, dve):
        dve.wait_ge(self.den_loaded, 16)
        dve.reciprocal(self.rden[:, :], self.den[:, :]).then_inc(self.rden_ready, 1)

    def load(self, sp):
        g, o, r = self.g, self.g["o_dram"].tensor, self.g["r_dram"].tensor
        half = T // 2
        sp.dma_start(self.den[:, :], bass.AP(o, HD * T, [[VW * T, HEADS * B], [half, 2], [1, half]])).then_inc(self.den_loaded, 16)
        for b in range(2):
            self.load_num(sp, b)
        sp.wait_ge(self.rden_ready, 1)
        sp.dma_start(bass.AP(r, 0, [[half, P], [1, half]]), self.rden[:, :]).then_inc(self.rden_stored, 16)
        sp.wait_ge(self.rden_stored, 16)
        for b in range(B):
            if b >= 2:
                sp.wait_ge(self.att_ready, (b - 1) * CPB)
                self.load_num(sp, b)
            sp.dma_start(self.inv[b % 2][:, :], bass.AP(r, b * T, [[B * T, HEADS], [0, HD], [1, T]])).then_inc(self.loaded[b], 16)

    def load_num(self, sp, b):
        o = self.g["o_dram"].tensor
        sp.dma_start(self.num[b % 2][:, :], bass.AP(o, b * (VW * T), [[B * VW * T, HEADS], [T, HD], [1, T]])).then_inc(self.loaded[b], 16)


def add_projected(nc, m, g):
    norm, gather = Norm(m, g["x"]), Gather(nc, m, g)
    att = m.sb("att", [P, 2, TPC, P])
    xnT_now = m.sb("xnT_now", [P, 2, CH])
    NN = FF * NODES
    score = m.sb("score", [P, TPC, NN])
    bits = m.sb("bits", [P, TPC, NN])
    nbits = m.sb("nbits", [P, TPC, NN])
    way = [m.sb(f"way{i}", [P, TPC, FF, 2 ** (i + 1)]) for i in range(DEPTH - 1)]
    sel = m.sb("sel", [P, 2, TPC, P])
    psY = [m.ps(f"psY{u}", [P, TPC, D]) for u in range(2)]
    psT = [m.ps(f"psT{u}", [P, CH]) for u in range(2)]
    psN = [m.ps(f"psN{u}", [P, TPC, NN]) for u in range(2)]
    psL = m.ps("psL", [P, CH])
    projected, added, bias_added = m.sem("projected"), m.sem("added"), m.sem("bias_added")
    transposed, xnT_ready = m.sem("transposed"), m.sem("xnT_ready")
    noded, sel_ready, sel_turned, sel_taken = m.sem("noded"), m.sem("sel_ready"), m.sem("sel_turned"), m.sem("sel_taken")
    route_steps, cleared = m.sem("route_steps"), m.sem("cleared")
    ROUTE = 3 + DEPTH

    with nc.Block() as block:

        @block.sync
        def _(sp):
            gather.load(sp)

        @block.gpsimd
        def _(pool):
            def bias(c):
                xs = g["x"][:, c * TPC:(c + 1) * TPC, :]
                pool.tensor_tensor(xs, xs, g["bo"][:, :].unsqueeze(1).to_broadcast([P, TPC, D]), ALU.add).then_inc(bias_added, 1)

            def divide(c):
                b, u = c // CPB, c % CPB
                num, inv = (t[b % 2][:, :].rearrange("p (c q w) -> p c q w", q=2, w=P) for t in (gather.num, gather.inv))
                if u == 0:
                    pool.wait_ge(gather.loaded[b], 32)
                if c >= 2:
                    pool.wait_ge(projected, c - 1)
                for k in range(TPC):
                    at = k if u == 0 else TPC - 1 - k
                    last = pool.tensor_tensor(att[:, u, k, :], num[:, at, u, :], inv[:, at, u, :], ALU.mult)
                last.then_inc(gather.att_ready, 1)

            AHEAD = 4
            for c in range(AHEAD):
                bias(c)
            for c in range(NCH):
                divide(c)
                if c + AHEAD < NCH:
                    bias(c + AHEAD)

        @block.vector
        def _(dve):
            dve.memset(sel[:, :, :, :], 0.0).then_inc(cleared, 1)
            gather.reciprocals(dve)

            def add(c, u, early):
                xs = g["x"][:, bass.ds(c * TPC, TPC), :]
                dve.wait_ge(bias_added, c + 1)
                dve.wait_ge(projected, c + 1)
                dve.tensor_tensor(xs, psY[u][:, :, :], xs, ALU.add).then_inc(added, 1)
                wait_alone(dve, added, c + 1, norm.passed)
                norm.statistics(dve, c, u)

            def scale(c, u, early):
                norm.scale(dve, c, u, transposed, early)

            def route(c, u, early):
                st = Steps(dve, route_steps, c * ROUTE)
                dve.wait_ge(noded, c + 1)
                st.did(dve.tensor_tensor(score[:, :, :], psN[u][:, :, :], g["node_b"][:, :].unsqueeze(1).to_broadcast([P, TPC, NN]), ALU.add))
                st.settle()
                st.did(dve.tensor_scalar(nbits[:, :, :], score[:, :, :], 0.0, None, ALU.is_lt))
                st.did(dve.tensor_scalar(bits[:, :, :], score[:, :, :], 0.0, None, ALU.is_ge))
                st.settle()
                if not early:
                    dve.wait_ge(sel_turned, c - 1)
                for d in range(DEPTH):
                    lo, w = 2 ** d - 1, 2 ** d
                    for tree in range(FF):
                        if d < DEPTH - 1:
                            out = way[d][:, :, tree, :].rearrange("p t (n s) -> p t n s", s=2)
                        else:
                            a = SELROW + tree * LEAVES
                            out = sel[:, u, :, a:a + LEAVES].rearrange("p t (n s) -> p t n s", s=2)
                        for side, taken in enumerate((nbits, bits)):
                            node = taken[:, :, tree * NODES + lo:tree * NODES + lo + w]
                            if d == 0:
                                last = dve.tensor_copy(out[:, :, :, side], node)
                            else:
                                last = dve.tensor_tensor(out[:, :, :, side], way[d - 1][:, :, tree, :], node, ALU.mult)
                    st.did(last)
                    st.settle()
                assert st.n == ROUTE
                dve.tensor_scalar(sel[:, u, :, 0:FF * LEAVES], sel[:, u, :, SELROW:SELROW + FF * LEAVES], -1.0, None, ALU.add).then_inc(sel_ready, 1)

            pipeline(dve, [(scale, 2), (add, 1), (route, 3)])

        @block.scalar
        def _(act):
            def root(c, u, early):
                norm.take_root(act, c, u)

            def turned(c, u, early):
                act.wait_ge(transposed, c + 1)
                if not early:
                    act.wait_ge(noded, c - 1)
                act.activation(xnT_now[:, u, :], psT[u][:, :], ACT.Copy).then_inc(xnT_ready, 1)
                act.activation(g["xnT_all"][:, bass.ds(c * CH, CH)], psT[u][:, :], ACT.Copy).then_inc(xnT_ready, 1)

            def selected(c, u, early):
                act.wait_ge(sel_turned, c + 1)
                act.activation(g["selT"][:, bass.ds(c * CH, CH)], psL[:, :], ACT.Copy).then_inc(sel_taken, 1)

            pipeline(act, [(turned, 2), (root, 1), (selected, 4)])

        @block.tensor
        def _(pe):
            def project(c, u, early):
                pe.wait_ge(gather.att_ready, c + 1)
                if not early:
                    pe.wait_ge(added, c - 1)
                for t in range(TPC):
                    last = pe.matmul(psY[u][:, t, :], att[:, u, t, :], g["w_a"][:, 3, :], start=True, stop=True)
                last.then_inc(projected, 1)

            def turn(c, u, early):
                pe.wait_ge(norm.xn_ready, c + 1)
                if not early:
                    pe.wait_ge(xnT_ready, 2 * (c - 1))
                for t in range(TPC):
                    last = pe.transpose(psT[u][:, t * P:(t + 1) * P], norm.xn[:, u, t, :], g["identf"][:, :])
                last.then_inc(transposed, 1)

            def nodes(c, u, early):
                pe.wait_ge(xnT_ready, 2 * c + 1)
                if not early:
                    pe.wait_ge(route_steps, (c - 2) * ROUTE + 1)
                for t in range(TPC):
                    last = pe.matmul(psN[u][:, t, :], xnT_now[:, u, t * P:(t + 1) * P], g["node_wT"][:, :], start=True, stop=True)
                last.then_inc(noded, 1)

            def select(c, u, early):
                pe.wait_ge(sel_ready, c + 1)
                if not (early and isinstance(c, int) and c == 0):
                    pe.wait_ge(sel_taken, c)
                for t in range(TPC):
                    last = pe.transpose(psL[:, t * P:(t + 1) * P], sel[:, u, t, :], g["identf"][:, :])
                last.then_inc(sel_turned, 1)

            pipeline(pe, [(project, 0), (turn, 2), (select, 4), (nodes, 2)])


def trees(nc, m, g):
    NH = 4
    hid = [m.sb(f"hid{i}", [P, CH]) for i in range(NH)]
    vT = m.sb("vT", [P, CH])
    psH = [m.ps(f"psH{i}", [P, CH]) for i in range(2)]
    psO = [m.ps(f"psO{i}", [P, CH]) for i in range(2)]
    psV = m.ps("psV", [P, CH])
    hidden_done, hid_ready, out_done, out_taken = m.sem("hidden_done"), m.sem("hid_ready"), m.sem("out_done"), m.sem("out_taken")
    v_turned, v_taken = m.sem("v_turned"), m.sem("v_taken")
    used = m.sem("used")
    LAG = 2

    with nc.Block() as block:

        def rounds(eng, body):
            for f in range(FF):
                if f == 0:
                    for u in range(CPB):
                        body(f, 0, u, u == 0)
                with eng.Fori(1 if f == 0 else 0, B) as b:
                    for u in range(CPB):
                        body(f, b, u, False)

        @block.tensor
        def _(pe):
            def body(f, b, u, first):
                c = b * CPB + u + f * NCH
                toks = bass.ds(b * T + u * CH, CH)
                for i in range(HID + LAG):
                    if i < HID:
                        n = c * HID + i
                        if not first or i >= 2:
                            pe.wait_ge(hid_ready, n - 1)
                        pe.matmul(psH[i % 2][:, :], g["w1"][:, f, i * P:(i + 1) * P], g["xnT_all"][:, toks], start=True, stop=False)
                        a = (f * LEAVES + 2 * i) * LW
                        pe.matmul(psH[i % 2][:, :], g["leafx"][:, a:a + P], g["selT"][:, toks], start=False, stop=True).then_inc(hidden_done, 1)
                    if i >= LAG:
                        j = i - LAG
                        pe.wait_ge(hid_ready, c * HID + j + 1)
                        if j == 0 and not (first or (isinstance(b, int) and b == 0 and f == 0)):
                            pe.wait_ge(out_taken, c - 1)
                        pe.matmul(psO[u][:, :], g["w2"][:, f, j, :], hid[j % NH][:, :], start=j == 0, stop=False).then_inc(used, 1)
                for part in range(PARTS):
                    last = pe.matmul(psO[u][:, :], g["b2p"][:, part, f, :], g["selT"][:, toks], start=False, stop=part == PARTS - 1)
                last.then_inc(out_done, 1)
                if f == FF - 1:
                    pe.wait_ge(out_taken, c + 1)
                    pe.wait_ge(v_taken, b * CPB + u + 1)
                    for t in range(TPC):
                        last = pe.transpose(psV[:, t * P:(t + 1) * P], vT[:, t * P:(t + 1) * P], g["identf"][:, :])
                    last.then_inc(v_turned, 1)

            rounds(pe, body)

        @block.scalar
        def _(act):
            def body(f, b, u, first):
                c = b * CPB + u + f * NCH
                for i in range(HID):
                    n = c * HID + i
                    act.wait_ge(hidden_done, n + 1)
                    if not first or i >= NH:
                        act.wait_ge(used, n - NH + 1)
                    act.activation(hid[i % NH][:, :], psH[i % 2][:, :], ACT.Relu, bias=g["b1"][:, f, i:i + 1]).then_inc(hid_ready, 1)

            rounds(act, body)

        @block.vector
        def _(dve):
            dve.sem_inc(v_taken, 1)

            def body(f, b, u, first):
                c = b * CPB + u + f * NCH
                dve.wait_ge(out_done, c + 1)
                if f < FF - 1:
                    dve.tensor_copy(g["qkT"][:, f, bass.ds(b * T + u * CH, CH)], psO[u][:, :]).then_inc(out_taken, 1)
                else:
                    dve.tensor_copy(vT[:, :], psO[u][:, :]).then_inc(out_taken, 1)
                    dve.wait_ge(v_turned, b * CPB + u + 1)
                    dve.tensor_copy(g["v_tok"][:, bass.ds(b * TPB + u * TPC, TPC), :], psV[:, :].rearrange("p (t d) -> p t d", t=TPC)).then_inc(v_taken, 1)

            rounds(dve, body)


def attend_wide(nc, m, g):
    SC = float(D) ** -0.5
    qs = m.sb("qs", [P, T])
    probs = [m.sb(f"probs{i}", [P, T]) for i in range(2)]
    turned = [m.sb(f"turned{i}", [P, T]) for i in range(2)]
    mx, nmx, den, rden = m.sb("mx", [P, 2]), m.sb("nmx", [P, 2]), m.sb("den", [P, 2]), m.sb("rden", [P, 2])
    psS = [m.ps(f"psS{i}", [P, T]) for i in range(2)]
    psT = m.ps("psT", [P, 2, CH])
    psY = m.ps("psY", [P, CH])
    q_staged, scored, max_taken, shift_ready = m.sem("q_staged"), m.sem("scored"), m.sem("max_taken"), m.sem("shift_ready")
    exp_done, flipped, valued, added, rden_ready = (m.sem(n) for n in ("exp_done", "flipped", "valued", "added", "rden_ready"))
    flip_taken = [m.sem(f"flip_taken{h}") for h in range(2)]

    def batches(eng, body):
        body(0, True)
        with eng.Fori(1, B) as b:
            body(b, False)

    with nc.Block() as block:

        @block.tensor
        def _(pe):
            def score(b, qb, first):
                n = b * TPB + qb
                if qb == 0:
                    pe.wait_ge(q_staged, b + 1)
                if not first or qb >= 2:
                    pe.wait_ge(exp_done, n - 1)
                for h in range(2):
                    last = pe.matmul(psS[qb % 2][:, h * CH:(h + 1) * CH], qs[:, qb * P:(qb + 1) * P],
                                     g["qkT"][:, 1, bass.ds(b * T + h * CH, CH)], start=True, stop=True)
                last.then_inc(scored, 1)

            def turn(b, qb, first):
                n = b * TPB + qb
                pe.wait_ge(exp_done, n + 1)
                for h in range(2):
                    if not first or qb:
                        pe.wait_ge(flip_taken[h], n)
                    for k in range(4):
                        kb = 4 * h + k
                        last = pe.transpose(psT[:, h, k * P:(k + 1) * P], probs[qb % 2][:, kb * P:(kb + 1) * P], g["identf"][:, :])
                    last.then_inc(flipped, 1)

            def value(b, qb, first):
                n = b * TPB + qb
                if not first or qb:
                    pe.wait_ge(added, n)
                for h in range(2):
                    pe.wait_ge(flip_taken[h], n + 1)
                    for k in range(4):
                        kb = 4 * h + k
                        last = pe.matmul(psY[:, 0:D], turned[qb % 2][:, kb * P:(kb + 1) * P], g["v_tok"][:, b * TPB + kb, :],
                                         start=kb == 0, stop=kb == TPB - 1)
                last.then_inc(valued, 1)

            def body(b, first):
                score(b, 0, first)
                score(b, 1, first)
                for qb in range(TPB):
                    turn(b, qb, first)
                    if qb + 2 < TPB:
                        score(b, qb + 2, first)
                    value(b, qb, first)

            batches(pe, body)

        @block.gpsimd
        def _(pool):
            def body(b, first):
                if not first:
                    pool.wait_ge(scored, b * TPB)
                pool.tensor_copy(qs[:, :], g["qkT"][:, 0, bass.ds(b * T, T)]).then_inc(q_staged, 1)

            batches(pool, body)

        @block.vector
        def _(dve):
            def body(b, first):
                def shift(qb):
                    n = b * TPB + qb
                    p = qb % 2
                    dve.wait_ge(scored, n + 1)
                    dve.tensor_reduce(mx[:, p:p + 1], psS[p][:, :], AXX, ALU.max).then_inc(max_taken, 1)
                    dve.wait_ge(max_taken, n + 1)
                    if not first or qb >= 2:
                        dve.wait_ge(exp_done, n - 1)
                    dve.tensor_scalar(nmx[:, p:p + 1], mx[:, p:p + 1], -SC, None, ALU.mult).then_inc(shift_ready, 1)

                def flip(qb):
                    n = b * TPB + qb
                    dve.wait_ge(flipped, 2 * n + 2)
                    dve.tensor_copy(turned[qb % 2][:, CH:T], psT[:, 1, :]).then_inc(flip_taken[1], 1)

                def finish(qb):
                    n = b * TPB + qb
                    p = qb % 2
                    if not first or qb >= 1:
                        dve.wait_ge(added, n)
                    dve.reciprocal(rden[:, p:p + 1], den[:, p:p + 1]).then_inc(rden_ready, 1)
                    dve.wait_ge(rden_ready, n + 1)
                    dve.wait_ge(valued, n + 1)
                    dve.scalar_tensor_tensor(g["x"][:, b * TPB + qb, :], psY[:, 0:D], rden[:, p:p + 1], g["x"][:, b * TPB + qb, :],
                                             ALU.mult, ALU.add).then_inc(added, 1)

                shift(0)
                shift(1)
                for qb in range(TPB):
                    flip(qb)
                    if qb + 2 < TPB:
                        shift(qb + 2)
                    finish(qb)

            batches(dve, body)

        @block.scalar
        def _(act):
            def body(b, first):
                def exponentials(qb):
                    n = b * TPB + qb
                    p = qb % 2
                    act.wait_ge(shift_ready, n + 1)
                    if not first or qb >= 2:
                        act.wait_ge(flipped, 2 * n - 2)
                        act.wait_ge(rden_ready, n - 1)
                    act.activation(probs[p][:, :], psS[p][:, :], ACT.Exp, bias=nmx[:, p:p + 1], scale=SC,
                                   accum_out=den[:, p:p + 1]).then_inc(exp_done, 1)

                exponentials(0)
                for qb in range(TPB):
                    n = b * TPB + qb
                    act.wait_ge(flipped, 2 * n + 1)
                    if not first or qb >= 2:
                        act.wait_ge(valued, n - 1)
                    act.activation(turned[qb % 2][:, 0:CH], psT[:, 0, :], ACT.Copy).then_inc(flip_taken[0], 1)
                    if qb + 1 < TPB:
                        exponentials(qb + 1)

            batches(act, body)


def finish_layers(nc, m, g, out):
    norm, gather = Norm(m, g["x"]), Gather(nc, m, g)
    att = m.sb("att", [P, 2, CH])
    xT = [m.sb(f"xT{u}", [P, 1 + CH]) for u in range(2)]
    omm = m.sb("omm", [P, 2])
    prev = m.sb("prev", [P, 2, 2, CH])
    mix = m.sb("mix", [P, 2, 2, CH])
    krelu = m.sb("krelu", [P, 2, CH])
    kact = m.sb("kact", [P, 2, CH])
    gate = m.sb("gate", [P, 2, CH])
    gated = m.sb("gated", [P, 2, CH])
    res = m.sb("res", [P, 2, TPC, D])
    psA = m.ps("psA", [P, TPC, D])
    psT = [m.ps(f"psT{u}", [P, CH]) for u in range(2)]
    psK = m.ps("psK", [P, CH])
    psR = [m.ps(f"psR{u}", [P, CH]) for u in range(2)]
    psV = [m.ps(f"psV{u}", [P, CH]) for u in range(2)]
    names = ["att_turned", "added", "transposed", "xT_ready", "edge_ready", "mu_ready", "prev_ready", "mix_ready", "keys_done",
             "relu_done", "kact_ready", "gates_done", "gate_ready", "wide_done", "gated_ready", "out_ready"]
    (att_turned, added, transposed, xT_ready, edge_ready, mu_ready, prev_ready, mix_ready, keys_done,
     relu_done, kact_ready, gates_done, gate_ready, wide_done, gated_ready, out_ready) = (m.sem(n) for n in names)
    out_stored = [m.sem(f"out_stored{u}") for u in range(2)]

    with nc.Block() as block:

        @block.sync
        def _(sp):
            gather.load(sp)
            for c in range(NCH):
                sp.wait_ge(out_ready, c + 1)
                dst = bass.AP(out.tensor, c * (CH * D), [[D, P], [P * D, TPC], [1, D]])
                sp.dma_start(dst, res[:, c % 2, :, :]).then_inc(out_stored[c % 2], 16)
            for u in range(2):
                sp.wait_ge(out_stored[u], 16 * NCH // 2)

        @block.gpsimd
        def _(pool):
            def divide(c, u):
                if u == 0:
                    pool.wait_ge(gather.loaded[c // CPB], 32)
                if c >= 2:
                    pool.wait_ge(att_turned, c - 1)
                b = c // CPB
                pool.tensor_tensor(att[:, u, :], gather.num[b % 2][:, u * CH:(u + 1) * CH], gather.inv[b % 2][:, u * CH:(u + 1) * CH],
                                   ALU.mult).then_inc(gather.att_ready, 1)

            def squares(c, u):
                pool.wait_ge(relu_done, c + 1)
                if c >= 2:
                    pool.wait_ge(wide_done, c - 1)
                pool.tensor_tensor(kact[:, u, :], krelu[:, u, :], krelu[:, u, :], ALU.mult).then_inc(kact_ready, 1)

            def result(c, u):
                pool.wait_ge(gated_ready, c + 1)
                if c >= 2:
                    pool.wait_ge(out_stored[u], (c // 2) * 16)
                pool.tensor_tensor(res[:, u, :, :], gated[:, u, :].rearrange("p (t d) -> p t d", d=D), g["x"][:, c * TPC:(c + 1) * TPC, :],
                                   ALU.add).then_inc(out_ready, 1)

            for n in range(NCH + 5):
                if n < NCH:
                    divide(n, n % 2)
                if 0 <= n - 4 < NCH:
                    squares(n - 4, n % 2)
                if 0 <= n - 5 < NCH:
                    result(n - 5, (n - 5) % 2)

        @block.vector
        def _(dve):
            dve.tensor_scalar(omm[:, :], g["mu"][:, :], -1.0, 1.0, ALU.mult, ALU.add).then_inc(mu_ready, 1)
            gather.reciprocals(dve)
            dve.wait_ge(mu_ready, 1)

            def add(c, u):
                xs = g["x"][:, c * TPC:(c + 1) * TPC, :]
                dve.wait_ge(att_turned, c + 1)
                dve.tensor_tensor(xs, psA[:, :, :], xs, ALU.add).then_inc(added, 1)
                dve.wait_ge(added, c + 1)
                norm.statistics(dve, c, u)

            def edge(c, u):
                dve.wait_ge(xT_ready, c + 1)
                if u == 0:
                    if c >= 2:
                        dve.wait_ge(mix_ready, c - 1)
                    dve.memset(xT[0][:, 0:1], 0.0).then_inc(edge_ready, 1)
                else:
                    dve.tensor_copy(xT[1][:, 0:1], xT[0][:, CH:CH + 1]).then_inc(edge_ready, 1)

            def mixes(c, u):
                dve.wait_ge(prev_ready, c + 1)
                if c >= 2:
                    dve.wait_ge(gates_done, c - 1)
                for i in range(2):
                    last = dve.scalar_tensor_tensor(mix[:, u, i, :], xT[u][:, 1:CH + 1], g["mu"][:, i:i + 1], prev[:, u, i, :], ALU.mult, ALU.add)
                last.then_inc(mix_ready, 1)

            def gated_values(c, u):
                dve.wait_ge(gate_ready, c + 1)
                dve.wait_ge(wide_done, c + 1)
                if c >= 2:
                    dve.wait_ge(out_ready, c - 1)
                dve.tensor_tensor(gated[:, u, :], psV[u][:, :], gate[:, u, :], ALU.mult).then_inc(gated_ready, 1)

            for n in range(NCH + 5):
                if 0 <= n - 4 < NCH:
                    mixes(n - 4, n % 2)
                if 0 <= n - 3 < NCH:
                    edge(n - 3, (n - 3) % 2)
                if 0 <= n - 5 < NCH:
                    gated_values(n - 5, (n - 5) % 2)
                if 0 <= n - 2 < NCH:
                    norm.scale(dve, n - 2, n % 2, transposed, n - 2 < 2)
                if 0 <= n - 1 < NCH:
                    add(n - 1, (n - 1) % 2)

        @block.scalar
        def _(act):
            def root(c, u, early):
                norm.take_root(act, c, u)

            def turned(c, u, early):
                act.wait_ge(transposed, c + 1)
                if not early:
                    act.wait_ge(mix_ready, c - 1)
                    act.wait_ge(edge_ready, c)
                act.activation(xT[u][:, 1:1 + CH], psT[u][:, :], ACT.Copy).then_inc(xT_ready, 1)

            def earlier(c, u, early):
                act.wait_ge(edge_ready, c + 1)
                if not early:
                    act.wait_ge(mix_ready, c - 1)
                for i in range(2):
                    last = act.activation(prev[:, u, i, :], xT[u][:, 0:CH], ACT.Copy, scale=omm[:, i:i + 1])
                last.then_inc(prev_ready, 1)

            def gates(c, u, early):
                act.wait_ge(keys_done, c + 1)
                if not early:
                    act.wait_ge(kact_ready, c - 1)
                act.activation(krelu[:, u, :], psK[:, :], ACT.Relu).then_inc(relu_done, 1)
                act.wait_ge(gates_done, c + 1)
                if not early:
                    act.wait_ge(gated_ready, c - 1)
                act.activation(gate[:, u, :], psR[u][:, :], ACT.Sigmoid).then_inc(gate_ready, 1)

            pipeline(act, [(earlier, 3), (gates, 4), (turned, 2), (root, 1)])

        @block.tensor
        def _(pe):
            def untransposed(c, u, early):
                pe.wait_ge(gather.att_ready, c + 1)
                if not (isinstance(c, int) and c == 0):
                    pe.wait_ge(added, c)
                for t in range(TPC):
                    last = pe.transpose(psA[:, t, :], att[:, u, t * P:(t + 1) * P], g["identf"][:, :])
                last.then_inc(att_turned, 1)

            def turn(c, u, early):
                pe.wait_ge(norm.xn_ready, c + 1)
                if not early:
                    pe.wait_ge(xT_ready, c - 1)
                for t in range(TPC):
                    last = pe.transpose(psT[u][:, t * P:(t + 1) * P], norm.xn[:, u, t, :], g["identf"][:, :])
                last.then_inc(transposed, 1)

            def keys(c, u, early):
                pe.wait_ge(mix_ready, c + 1)
                if not (isinstance(c, int) and c == 0):
                    pe.wait_ge(relu_done, c)
                pe.matmul(psK[:, :], g["w_d"][:, 1, :], mix[:, u, 1, :], start=True, stop=True).then_inc(keys_done, 1)
                if not early:
                    pe.wait_ge(gate_ready, c - 1)
                for t in range(TPC):
                    last = pe.matmul(psR[u][:, t * P:(t + 1) * P], mix[:, u, 0, t * P:(t + 1) * P], g["w_d"][:, 0, :], start=True, stop=True)
                last.then_inc(gates_done, 1)

            def wide(c, u, early):
                pe.wait_ge(kact_ready, c + 1)
                if not early:
                    pe.wait_ge(gated_ready, c - 1)
                for t in range(TPC):
                    last = pe.matmul(psV[u][:, t * P:(t + 1) * P], kact[:, u, t * P:(t + 1) * P], g["w_d"][:, 2, :], start=True, stop=True)
                last.then_inc(wide_done, 1)

            pipeline(pe, [(untransposed, 0), (keys, 4), (turn, 2), (wide, 4)])


def build(nc, ins, out, phases=99):
    ctx = ExitStack()
    with ctx:
        gm = Mem(nc, ctx, "g")
        g = {
            "x": gm.sb("x", [P, NT, D]),
            "identf": gm.sb("identf", [P, P]), "identb": gm.sb("identb", [P, P], BF16),
            "w_a": gm.sb("w_a", [P, 4, D]), "w_c": gm.sb("w_c", [P, 3, D]), "w_d": gm.sb("w_d", [P, 3, D]),
            "node_wT": gm.sb("node_wT", [P, FF * NODES]), "node_b": gm.sb("node_b", [P, FF * NODES]),
            "bias_qk": gm.sb("bias_qk", [P, 2]), "bv": gm.sb("bv", [P, D]), "bo": gm.sb("bo", [P, D]),
            "mu": gm.sb("mu", [P, 2]), "b1": gm.sb("b1", [P, FF, HID]),
            "tri": gm.sb("tri", [P, NEAR]), "maskneg": gm.sb("maskneg", [P, P], BF16),
            "masknegT": gm.sb("masknegT", [P, P], BF16),
            "q_dram": nc.dram_tensor("q_parts", [HEADS, B, PARTS, HD, T], BF16, kind="Internal").ap(),
            "k_dram": nc.dram_tensor("k_parts", [HEADS, B, HD, PARTS, T], BF16, kind="Internal").ap(),
            "o_dram": nc.dram_tensor("head_outputs", [HEADS, B, VW, T], F32, kind="Internal").ap(),
            "r_dram": nc.dram_tensor("reciprocals", [HEADS, B, T], F32, kind="Internal").ap(),
            "erow_dram": nc.dram_tensor("bias_rows", [HEADS, ERW], F32, kind="Internal").ap(),
        }

        def phase(tag, f, *args):
            with nc.cleanup_on_exit(), ExitStack() as own:
                f(nc, Mem(nc, own, tag), g, *args)

        g["w1"], g["w2"] = gm.sb("w1", [P, FF, LEAVES * LW]), gm.sb("w2", [P, FF, HID, D])
        g["b2p"] = gm.sb("b2p", [P, PARTS, FF, D], BF16)
        g["leafx"] = gm.sb("leafx", [P, FF * LEAVES * LW], BF16)
        g["selT"] = gm.sb("selT", [P, B * T], BF16)

        with ExitStack() as one:
            m1 = Mem(nc, one, "one")
            g["ebias"] = m1.sb("ebias", [P, HEADS, NEAR])
            g["v_all"] = m1.sb("v_all", [P, HEADS, B * TPB, HD])
            phase("setup", load_weights, ins)
            phase("proj1", project_heads, g["w_a"], True)
            phase("heads1", attend_heads, True)
        if phases < 3:
            return
        with ExitStack() as two:
            m2 = Mem(nc, two, "two")
            g["xnT_all"] = m2.sb("xnT_all", [P, B * T])
            g["qkT"], g["v_tok"] = m2.sb("qkT", [P, 2, B * T]), m2.sb("v_tok", [P, NT, D])
            phase("route", add_projected)
            phase("trees", trees)
            phase("wide", attend_wide)
        with ExitStack() as three:
            g["v_all"] = Mem(nc, three, "three").sb("v_all", [P, HEADS, B * TPB, HD])
            phase("proj3", project_heads, g["w_c"], False)
            phase("heads3", attend_heads, False)
        phase("finish", finish_layers, out)


def bucket_onehot():
    import numpy as np

    n = np.arange(P + NEAR) - (P - 1)
    near = np.maximum(n, 0)
    exact = BUCKETS // 2
    ratio = np.log(np.maximum(near, 1).astype(np.float32) / np.float32(exact)) / np.float32(np.log(MAX_DIST / exact))
    large = np.minimum(exact + (ratio * np.float32(BUCKETS - exact)).astype(np.int32), BUCKETS - 1)
    bucket = np.where(near < exact, near, large)
    table = (np.arange(BUCKETS)[:, None] == bucket[None, :]).astype(np.float32)
    table[BUCKETS - 1] -= 1.0
    return table


_INS = ['L0_attn_x', 'L0_attn_Wq', 'L0_attn_bq', 'L0_attn_Wk', 'L0_attn_bk', 'L0_attn_Wv', 'L0_attn_bv', 'L0_attn_Wo',
        'L0_attn_bo', 'L0_attn_rel_emb', 'L0_ffn_q_node_w', 'L0_ffn_q_node_b', 'L0_ffn_q_w1', 'L0_ffn_q_b1',
        'L0_ffn_q_w2', 'L0_ffn_q_b2', 'L0_ffn_k_node_w', 'L0_ffn_k_node_b', 'L0_ffn_k_w1', 'L0_ffn_k_b1',
        'L0_ffn_k_w2', 'L0_ffn_k_b2', 'L0_ffn_v_node_w', 'L0_ffn_v_node_b', 'L0_ffn_v_w1', 'L0_ffn_v_b1',
        'L0_ffn_v_w2', 'L0_ffn_v_b2', 'L1_attn_Wq', 'L1_attn_Wk', 'L1_attn_Wv', 'L1_ffn_W_r', 'L1_ffn_W_k',
        'L1_ffn_W_v', 'L1_ffn_mu_r', 'L1_ffn_mu_k']


def kernel(**inputs):
    import numpy as _np
    import concourse.bacc as _bacc
    from concourse import mybir as _mybir
    from concourse.bass_utils import run_bass_kernel_spmd as _run

    nc = _bacc.Bacc("TRN2", target_bir_lowering=False, num_devices=1)
    arrays, ins = {}, {}
    for name in [*_INS, "bucket_onehot"]:
        a = bucket_onehot() if name == "bucket_onehot" else _np.ascontiguousarray(inputs[name])
        arrays[f"in_{name}"] = a
        ins[name] = nc.dram_tensor(f"in_{name}", a.shape, _mybir.dt.from_np(a.dtype), kind="ExternalInput").ap()
    out = nc.dram_tensor("out_x", (B, T, D), F32, kind="ExternalOutput").ap()
    build(nc, ins, out)
    r = _run(nc, [arrays], core_ids=[0])
    return r.results[0]["out_x"]
```

```python
from contextlib import ExitStack

import concourse.bass as bass
from concourse import mybir

ALU = mybir.AluOpType
ACT = mybir.ActivationFunctionType
AXX = mybir.AxisListType.X
F32, F32R = mybir.dt.float32, mybir.dt.float32r
BF16 = mybir.dt.bfloat16

P = 128
B = 4
T = 1024
D = 128
HEADS = 16
HD = D // HEADS
NT = B * T // P
TPB = T // P
CH = 512
TPC = CH // P
CPB = T // CH
NCH = B * T // CH
EPS = 1e-5
PARTS = 3
SROWS = PARTS * PARTS * HD
MROW = 96
HSZ = PARTS * HD * T
BUCKETS = 32
MAX_DIST = 128
NEAR = 2 * P
ERW = 3 * P
NEG = -1.0e30
HEAD_SCALE = HD ** -0.5
LEAVES = 16
NODES = 15
DEPTH = 4
LW = 64
FF = 3
HID = LEAVES * LW // P
SELROW = 64
VW = 32


class Mem:

    def __init__(self, nc, ctx, tag):
        self.nc, self.ctx, self.tag = nc, ctx, tag

    def sb(self, name, shape, dt=F32):
        return self.ctx.enter_context(self.nc.sbuf_tensor(f"{self.tag}_{name}", shape, dt))

    def ps(self, name, shape, dt=F32):
        return self.ctx.enter_context(self.nc.psum_tensor(f"{self.tag}_{name}", shape, dt))

    def sem(self, name):
        return self.nc.alloc_semaphore(name=f"{self.tag}_{name}")


class Steps:

    def __init__(self, eng, sem, base=0):
        self.eng, self.sem, self.base, self.n = eng, sem, base, 0

    def did(self, ins):
        self.n += 1
        return ins.then_inc(self.sem, 1)

    def settle(self):
        self.eng.wait_ge(self.sem, self.base + self.n)

    def settle_alone(self, passed):
        wait_alone(self.eng, self.sem, self.base + self.n, passed)


def wait_alone(eng, sem, value, passed):
    eng.wait_ge(sem, value)
    eng.sem_inc(passed, 1)


def load_weights(nc, m, g, ins):
    wnat = m.sb("wnat", [P, 7, D])
    nodes_nat = m.sb("nodes_nat", [FF * NODES, D])
    rel = m.sb("rel", [BUCKETS, HEADS])
    onehot = m.sb("onehot", [BUCKETS, ERW])
    erow = m.sb("erow", [HEADS, ERW])
    identf = g["identf"]
    ebrev = m.sb("ebrev", [P, HEADS, NEAR])
    flip = m.sb("flip", [P, P])
    b2f = m.sb("b2f", [P, FF, D])
    b2d = m.sb("b2d", [P, FF, D])
    psW = m.ps("psW", [P, 8, D])
    psN = m.ps("psN", [P, 512])
    psE = m.ps("psE", [P, 512])
    psF = [m.ps(f"psF{i}", [P, CH]) for i in range(2)]
    flipped, flip_taken = m.sem("flipped"), m.sem("flip_taken")
    loaded_x, loaded_w, loaded_misc = m.sem("loaded_x"), m.sem("loaded_w"), m.sem("loaded_misc")
    loaded_b2, loaded_rel = m.sem("loaded_b2"), m.sem("loaded_rel")
    made, zeroed = m.sem("made"), m.sem("zeroed")
    transposed, bias_ready, erow_ready = m.sem("transposed"), m.sem("bias_ready"), m.sem("erow_ready")
    erow_stored, eb_loaded = m.sem("erow_stored"), m.sem("eb_loaded")
    copied, split = m.sem("copied"), m.sem("split")
    squares = ["L0_attn_Wq", "L0_attn_Wk", "L0_attn_Wv", "L0_attn_Wo", "L1_ffn_W_r", "L1_ffn_W_k", "L1_ffn_W_v"]

    def bcast(name, parts=P):
        a = ins[name]
        n = 1
        for s in a.shape:
            n *= s
        return bass.AP(a.tensor, 0, [[0, parts], [1, n]])

    def column(name):
        return ins[name].rearrange("(d o) -> d o", o=1)

    W_N = len(squares) + FF

    with nc.Block() as block:

        @block.sync
        def _(sp):
            sp.dma_start(rel[:, :], ins["L0_attn_rel_emb"]).then_inc(loaded_rel, 16)
            sp.dma_start(onehot[:, :], ins["bucket_onehot"]).then_inc(loaded_rel, 16)
            for i, name in enumerate(squares):
                sp.dma_start(wnat[:, i, :], ins[name]).then_inc(loaded_w, 16)
            for f, n in enumerate("qkv"):
                sp.dma_start(nodes_nat[f * NODES:(f + 1) * NODES, :], ins[f"L0_ffn_{n}_node_w"]).then_inc(loaded_w, 16)
            sp.wait_ge(erow_ready, 2)
            sp.dma_start(g["erow_dram"], erow[:, :]).then_inc(erow_stored, 16)
            x_t = ins["L0_attn_x"].rearrange("b (t p) d -> p (b t) d", p=P)
            for b in range(B):
                sp.dma_start(g["x"][:, b * TPB:(b + 1) * TPB, :], x_t[:, b * TPB:(b + 1) * TPB, :]).then_inc(loaded_x, 16)
            for i, name in enumerate(["L1_attn_Wq", "L1_attn_Wk", "L1_attn_Wv"]):
                sp.dma_start(g["w_c"][:, i, :], ins[name]).then_inc(loaded_x, 16)
            sp.wait_ge(erow_stored, 16)
            sp.dma_start(ebrev[:, :, :], bass.AP(g["erow_dram"].tensor, 0, [[1, P], [ERW, HEADS], [1, NEAR]])).then_inc(eb_loaded, 16)
            sp.wait_ge(loaded_w, 16 * W_N)
            sp.wait_ge(loaded_x, 16 * (B + 3))

        @block.scalar
        def _(act):
            act.wait_ge(bias_ready, 1)
            act.activation(erow[:, :], psE[0:HEADS, 0:ERW], ACT.Exp, scale=HEAD_SCALE).then_inc(erow_ready, 1)
            with nc.allow_non_contiguous_dma(reason="columns of biases, once"):
                for i, name in enumerate(["L0_attn_bq", "L0_attn_bk"]):
                    act.dma_start(g["bias_qk"][:, i:i + 1], column(name)).then_inc(loaded_misc, 16)
                for i, name in enumerate(["L1_ffn_mu_r", "L1_ffn_mu_k"]):
                    act.dma_start(g["mu"][:, i:i + 1], column(name)).then_inc(loaded_misc, 16)
                for f, nm in enumerate("qkv"):
                    act.dma_start(g["b1"][:, f, :], ins[f"L0_ffn_{nm}_b1"].rearrange("(m l) h -> (l h) m", l=2)).then_inc(loaded_misc, 16)
            act.dma_start(g["bv"][:, :], bcast("L0_attn_bv")).then_inc(loaded_misc, 16)
            act.dma_start(g["bo"][:, :], bcast("L0_attn_bo")).then_inc(loaded_misc, 16)
            for f, nm in enumerate("qkv"):
                act.dma_start(g["node_b"][:, f * NODES:(f + 1) * NODES], bcast(f"L0_ffn_{nm}_node_b")).then_inc(loaded_misc, 16)
                act.dma_start(g["w1"][:, f, :].rearrange("d (l h) -> d l h", l=LEAVES), ins[f"L0_ffn_{nm}_w1"].rearrange("l d h -> d l h")).then_inc(loaded_misc, 16)
                act.dma_start(g["w2"][:, f, :, :], ins[f"L0_ffn_{nm}_w2"].rearrange("(m l) h o -> (l h) m o", l=2)).then_inc(loaded_misc, 16)
            act.wait_ge(zeroed, 1)
            for f, nm in enumerate("qkv"):
                r = SELROW + f * LEAVES
                act.dma_start(b2f[r:r + LEAVES, f, :], ins[f"L0_ffn_{nm}_b2"]).then_inc(loaded_b2, 16)
            act.wait_ge(transposed, 1)
            act.activation(g["w_a"][:, :, :], psW[:, 0:4, :], ACT.Copy).then_inc(copied, 1)
            act.activation(g["w_d"][:, :, :], psW[:, 4:7, :], ACT.Copy).then_inc(copied, 1)
            act.activation(g["node_wT"][:, :], psN[:, 0:FF * NODES], ACT.Copy).then_inc(copied, 1)
            act.wait_ge(copied, 3)
            for i in range(HEADS // 2):
                act.wait_ge(flipped, i + 1)
                act.activation(g["ebias"][:, 2 * i:2 * i + 2, :].rearrange("p h q -> p (h q)"), psF[i % 2][:, :], ACT.Copy).then_inc(flip_taken, 1)
            act.wait_ge(flip_taken, HEADS // 2)
            act.wait_ge(loaded_misc, 16 * (7 + 2 + 3 * FF))

        @block.gpsimd
        def _(pool):
            st = Steps(pool, made)
            st.did(pool.memset(identf[:, :], 0.0))
            st.did(pool.memset(g["identb"][:, :], 0.0))
            st.did(pool.memset(flip[:, :], 0.0))
            st.did(pool.memset(g["tri"][:, :], 1.0))
            st.did(pool.memset(g["maskneg"][:, :], 0.0))
            st.did(pool.memset(g["masknegT"][:, :], 0.0))
            st.did(pool.memset(g["leafx"][:, :], -NEG))
            st.settle()
            for t in (identf, g["identb"]):
                st.did(pool.affine_select(out=t[:, :], in_=t[:, :], compare_op=ALU.not_equal, fill=1.0, base=0,
                                          pattern=[[-1, P]], channel_multiplier=1))
            st.did(pool.affine_select(out=flip[:, :], in_=flip[:, :], compare_op=ALU.not_equal, fill=1.0, base=1 - P,
                                      pattern=[[1, P]], channel_multiplier=1))
            st.did(pool.affine_select(out=g["tri"][:, :], in_=g["tri"][:, :], compare_op=ALU.is_ge, fill=0.0, base=0,
                                      pattern=[[1, NEAR]], channel_multiplier=-1))
            st.did(pool.affine_select(out=g["maskneg"][:, :], in_=g["maskneg"][:, :], compare_op=ALU.is_ge, fill=NEG, base=0,
                                      pattern=[[-1, P]], channel_multiplier=1))
            st.did(pool.affine_select(out=g["masknegT"][:, :], in_=g["masknegT"][:, :], compare_op=ALU.is_ge, fill=NEG, base=0,
                                      pattern=[[1, P]], channel_multiplier=-1))
            st.did(pool.affine_select(out=g["leafx"][:, :], in_=g["leafx"][:, :], compare_op=ALU.is_ge, fill=0.0, base=0,
                                      pattern=[[1, FF * LEAVES * LW]], channel_multiplier=-LW))
            st.settle()
            st.did(pool.affine_select(out=g["leafx"][:, :], in_=g["leafx"][:, :], compare_op=ALU.is_ge, fill=0.0, base=LW - 1,
                                      pattern=[[-1, FF * LEAVES * LW]], channel_multiplier=LW))
            st.settle()

        @block.vector
        def _(dve):
            dve.memset(b2f[:, :, :], 0.0).then_inc(zeroed, 1)
            st = Steps(dve, split)
            st.did(dve.memset(g["selT"][:, :], 0.0))
            dve.wait_ge(erow_ready, 1)
            dve.memset(erow[:, 0:P - 1], 0.0).then_inc(erow_ready, 1)
            dve.wait_ge(loaded_b2, 16 * FF)
            dve.wait_ge(zeroed, 1)
            for i in range(PARTS):
                src = b2f if i == 0 else b2d
                st.did(dve.tensor_copy(g["b2p"][:, i, :, :], src[:, :, :]))
                st.settle()
                if i < PARTS - 1:
                    st.did(dve.tensor_tensor(b2d[:, :, :], src[:, :, :], g["b2p"][:, i, :, :], ALU.subtract))
                    st.settle()

        @block.tensor
        def _(pe):
            pe.wait_ge(loaded_rel, 32)
            pe.matmul(psE[0:HEADS, 0:ERW], rel[:, :], onehot[:, :], start=True, stop=True).then_inc(bias_ready, 1)
            pe.wait_ge(made, 10)
            pe.wait_ge(loaded_w, 16 * W_N)
            for i in range(7):
                pe.transpose(psW[:, i, :], wnat[:, i, :], identf[:, :])
            pe.transpose(psN[:, 0:FF * NODES], nodes_nat[:, :], identf[0:FF * NODES, 0:FF * NODES]).then_inc(transposed, 1)
            pe.wait_ge(eb_loaded, 16)
            for i in range(HEADS // 2):
                if i >= 2:
                    pe.wait_ge(flip_taken, i - 1)
                pe.matmul(psF[i % 2][:, :], flip[:, :], ebrev[:, 2 * i:2 * i + 2, :].rearrange("p h q -> p (h q)"), start=True, stop=True).then_inc(flipped, 1)


def pipeline(eng, stages, count=NCH):
    most = max(lag for _, lag in stages)
    start = most + 2 + most % 2

    def step(n, u, static):
        for stage, lag in stages:
            if not static:
                stage(n - lag, (u - lag) % 2, False)
            elif 0 <= n - lag < count:
                stage(n - lag, (u - lag) % 2, n - lag < 2)

    for n in range(start):
        step(n, n % 2, True)
    if start < count:
        with eng.Fori(start // 2, count // 2) as pair:
            for u in range(2):
                step(pair * 2 + u, u, False)
    for n in range(count, count + most):
        step(n, n % 2, True)


class Norm:
    STATS, SCALE = TPC + TPC, 4

    def __init__(self, m, x):
        self.x = x
        self.stats, self.mv = m.sb("stats", [P, 2, TPC, 6]), m.sb("mv", [P, 2, TPC, 2])
        self.var, self.root = m.sb("var", [P, 2, TPC]), m.sb("root", [P, 2, TPC])
        self.newton, self.xn = m.sb("newton", [P, 2, 2, TPC]), m.sb("xn", [P, 2, TPC, D])
        self.stat_steps, self.scale_steps = m.sem("stat_steps"), m.sem("scale_steps")
        self.var_ready, self.root_ready, self.xn_ready = m.sem("var_ready"), m.sem("root_ready"), m.sem("xn_ready")
        self.passed = m.sem("passed")

    def statistics(self, dve, c, u):
        st = Steps(dve, self.stat_steps, c * self.STATS)
        for t in range(TPC):
            st.did(dve.bn_stats(self.stats[:, u, t, :], self.x[:, c * TPC + t, :]))
        st.settle_alone(self.passed)
        for t in range(TPC):
            st.did(dve.bn_aggr(self.mv[:, u, t, :], self.stats[:, u, t, :]))
        st.settle()
        dve.tensor_scalar(self.var[:, u, :], self.mv[:, u, :, 1], EPS, None, ALU.add).then_inc(self.var_ready, 1)

    def take_root(self, act, c, u):
        act.wait_ge(self.var_ready, c + 1)
        act.activation(self.root[:, u, :], self.var[:, u, :], ACT.Sqrt).then_inc(self.root_ready, 1)

    def scale(self, dve, c, u, transposed, early):
        st = Steps(dve, self.scale_steps, c * self.SCALE)
        r, t = self.newton[:, u, 0, :], self.newton[:, u, 1, :]
        dve.wait_ge(self.root_ready, c + 1)
        st.did(dve.reciprocal(r, self.root[:, u, :]))
        st.settle()
        st.did(dve.scalar_tensor_tensor(t, r, -0.5, r, ALU.mult, ALU.mult))
        st.settle()
        st.did(dve.tensor_tensor(t, t, self.var[:, u, :], ALU.mult))
        st.settle()
        st.did(dve.scalar_tensor_tensor(r, t, 1.5, r, ALU.add, ALU.mult))
        st.settle()
        if not early:
            dve.wait_ge(transposed, c - 1)
        for t in range(TPC):
            last = dve.tensor_scalar(self.xn[:, u, t, :], self.x[:, c * TPC + t, :], self.mv[:, u, t, 0:1],
                                     self.newton[:, u, 0, t:t + 1], ALU.subtract, ALU.mult)
        last.then_inc(self.xn_ready, 1)


def project_heads(nc, m, g, w, biased):
    norm = Norm(m, g["x"])
    xnT = m.sb("xnT", [P, 2, CH])
    qk = m.sb("qk", [P, 2, 2, CH])
    rest = m.sb("rest", [P, 2, 2, CH])
    parts = [m.sb(f"parts{u}", [P, 2, PARTS, CH], BF16) for u in range(2)]
    psT = [m.ps(f"psT{u}", [P, CH]) for u in range(2)]
    psQK = [m.ps(f"psQK{u}", [P, 2, CH]) for u in range(2)]
    psV = [m.ps(f"psV{u}", [P, TPC, D]) for u in range(2)]
    transposed, xnT_ready = m.sem("transposed"), m.sem("xnT_ready")
    qkv_done, qk_ready, v_taken = m.sem("qkv_done"), m.sem("qk_ready"), m.sem("v_taken")
    hi_ready, rest_ready, mid_ready, lo_ready = m.sem("hi_ready"), m.sem("rest_ready"), m.sem("mid_ready"), m.sem("lo_ready")
    passed = m.sem("passed_split")
    stored = [m.sem(f"stored{u}") for u in range(2)]
    STORES = 2 * PARTS

    with nc.Block() as block:

        @block.vector
        def _(dve):
            def statistics(c, u, early):
                norm.statistics(dve, c, u)

            def scale(c, u, early):
                norm.scale(dve, c, u, transposed, early)

            def values(c, u, early):
                dve.wait_ge(qkv_done, c + 1)
                v_all = g["v_all"][:, :, :, :].rearrange("p h (c t) e -> p h c t e", t=TPC)
                for t in range(TPC):
                    vout = v_all[:, :, c, t, :]
                    vin = psV[u][:, t, :].rearrange("p (h e) -> p h e", h=HEADS)
                    if biased:
                        last = dve.tensor_tensor(vout, vin, g["bv"][:, :].rearrange("p (h e) -> p h e", h=HEADS), ALU.add)
                    else:
                        last = dve.tensor_copy(vout, vin)
                last.then_inc(v_taken, 1)

            def lows(c, u, early):
                dve.wait_ge(mid_ready, c + 1)
                dve.tensor_tensor(parts[u][:, :, 2, :], rest[:, u], parts[u][:, :, 1, :], ALU.subtract).then_inc(lo_ready, 1)

            pipeline(dve, [(scale, 1), (statistics, 0), (values, 3), (lows, 4)])

        @block.gpsimd
        def _(pool):
            def rests(c, u, early):
                wait_alone(pool, hi_ready, c + 1, passed)
                pool.tensor_tensor(rest[:, u], qk[:, u], parts[u][:, :, 0, :], ALU.subtract).then_inc(rest_ready, 1)

            pipeline(pool, [(rests, 3)])

        @block.scalar
        def _(act):
            def root(c, u, early):
                norm.take_root(act, c, u)

            def turned(c, u, early):
                act.wait_ge(transposed, c + 1)
                if not early:
                    act.wait_ge(qkv_done, c - 1)
                act.activation(xnT[:, u, :], psT[u][:, :], ACT.Copy).then_inc(xnT_ready, 1)

            def highs(c, u, early):
                act.wait_ge(qkv_done, c + 1)
                if not early:
                    act.wait_ge(rest_ready, c - 1)
                for i in range(2):
                    if biased:
                        ins = act.activation(qk[:, u, i, :], psQK[u][:, i, :], ACT.Identity, bias=g["bias_qk"][:, i:i + 1])
                    else:
                        ins = act.activation(qk[:, u, i, :], psQK[u][:, i, :], ACT.Copy, scale=HEAD_SCALE if i == 0 else 1.0)
                ins.then_inc(qk_ready, 1)
                act.wait_ge(qk_ready, c + 1)
                if not early:
                    act.wait_ge(stored[u], (c - u) * (8 * STORES))
                act.activation(parts[u][:, :, 0, :], qk[:, u], ACT.Copy).then_inc(hi_ready, 1)

            def mids(c, u, early):
                act.wait_ge(rest_ready, c + 1)
                act.activation(parts[u][:, :, 1, :], rest[:, u], ACT.Copy).then_inc(mid_ready, 1)

            pipeline(act, [(turned, 1), (root, 0), (highs, 3), (mids, 4)])

        @block.tensor
        def _(pe):
            def turn(c, u, early):
                pe.wait_ge(norm.xn_ready, c + 1)
                if not early:
                    pe.wait_ge(xnT_ready, c - 1)
                for t in range(TPC):
                    last = pe.transpose(psT[u][:, t * P:(t + 1) * P], norm.xn[:, u, t, :], g["identf"][:, :])
                last.then_inc(transposed, 1)

            def project(c, u, early):
                pe.wait_ge(xnT_ready, c + 1)
                if not early:
                    pe.wait_ge(qk_ready, c - 1)
                    pe.wait_ge(v_taken, c - 1)
                for i in range(2):
                    pe.matmul(psQK[u][:, i, :], w[:, i, :], xnT[:, u, :], start=True, stop=True)
                for t in range(TPC):
                    last = pe.matmul(psV[u][:, t, :], xnT[:, u, t * P:(t + 1) * P], w[:, 2, :], start=True, stop=True)
                last.then_inc(qkv_done, 1)

            pipeline(pe, [(turn, 1), (project, 2)])

        @block.sync
        def _(sp):
            def store(part, ready):
                def run(c, u, early):
                    sp.wait_ge(ready, c + 1)
                    at = (c - u) * (HSZ // 2) + u * CH
                    q = bass.AP(g["q_dram"].tensor, at + part * HD * T, [[B * HSZ, HEADS], [T, HD], [1, CH]])
                    sp.dma_start(q, parts[u][:, 0, part, :]).then_inc(stored[u], 16)
                    k = bass.AP(g["k_dram"].tensor, at + part * T, [[B * HSZ, HEADS], [PARTS * T, HD], [1, CH]])
                    sp.dma_start(k, parts[u][:, 1, part, :]).then_inc(stored[u], 16)
                return run

            pipeline(sp, [(store(0, hi_ready), 0), (store(1, mid_ready), 1), (store(2, lo_ready), 1)])
            for u in range(2):
                sp.wait_ge(stored[u], 16 * STORES * NCH // 2)


def attend_heads(nc, m, g, causal):
    SUMMED = TPB // 2
    ORDER = list(range(TPB)) if causal else [5, 4, 6, 3, 1, 0, 2, 7]

    def sums_before(k):
        return sum(qb < SUMMED for qb in ORDER[:k])

    NG = HEADS * B
    LAG = 3
    ROWS_AT = LAG
    halves = [[h for h in range(2) if (h + 1) * CH > kb * P] for kb in range(TPB)]
    first_unit = [sum(len(x) for x in halves[:kb]) for kb in range(TPB + 1)]
    UNITS = first_unit[-1]
    NS = 3
    assert UNITS % NS == 0

    def columns(kb, h):
        lo = max(h * CH, kb * P) if causal or kb < SUMMED else h * CH
        return lo, (h + 1) * CH

    def near(kb):
        return kb * P, min(T, kb * P + (NEAR if causal else P))

    qS = [m.sb(f"qS{u}", [P, T], BF16) for u in range(B)]
    kS = [m.sb(f"kS{u}", [P, T], BF16) for u in range(B)]
    probs = [m.sb(f"probs{p}", [P, TPB, T]) for p in range(2)]
    masked = [m.sb(f"masked{p}", [P, TPB, P]) for p in range(2)] if not causal else None
    v_ones = [m.sb(f"v_ones{p}", [P, TPB, VW]) for p in range(2)]
    v_only = [m.sb(f"v_only{p}", [P, TPB, VW]) for p in range(2)] if not causal else None
    ones_only = m.sb("ones_only", [P, VW]) if not causal else None
    mx = m.sb("mx", [P, 2, TPB])
    NMP = 2 if causal else 3
    nm = m.sb("nm", [P, 2, NMP, TPB], BF16)
    mrow = [m.sb(f"mrow{p}", [NMP * TPB, P], BF16) for p in range(2)]
    if not causal:
        nm_rest = m.sb("nm_rest", [P, 2, TPB])
        unused = m.sb("unused", [P, 2, T])
        later = m.sb("later", [P, 2, SUMMED])
    oT = [m.sb(f"oT{p}", [P, 2 * P]) for p in range(2)]
    psM = [m.ps(f"psM{i}", [P, T]) for i in range(2)]
    psS = [m.ps(f"psS{i}", [P, CH]) for i in range(NS)]
    psO = m.ps("psO", [P, CH])
    psR = psO[0:NMP * TPB, 2 * P:3 * P]

    cleared, pool_ready = m.sem("cleared"), m.sem("pool_ready")
    s_loaded = [m.sem(f"s_loaded{u}") for u in range(B)]
    r_loaded = [m.sem(f"r_loaded{u}") for u in range(B)]
    o_stored = [m.sem(f"o_stored{p}") for p in range(2)]
    maxima_done = m.sem("maxima_done")
    max_taken = m.sem("max_taken")
    nm_hi, nm_ready = m.sem("nm_hi"), m.sem("nm_ready")
    later_done, later_kept = m.sem("later_done"), m.sem("later_kept")
    nm_steps = m.sem("nm_steps")
    rows_done, rows_taken = m.sem("rows_done"), m.sem("rows_taken")
    scores_done = m.sem("scores_done")
    exp_done = m.sem("exp_done")
    near_done = m.sem("near_done")
    v_staged, passed = m.sem("v_staged"), m.sem("passed")
    pv_done, o_taken = m.sem("pv_done"), m.sem("o_taken")

    def program(eng, step):
        for u in range(B):
            step(u, u, u)
        with eng.Fori(1, HEADS - 1) as h:
            for u in range(B):
                step(h * B + u, u, None)
        for u in range(B):
            step(NG - B + u, u, NG - B + u)

    with nc.Block() as block:

        @block.sync
        def _(sp):
            def load_s(n, u):
                q = bass.AP(g["q_dram"].tensor, n * HSZ, [[T, PARTS * HD], [0, PARTS], [1, T]])
                sp.dma_start(qS[u][0:SROWS, :], q).then_inc(s_loaded[u], 16)
                k = bass.AP(g["k_dram"].tensor, n * HSZ, [[0, PARTS], [T, HD * PARTS], [1, T]])
                sp.dma_start(kS[u][0:SROWS, :], k).then_inc(s_loaded[u], 16)

            def load_r(n, u):
                sp.wait_ge(rows_taken, n + 1)
                sp.dma_start(qS[u][MROW:MROW + NMP, :].rearrange("s (q w) -> s q w", w=P), mrow[u % 2][:, :]).then_inc(r_loaded[u], 16)

            for n in range(3):
                sp.wait_ge(cleared, n + 1)
                load_s(n, n)
            sp.wait_ge(cleared, B)
            load_r(0, 0)

            def step(n, u, known):
                if known is None or known < NG - 3:
                    if known != 0:
                        sp.wait_ge(scores_done, n * UNITS)
                    load_s(n + 3, (u + 3) % B)
                if known is None or known < NG - 1:
                    load_r(n + 1, (u + 1) % B)
                if known != 0:
                    sp.wait_ge(o_taken, n)
                    sp.dma_start(store_at(n - 1), oT[(u + 1) % 2][:, :]).then_inc(o_stored[(u + 1) % 2], 16)

            def store_at(n):
                return bass.AP(g["o_dram"].tensor, n * (VW * T), [[2 * P, 4], [T, VW], [1, 2 * P]])

            program(sp, step)
            sp.wait_ge(o_taken, NG)
            sp.dma_start(store_at(NG - 1), oT[1][:, :]).then_inc(o_stored[1], 16)
            for p in range(2):
                sp.wait_ge(o_stored[p], 16 * NG // 2)

        @block.vector
        def _(dve):
            for u in range(B):
                dve.memset(qS[u][:, :].bitcast(F32), 0.0)
                dve.memset(kS[u][:, :], 1.0).then_inc(cleared, 1)

            def maxima(n, p, static):
                for k in range(TPB):
                    qb = ORDER[k]
                    dve.wait_ge(maxima_done, n * TPB + k + 1)
                    w = (qb + 1) * P if causal else T
                    if k == 0 and (static is None or static >= 2):
                        dve.wait_ge(nm_ready, n - 1)
                        if not causal:
                            dve.wait_ge(later_done, (n - 1) * SUMMED)
                    dve.tensor_reduce(mx[:, p, qb:qb + 1], psM[k % 2][:, 0:w], AXX, ALU.max, negate=not causal).then_inc(max_taken, 1)
                if not causal:
                    return
                dve.wait_ge(max_taken, (n + 1) * TPB)
                if static is None or static >= 2:
                    dve.wait_ge(rows_done, n - 1)
                dve.tensor_scalar(nm[:, p, 0, :], mx[:, p, :], -1.0, None, ALU.mult).then_inc(nm_hi, 1)
                dve.wait_ge(nm_hi, n + 1)
                dve.scalar_tensor_tensor(nm[:, p, 1, :], mx[:, p, :], -1.0, nm[:, p, 0, :], ALU.mult, ALU.subtract).then_inc(nm_ready, 1)

            for n in range(2):
                maxima(n, n, n)

            def step(n, u, known):
                if known is None or known < NG - 2:
                    maxima(n + 2, u % 2, None if known is None else known + 2)

            program(dve, step)

        @block.gpsimd
        def _(pool):
            for p in range(2):
                pool.memset(v_ones[p][:, :, :], 0.0)
                if not causal:
                    pool.memset(v_only[p][:, :, :], 0.0)
            if not causal:
                pool.memset(ones_only[:, :], 0.0)
                pool.memset(g["later"][:, :, :, :], 0.0)
            pool.memset(mrow[0][:, :], 0.0).then_inc(pool_ready, 1)
            pool.wait_ge(pool_ready, 1)
            if not causal:
                pool.memset(ones_only[:, HD:2 * HD], 1.0)
            pool.memset(v_ones[0][:, :, HD:2 * HD], 1.0)
            pool.memset(v_ones[1][:, :, HD:2 * HD], 1.0).then_inc(pool_ready, 1)

            def stage_v(n, p):
                src = g["v_all"][:, :, :, :].rearrange("p h (b t) e -> p (h b) t e", b=B)[:, n, :, :]
                ins = pool.tensor_copy(v_ones[p][:, :, 0:HD], src)
                if not causal:
                    ins = pool.tensor_copy(v_only[p][:, :, 0:HD], src)
                ins.then_inc(v_staged, 1)

            def minus_maxima(n, p, static):
                st = Steps(pool, nm_steps, n * 3)
                wait_alone(pool, max_taken, (n + 1) * TPB, passed)
                if static is None or static >= 2:
                    wait_alone(pool, rows_done, n - 1, passed)
                st.did(pool.tensor_copy(nm[:, p, 0, :], mx[:, p, :]))
                st.settle_alone(passed)
                st.did(pool.tensor_tensor(nm_rest[:, p, :], mx[:, p, :], nm[:, p, 0, :], ALU.subtract))
                st.settle_alone(passed)
                st.did(pool.tensor_copy(nm[:, p, 1, :], nm_rest[:, p, :]))
                st.settle_alone(passed)
                pool.tensor_tensor(nm[:, p, 2, :], nm_rest[:, p, :], nm[:, p, 1, :], ALU.subtract).then_inc(nm_ready, 1)

            def keep_later(n, p):
                pool.wait_ge(later_done, (n + 1) * SUMMED)
                pool.tensor_copy(g["later"][:, n, :, 0], later[:, p, :]).then_inc(later_kept, 1)

            pool.wait_ge(pool_ready, 2)
            stage_v(0, 0)
            if not causal:
                minus_maxima(0, 0, 0)
                keep_later(0, 0)

            def step(n, u, known):
                p = u % 2
                more = known is None or known < NG - 1
                if not causal and more:
                    minus_maxima(n + 1, 1 - p, None if known is None else known + 1)
                for kb in range(TPB):
                    a, z = near(kb)
                    wait_alone(pool, exp_done, n * UNITS + first_unit[kb + 1], passed)
                    if causal:
                        pool.tensor_tensor(probs[p][:, kb, a:z], probs[p][:, kb, a:z], ebias_of(n, u, z - a), ALU.mult).then_inc(near_done, 1)
                    else:
                        if kb == 0 and (known is None or known >= 2):
                            pool.wait_ge(pv_done, n - 1)
                        pool.tensor_tensor(masked[p][:, kb, 0:z - a], probs[p][:, kb, a:z], g["tri"][:, 0:z - a], ALU.mult).then_inc(near_done, 1)
                    if kb == 1 and not causal and more:
                        keep_later(n + 1, 1 - p)
                    if kb == LAG and more:
                        if known != 0:
                            pool.wait_ge(pv_done, n)
                        stage_v(n + 1, 1 - p)

            def ebias_of(n, u, w):
                return g["ebias"][:, n // B if isinstance(n, int) else (n - u) // B, 0:w]

            program(pool, step)

        @block.scalar
        def _(act):
            def take_rows(n, u, static):
                p = u % 2
                act.wait_ge(rows_done, n + 1)
                if static is None or static >= 2:
                    m2 = (u + 2) % B
                    act.wait_ge(r_loaded[m2], (n - 2 - m2 + B) * (16 // B))
                act.activation(mrow[p][:, :], psR, ACT.Copy).then_inc(rows_taken, 1)

            def sum_later(n, k, p, static):
                qb = ORDER[k]
                if qb >= SUMMED:
                    return
                a, before = (qb + 1) * P, sums_before(k)
                act.wait_ge(max_taken, n * TPB + k + 1)
                if static is None or static > 0 or before >= 2:
                    act.wait_ge(later_done, n * SUMMED + before - 1)
                if k == 0 and (static is None or static >= 2):
                    act.wait_ge(later_kept, n - 1)
                act.activation(unused[:, before % 2, 0:T - a], psM[k % 2][:, a:T], ACT.Exp, bias=mx[:, p, qb:qb + 1],
                               accum_out=later[:, p, qb:qb + 1]).then_inc(later_done, 1)

            act.wait_ge(pool_ready, 1)
            if not causal:
                for k in range(TPB):
                    sum_later(0, k, 0, 0)
            take_rows(0, 0, 0)
            if not causal:
                for k in range(TPB - 1):
                    sum_later(1, k, 1, 1)

            def take_o(n, p, static):
                act.wait_ge(pv_done, n + 1)
                if static is None or static >= 2:
                    act.wait_ge(o_stored[p], (n - p) * 8)
                act.activation(oT[p][:, :], psO[:, 0:2 * P], ACT.Copy).then_inc(o_taken, 1)

            def step(n, u, known):
                p = u % 2
                for kb in range(TPB):
                    for i, h in enumerate(halves[kb]):
                        a, z = columns(kb, h)
                        unit = first_unit[kb] + i
                        act.wait_ge(scores_done, n * UNITS + unit + 1)
                        if kb == 0 and i == 0 and (known is None or known >= 2):
                            act.wait_ge(pv_done, n - 1)
                        act.activation(probs[p][:, kb, a:z], psS[unit % NS][:, a - h * CH:z - h * CH], ACT.Exp).then_inc(exp_done, 1)
                        if i > 0:
                            continue
                        if not causal and kb == 0 and (known is None or known < NG - 1):
                            sum_later(n + 1, TPB - 1, 1 - p, None if known is None else known + 1)
                        elif not causal and kb > 0 and (known is None or known < NG - 2):
                            sum_later(n + 2, kb - 1, p, None if known is None else known + 2)
                        if kb == ROWS_AT and (known is None or known < NG - 1):
                            take_rows(n + 1, (u + 1) % B, None if known is None else known + 1)
                    if kb == LAG - 1 and known != 0:
                        take_o(n - 1, 1 - p, None if known is None else known - 1)

            program(act, step)
            take_o(NG - 1, 1, NG - 1)

        @block.tensor
        def _(pe):
            def max_scores(n, u, k, static):
                qb = ORDER[k]
                if static is None or static > 0 or k >= 2:
                    pe.wait_ge(max_taken, n * TPB + k - 1)
                    if not causal and ORDER[k - 2] < SUMMED:
                        pe.wait_ge(later_done, n * SUMMED + (sums_before(k - 1) if k >= 2 else sums_before(TPB + k - 1) - SUMMED))
                if k == 0:
                    pe.wait_ge(s_loaded[u], (n - u + B) * (32 // B))
                w = (qb + 1) * P if causal else T
                for h in range(-(-w // CH)):
                    a, z = h * CH, min((h + 1) * CH, w)
                    holds_diagonal = causal and z == w
                    last = pe.matmul(psM[k % 2][:, a:z], qS[u][0:MROW, qb * P:(qb + 1) * P], kS[u][0:MROW, a:z], start=True, stop=not holds_diagonal)
                if causal:
                    last = pe.matmul(psM[k % 2][:, w - P:w], g["identb"][:, :], g["maskneg"][:, :], start=False, stop=True)
                last.then_inc(maxima_done, 1)

            def max_rows(n, p, static):
                pe.wait_ge(nm_ready, n + 1)
                if static is None or static > 0:
                    pe.wait_ge(o_taken, n - 1)
                pe.matmul(psR, nm[:, p, :, :].rearrange("p s q -> p (s q)"), g["identb"][:, :], start=True, stop=True).then_inc(rows_done, 1)

            def scores(n, u, kb, static):
                if kb == 0:
                    pe.wait_ge(r_loaded[u], (n - u + B) * (16 // B))
                for i, h in enumerate(halves[kb]):
                    a, z = columns(kb, h)
                    unit = first_unit[kb] + i
                    if static is None or static > 0 or unit >= NS:
                        pe.wait_ge(exp_done, n * UNITS + unit + 1 - NS)
                    masks = causal and i == 0
                    last = pe.matmul(psS[unit % NS][:, a - h * CH:z - h * CH], kS[u][:, kb * P:(kb + 1) * P], qS[u][:, a:z], start=True, stop=not masks)
                    if masks:
                        last = pe.matmul(psS[unit % NS][:, a - h * CH:a - h * CH + P], g["identb"][:, :], g["masknegT"][:, :], start=False, stop=True)
                    last.then_inc(scores_done, 1)

            def values(n, p, kb, static):
                if kb == 0:
                    pe.wait_ge(v_staged, n + 1)
                    pe.wait_ge(rows_taken, min(n + 2, NG) if isinstance(n, int) else n + 2)
                    if static is None or static > 0:
                        pe.wait_ge(o_taken, n)
                if causal:
                    pe.wait_ge(near_done, n * TPB + kb + 1)
                    for c in range(4):
                        out = psO[c * VW:(c + 1) * VW, 0:2 * P]
                        pr = probs[p][:, kb, :].rearrange("p (q w) -> p q w", w=P)
                        if kb <= c:
                            last = pe.matmul(out.rearrange("p (q w) -> p q w", w=P), v_ones[p][:, kb, :], pr[:, c:TPB - c:TPB - 1 - 2 * c, :],
                                             start=kb == 0, stop=False, tile_position=(0, c * VW))
                        elif kb <= TPB - 1 - c:
                            b = TPB - 1 - c
                            last = pe.matmul(out[:, P:2 * P], v_ones[p][:, kb, :], pr[:, b, :],
                                             start=False, stop=kb == TPB - 1 - c, tile_position=(0, c * VW))
                    if kb == TPB - 1:
                        last.then_inc(pv_done, 1)
                    return
                pe.wait_ge(exp_done, n * UNITS + first_unit[kb + 1])
                pr = probs[p][:, kb, :].rearrange("p (q w) -> p q w", w=P)
                for c in range(4):
                    out = psO[c * VW:(c + 1) * VW, 0:2 * P]
                    if kb == 0 and c == 0:
                        pe.matmul(out.rearrange("p (q w) -> p q w", w=P), ones_only[:, :], pr[:, 0:TPB:TPB - 1, :],
                                  start=True, stop=False, tile_position=(0, 0))
                        pe.matmul(out[:, P:2 * P], v_only[p][:, 0, :], pr[:, TPB - 1, :], start=False, stop=False, tile_position=(0, 0))
                    elif kb < c:
                        pe.matmul(out.rearrange("p (q w) -> p q w", w=P), v_ones[p][:, kb, :], pr[:, c:TPB - c:TPB - 1 - 2 * c, :],
                                  start=kb == 0, stop=False, tile_position=(0, c * VW))
                    elif kb >= TPB - 1 - c:
                        pe.matmul(out[:, P:2 * P], ones_only[:, :], pr[:, TPB - 1 - c, :], start=False, stop=False, tile_position=(0, c * VW))
                    else:
                        pe.matmul(out[:, P:2 * P], v_ones[p][:, kb, :], pr[:, TPB - 1 - c, :], start=False, stop=False, tile_position=(0, c * VW))
                    if 0 < c == kb:
                        pe.matmul(out[:, 0:P], ones_only[:, :], pr[:, c, :], start=False, stop=False, tile_position=(0, c * VW))
                if kb < TPB - 1:
                    return
                pe.wait_ge(near_done, (n + 1) * TPB)
                for half in range(2):
                    for c in range(4):
                        qb = TPB - 1 - c if half else c
                        last = pe.matmul(psO[c * VW:(c + 1) * VW, half * P:(half + 1) * P], v_only[p][:, qb, :], masked[p][:, qb, :],
                                         start=False, stop=half == 1, tile_position=(0, c * VW))
                last.then_inc(pv_done, 1)

            pe.wait_ge(cleared, 1)
            for n in range(2):
                for qb in range(TPB):
                    max_scores(n, n, qb, n)
                if n == 0:
                    max_rows(0, 0, 0)

            def step(n, u, known):
                p = u % 2
                for kb in range(TPB):
                    scores(n, u, kb, known)
                    if known is None or known < NG - 2:
                        max_scores(n + 2, (u + 2) % B, kb, None)
                    if kb == ROWS_AT and (known is None or known < NG - 1):
                        max_rows(n + 1, 1 - p, None if known is None or known else 0)
                    if kb == LAG + 1:
                        values(n, p, 0, known)
                    if kb > LAG:
                        values(n, p, kb - LAG, known)
                    if kb < LAG and known != 0:
                        values(n - 1, 1 - p, kb - LAG + TPB, None if known is None else known - 1)

            program(pe, step)
            for kb in range(TPB - LAG, TPB):
                values(NG - 1, 1, kb, NG - 1)


class Gather:

    def __init__(self, nc, m, g):
        self.g = g
        self.den = m.sb("den", [P, B * T * HEADS // P])
        self.rden = m.sb("rden", [P, B * T * HEADS // P])
        self.num = [m.sb(f"num{i}", [P, T]) for i in range(2)]
        self.inv = [m.sb(f"inv{i}", [P, T]) for i in range(2)]
        self.den_loaded, self.rden_ready, self.rden_stored = m.sem("den_loaded"), m.sem("rden_ready"), m.sem("rden_stored")
        self.loaded = [m.sem(f"heads_loaded{i}") for i in range(B)]
        self.att_ready = m.sem("att_ready")

    def reciprocals(self, dve):
        dve.wait_ge(self.den_loaded, 16)
        dve.reciprocal(self.rden[:, :], self.den[:, :]).then_inc(self.rden_ready, 1)

    def divide(self, pool, c, u, att):
        b = c // CPB
        num, inv = (t[b % 2][:, :].rearrange("p (c q w) -> p c q w", q=2, w=P) for t in (self.num, self.inv))
        for k in range(TPC):
            at = k if u == 0 else TPC - 1 - k
            last = pool.tensor_tensor(att[:, u, k, :], num[:, at, u, :], inv[:, at, u, :], ALU.mult)
        last.then_inc(self.att_ready, 1)

    def load(self, sp):
        g, o, r = self.g, self.g["o_dram"].tensor, self.g["r_dram"].tensor
        half = T // 2
        sp.dma_start(self.den[:, :], bass.AP(o, HD * T, [[VW * T, HEADS * B], [half, 2], [1, half]])).then_inc(self.den_loaded, 16)
        for b in range(2):
            self.load_num(sp, b)
        sp.wait_ge(self.rden_ready, 1)
        sp.dma_start(bass.AP(r, 0, [[half, P], [1, half]]), self.rden[:, :]).then_inc(self.rden_stored, 16)
        sp.wait_ge(self.rden_stored, 16)
        for b in range(B):
            if b >= 2:
                sp.wait_ge(self.att_ready, (b - 1) * CPB)
                self.load_num(sp, b)
            sp.dma_start(self.inv[b % 2][:, :], bass.AP(r, b * T, [[B * T, HEADS], [0, HD], [1, T]])).then_inc(self.loaded[b], 16)

    def load_num(self, sp, b):
        o = self.g["o_dram"].tensor
        sp.dma_start(self.num[b % 2][:, :], bass.AP(o, b * (VW * T), [[B * VW * T, HEADS], [T, HD], [1, T]])).then_inc(self.loaded[b], 16)


def add_projected(nc, m, g):
    norm, gather = Norm(m, g["x"]), Gather(nc, m, g)
    att = m.sb("att", [P, 2, TPC, P])
    xnT_now = m.sb("xnT_now", [P, 2, CH])
    NN = FF * NODES
    score = m.sb("score", [P, TPC, NN])
    bits = m.sb("bits", [P, TPC, NN])
    nbits = m.sb("nbits", [P, TPC, NN])
    way = [m.sb(f"way{i}", [P, TPC, FF, 2 ** (i + 1)]) for i in range(DEPTH - 1)]
    sel = m.sb("sel", [P, 2, TPC, P])
    psY = [m.ps(f"psY{u}", [P, TPC, D]) for u in range(2)]
    psT = [m.ps(f"psT{u}", [P, CH]) for u in range(2)]
    psN = [m.ps(f"psN{u}", [P, TPC, NN]) for u in range(2)]
    psL = m.ps("psL", [P, CH])
    projected, added, bias_added = m.sem("projected"), m.sem("added"), m.sem("bias_added")
    transposed, xnT_ready = m.sem("transposed"), m.sem("xnT_ready")
    noded, sel_ready, sel_turned, sel_taken = m.sem("noded"), m.sem("sel_ready"), m.sem("sel_turned"), m.sem("sel_taken")
    route_steps, cleared, lows_done = m.sem("route_steps"), m.sem("cleared"), m.sem("lows_done")
    ROUTE = 3 + DEPTH

    with nc.Block() as block:

        @block.sync
        def _(sp):
            gather.load(sp)

        @block.gpsimd
        def _(pool):
            def bias(c):
                xs = g["x"][:, c * TPC:(c + 1) * TPC, :]
                pool.tensor_tensor(xs, xs, g["bo"][:, :].unsqueeze(1).to_broadcast([P, TPC, D]), ALU.add).then_inc(bias_added, 1)

            def divide(c):
                b, u = c // CPB, c % CPB
                if u == 0:
                    pool.wait_ge(gather.loaded[b], 32)
                if c >= 2:
                    pool.wait_ge(projected, c - 1)
                gather.divide(pool, c, u, att)

            def low_part(c):
                pool.wait_ge(xnT_ready, 2 * c + 2)
                pool.tensor_tensor(g["x_lo"][:, c * CH:(c + 1) * CH], xnT_now[:, c % 2, :], g["x_hi"][:, c * CH:(c + 1) * CH].bitcast(F32),
                                   ALU.subtract).then_inc(lows_done, 1)

            AHEAD = 4
            for c in range(AHEAD):
                bias(c)
            for c in range(NCH):
                divide(c)
                if c + AHEAD < NCH:
                    bias(c + AHEAD)
                if c >= 3:
                    low_part(c - 3)
            for c in range(NCH - 3, NCH):
                low_part(c)

        @block.vector
        def _(dve):
            dve.memset(sel[:, :, :, :], 0.0).then_inc(cleared, 1)
            gather.reciprocals(dve)

            def add(c, u, early):
                xs = g["x"][:, bass.ds(c * TPC, TPC), :]
                dve.wait_ge(bias_added, c + 1)
                dve.wait_ge(projected, c + 1)
                dve.tensor_tensor(xs, psY[u][:, :, :], xs, ALU.add).then_inc(added, 1)
                wait_alone(dve, added, c + 1, norm.passed)
                norm.statistics(dve, c, u)

            def scale(c, u, early):
                norm.scale(dve, c, u, transposed, early)

            def route(c, u, early):
                st = Steps(dve, route_steps, c * ROUTE)
                dve.wait_ge(noded, c + 1)
                st.did(dve.tensor_tensor(score[:, :, :], psN[u][:, :, :], g["node_b"][:, :].unsqueeze(1).to_broadcast([P, TPC, NN]), ALU.add))
                st.settle()
                st.did(dve.tensor_scalar(nbits[:, :, :], score[:, :, :], 0.0, None, ALU.is_lt))
                st.did(dve.tensor_scalar(bits[:, :, :], score[:, :, :], 0.0, None, ALU.is_ge))
                st.settle()
                if not early:
                    dve.wait_ge(sel_turned, c - 1)
                for d in range(DEPTH):
                    lo, w = 2 ** d - 1, 2 ** d
                    for tree in range(FF):
                        if d < DEPTH - 1:
                            out = way[d][:, :, tree, :].rearrange("p t (n s) -> p t n s", s=2)
                        else:
                            a = SELROW + tree * LEAVES
                            out = sel[:, u, :, a:a + LEAVES].rearrange("p t (n s) -> p t n s", s=2)
                        for side, taken in enumerate((nbits, bits)):
                            node = taken[:, :, tree * NODES + lo:tree * NODES + lo + w]
                            if d == 0:
                                last = dve.tensor_copy(out[:, :, :, side], node)
                            else:
                                last = dve.tensor_tensor(out[:, :, :, side], way[d - 1][:, :, tree, :], node, ALU.mult)
                    st.did(last)
                    st.settle()
                assert st.n == ROUTE
                dve.tensor_scalar(sel[:, u, :, 0:FF * LEAVES], sel[:, u, :, SELROW:SELROW + FF * LEAVES], -1.0, None, ALU.add).then_inc(sel_ready, 1)

            pipeline(dve, [(scale, 2), (add, 1), (route, 3)])

        @block.scalar
        def _(act):
            def root(c, u, early):
                norm.take_root(act, c, u)

            def turned(c, u, early):
                act.wait_ge(transposed, c + 1)
                if not early:
                    act.wait_ge(noded, c - 1)
                    act.wait_ge(lows_done, c - 1)
                act.activation(xnT_now[:, u, :], psT[u][:, :], ACT.Copy).then_inc(xnT_ready, 1)
                act.activation(g["x_hi"][:, bass.ds(c * CH, CH)], psT[u][:, :], ACT.Copy).then_inc(xnT_ready, 1)

            def selected(c, u, early):
                act.wait_ge(sel_turned, c + 1)
                act.activation(g["selT"][:, bass.ds(c * CH, CH)], psL[:, :], ACT.Copy).then_inc(sel_taken, 1)

            pipeline(act, [(turned, 2), (root, 1), (selected, 4)])

        @block.tensor
        def _(pe):
            def project(c, u, early):
                pe.wait_ge(gather.att_ready, c + 1)
                if not early:
                    pe.wait_ge(added, c - 1)
                for t in range(TPC):
                    last = pe.matmul(psY[u][:, t, :], att[:, u, t, :], g["w_a"][:, 3, :], start=True, stop=True)
                last.then_inc(projected, 1)

            def turn(c, u, early):
                pe.wait_ge(norm.xn_ready, c + 1)
                if not early:
                    pe.wait_ge(xnT_ready, 2 * (c - 1))
                for t in range(TPC):
                    last = pe.transpose(psT[u][:, t * P:(t + 1) * P], norm.xn[:, u, t, :], g["identf"][:, :])
                last.then_inc(transposed, 1)

            def nodes(c, u, early):
                pe.wait_ge(xnT_ready, 2 * c + 1)
                if not early:
                    pe.wait_ge(route_steps, (c - 2) * ROUTE + 1)
                for t in range(TPC):
                    last = pe.matmul(psN[u][:, t, :], xnT_now[:, u, t * P:(t + 1) * P], g["node_wT"][:, :], start=True, stop=True)
                last.then_inc(noded, 1)

            def select(c, u, early):
                pe.wait_ge(sel_ready, c + 1)
                if not (early and isinstance(c, int) and c == 0):
                    pe.wait_ge(sel_taken, c)
                for t in range(TPC):
                    last = pe.transpose(psL[:, t * P:(t + 1) * P], sel[:, u, t, :], g["identf"][:, :])
                last.then_inc(sel_turned, 1)

            pipeline(pe, [(project, 0), (turn, 2), (select, 4), (nodes, 2)])


def trees(nc, m, g):
    NH = 4
    hid_hi = [m.sb(f"hid_hi{i}", [P, CH], F32R) for i in range(NH)]
    hid_lo = [m.sb(f"hid_lo{i}", [P, CH], F32R) for i in range(NH)]
    hid = [m.sb(f"hid{i}", [P, CH]) for i in range(2)]
    wp = [[[m.sb(f"w{k + 1}{part}{b}", [P, LEAVES * LW], F32R) for part in ("hi", "lo")] for k in range(2)] for b in range(2)]
    vT = m.sb("vT", [P, CH])
    NP = 4
    psH = [m.ps(f"psH{i}", [P, CH]) for i in range(NP)]
    psO = [m.ps(f"psO{i}", [P, CH]) for i in range(2)]
    psV = m.ps("psV", [P, CH])
    hidden_done, hid_ready, out_taken = m.sem("hidden_done"), m.sem("hid_ready"), m.sem("out_taken")
    lo_ready = m.sem("lo_ready")
    w_hi = [[m.sem(f"w_hi{f}{k}") for k in range(2)] for f in range(FF)]
    w_lo = [[m.sem(f"w_lo{f}{k}") for k in range(2)] for f in range(FF)]
    v_turned, v_taken = m.sem("v_turned"), m.sem("v_taken")
    used = m.sem("used")
    LAG = 3

    def split_weights(eng, f, k):
        src = g["w1"][:, f, :] if k == 0 else g["w2"][:, f, :, :].rearrange("p m o -> p (m o)")
        hi, lo = wp[f % 2][k]
        eng.tensor_copy(hi[:, :], src).then_inc(w_hi[f][k], 1)
        eng.wait_ge(w_hi[f][k], 1)
        eng.tensor_tensor(lo[:, :], src, hi[:, :].bitcast(F32), ALU.subtract).then_inc(w_lo[f][k], 1)

    with nc.Block() as block:

        def rounds(eng, body, start=None):
            for f in range(FF):
                if start:
                    start(f)
                if f == 0:
                    for u in range(CPB):
                        body(f, 0, u, u == 0)
                with eng.Fori(1 if f == 0 else 0, B) as b:
                    for u in range(CPB):
                        body(f, b, u, False)

        @block.gpsimd
        def _(pool):
            split_weights(pool, 0, 1)
            for f in range(1, FF):
                if f >= 2:
                    pool.wait_ge(used, (f - 1) * NCH * HID)
                for k in range(2):
                    split_weights(pool, f, k)

        @block.tensor
        def _(pe):
            def start(f):
                for k in range(2):
                    pe.wait_ge(w_lo[f][k], 1)

            def body(f, b, u, first):
                c = b * CPB + u + f * NCH
                toks = bass.ds(b * T + u * CH, CH)
                (w1_hi, w1_lo), (w2_hi, w2_lo) = wp[f % 2]
                for i in range(HID + LAG):
                    if i < HID:
                        n = c * HID + i
                        if not first or i >= NP:
                            pe.wait_ge(hid_ready, n - NP + 1)
                        rows = slice(i * P, (i + 1) * P)
                        pe.matmul(psH[i % NP][:, :], w1_hi[:, rows], g["x_hi"][:, toks], start=True, stop=False)
                        pe.matmul(psH[i % NP][:, :], w1_hi[:, rows], g["x_lo"][:, toks], start=False, stop=False)
                        pe.matmul(psH[i % NP][:, :], w1_lo[:, rows], g["x_hi"][:, toks], start=False, stop=False)
                        a = (f * LEAVES + 2 * i) * LW
                        pe.matmul(psH[i % NP][:, :], g["leafx"][:, a:a + P], g["selT"][:, toks], start=False, stop=True).then_inc(hidden_done, 1)
                    if i == HID:
                        for part in range(PARTS):
                            pe.matmul(psO[u][:, :], g["b2p"][:, part, f, :], g["selT"][:, toks], start=False, stop=False)
                    if i >= LAG:
                        j = i - LAG
                        rows = slice(j * P, (j + 1) * P)
                        pe.wait_ge(hid_ready, c * HID + j + 1)
                        if j == 0 and not (first or (isinstance(b, int) and b == 0 and f == 0)):
                            pe.wait_ge(out_taken, c - 1)
                        pe.matmul(psO[u][:, :], w2_hi[:, rows], hid_hi[j % NH][:, :], start=j == 0, stop=False)
                        pe.matmul(psO[u][:, :], w2_lo[:, rows], hid_hi[j % NH][:, :], start=False, stop=False)
                        pe.wait_ge(lo_ready, c * HID + j + 1)
                        pe.matmul(psO[u][:, :], w2_hi[:, rows], hid_lo[j % NH][:, :], start=False, stop=j == HID - 1).then_inc(used, 1)
                if f == FF - 1:
                    pe.wait_ge(out_taken, c + 1)
                    pe.wait_ge(v_taken, b * CPB + u + 1)
                    for t in range(TPC):
                        last = pe.transpose(psV[:, t * P:(t + 1) * P], vT[:, t * P:(t + 1) * P], g["identf"][:, :])
                    last.then_inc(v_turned, 1)

            rounds(pe, body, start)

        @block.scalar
        def _(act):
            def body(f, b, u, first):
                c = b * CPB + u + f * NCH
                for i in range(HID):
                    n = c * HID + i
                    act.wait_ge(hidden_done, n + 1)
                    if not first or i >= 2:
                        act.wait_ge(lo_ready, n - 1)
                    if not first or i >= NH:
                        act.wait_ge(used, n - NH + 1)
                    act.activation(hid[i % 2][:, :], psH[i % NP][:, :], ACT.Relu, bias=g["b1"][:, f, i:i + 1])
                    act.activation(hid_hi[i % NH][:, :], psH[i % NP][:, :], ACT.Relu, bias=g["b1"][:, f, i:i + 1]).then_inc(hid_ready, 1)

            rounds(act, body)

        @block.vector
        def _(dve):
            dve.sem_inc(v_taken, 1)
            split_weights(dve, 0, 0)

            def body(f, b, u, first):
                c = b * CPB + u + f * NCH
                for i in range(HID):
                    n = c * HID + i
                    dve.wait_ge(hid_ready, n + 1)
                    if not first or i >= NH:
                        dve.wait_ge(used, n - NH + 1)
                    dve.tensor_tensor(hid_lo[i % NH][:, :], hid[i % 2][:, :], hid_hi[i % NH][:, :].bitcast(F32), ALU.subtract).then_inc(lo_ready, 1)
                outputs(f, b, u)

            def outputs(f, b, u):
                c = b * CPB + u + f * NCH
                dve.wait_ge(used, (c + 1) * HID)
                if f < FF - 1:
                    dve.tensor_copy(g["qkT"][:, f, bass.ds(b * T + u * CH, CH)], psO[u][:, :]).then_inc(out_taken, 1)
                else:
                    dve.tensor_copy(vT[:, :], psO[u][:, :]).then_inc(out_taken, 1)
                    dve.wait_ge(v_turned, b * CPB + u + 1)
                    dve.tensor_copy(g["v_tok"][:, bass.ds(b * TPB + u * TPC, TPC), :], psV[:, :].rearrange("p (t d) -> p t d", t=TPC)).then_inc(v_taken, 1)

            rounds(dve, body)


def attend_wide(nc, m, g):
    SC = float(D) ** -0.5
    qs = m.sb("qs", [P, T])
    probs = [m.sb(f"probs{i}", [P, T]) for i in range(2)]
    turned = [m.sb(f"turned{i}", [P, T]) for i in range(2)]
    mx, nmx, den, rden = m.sb("mx", [P, 2]), m.sb("nmx", [P, 2]), m.sb("den", [P, 2]), m.sb("rden", [P, 2])
    psS = [m.ps(f"psS{i}", [P, T]) for i in range(2)]
    psT = m.ps("psT", [P, 2, CH])
    psY = m.ps("psY", [P, CH])
    q_staged, scored, max_taken, shift_ready = m.sem("q_staged"), m.sem("scored"), m.sem("max_taken"), m.sem("shift_ready")
    exp_done, flipped, valued, added, rden_ready = (m.sem(n) for n in ("exp_done", "flipped", "valued", "added", "rden_ready"))
    flip_taken = [m.sem(f"flip_taken{h}") for h in range(2)]

    def batches(eng, body):
        body(0, True)
        with eng.Fori(1, B) as b:
            body(b, False)

    with nc.Block() as block:

        @block.tensor
        def _(pe):
            def score(b, qb, first):
                n = b * TPB + qb
                if qb == 0:
                    pe.wait_ge(q_staged, b + 1)
                if not first or qb >= 2:
                    pe.wait_ge(exp_done, n - 1)
                for h in range(2):
                    last = pe.matmul(psS[qb % 2][:, h * CH:(h + 1) * CH], qs[:, qb * P:(qb + 1) * P],
                                     g["qkT"][:, 1, bass.ds(b * T + h * CH, CH)], start=True, stop=True)
                last.then_inc(scored, 1)

            def turn(b, qb, first):
                n = b * TPB + qb
                pe.wait_ge(exp_done, n + 1)
                for h in range(2):
                    if not first or qb:
                        pe.wait_ge(flip_taken[h], n)
                    for k in range(4):
                        kb = 4 * h + k
                        last = pe.transpose(psT[:, h, k * P:(k + 1) * P], probs[qb % 2][:, kb * P:(kb + 1) * P], g["identf"][:, :])
                    last.then_inc(flipped, 1)

            def value(b, qb, first):
                n = b * TPB + qb
                if not first or qb:
                    pe.wait_ge(added, n)
                for h in range(2):
                    pe.wait_ge(flip_taken[h], n + 1)
                    for k in range(4):
                        kb = 4 * h + k
                        last = pe.matmul(psY[:, 0:D], turned[qb % 2][:, kb * P:(kb + 1) * P], g["v_tok"][:, b * TPB + kb, :],
                                         start=kb == 0, stop=kb == TPB - 1)
                last.then_inc(valued, 1)

            def body(b, first):
                score(b, 0, first)
                score(b, 1, first)
                for qb in range(TPB):
                    turn(b, qb, first)
                    if qb + 2 < TPB:
                        score(b, qb + 2, first)
                    value(b, qb, first)

            batches(pe, body)

        @block.gpsimd
        def _(pool):
            def body(b, first):
                if not first:
                    pool.wait_ge(scored, b * TPB)
                pool.tensor_copy(qs[:, :], g["qkT"][:, 0, bass.ds(b * T, T)]).then_inc(q_staged, 1)

            batches(pool, body)

        @block.vector
        def _(dve):
            def body(b, first):
                def shift(qb):
                    n = b * TPB + qb
                    p = qb % 2
                    dve.wait_ge(scored, n + 1)
                    dve.tensor_reduce(mx[:, p:p + 1], psS[p][:, :], AXX, ALU.max).then_inc(max_taken, 1)
                    dve.wait_ge(max_taken, n + 1)
                    if not first or qb >= 2:
                        dve.wait_ge(exp_done, n - 1)
                    dve.tensor_scalar(nmx[:, p:p + 1], mx[:, p:p + 1], -SC, None, ALU.mult).then_inc(shift_ready, 1)

                def flip(qb):
                    n = b * TPB + qb
                    dve.wait_ge(flipped, 2 * n + 2)
                    dve.tensor_copy(turned[qb % 2][:, CH:T], psT[:, 1, :]).then_inc(flip_taken[1], 1)

                def finish(qb):
                    n = b * TPB + qb
                    p = qb % 2
                    if not first or qb >= 1:
                        dve.wait_ge(added, n)
                    dve.reciprocal(rden[:, p:p + 1], den[:, p:p + 1]).then_inc(rden_ready, 1)
                    dve.wait_ge(rden_ready, n + 1)
                    dve.wait_ge(valued, n + 1)
                    dve.scalar_tensor_tensor(g["x"][:, b * TPB + qb, :], psY[:, 0:D], rden[:, p:p + 1], g["x"][:, b * TPB + qb, :],
                                             ALU.mult, ALU.add).then_inc(added, 1)

                shift(0)
                shift(1)
                for qb in range(TPB):
                    flip(qb)
                    if qb + 2 < TPB:
                        shift(qb + 2)
                    finish(qb)

            batches(dve, body)

        @block.scalar
        def _(act):
            def body(b, first):
                def exponentials(qb):
                    n = b * TPB + qb
                    p = qb % 2
                    act.wait_ge(shift_ready, n + 1)
                    if not first or qb >= 2:
                        act.wait_ge(flipped, 2 * n - 2)
                        act.wait_ge(rden_ready, n - 1)
                    act.activation(probs[p][:, :], psS[p][:, :], ACT.Exp, bias=nmx[:, p:p + 1], scale=SC,
                                   accum_out=den[:, p:p + 1]).then_inc(exp_done, 1)

                exponentials(0)
                for qb in range(TPB):
                    n = b * TPB + qb
                    act.wait_ge(flipped, 2 * n + 1)
                    if not first or qb >= 2:
                        act.wait_ge(valued, n - 1)
                    act.activation(turned[qb % 2][:, 0:CH], psT[:, 0, :], ACT.Copy).then_inc(flip_taken[0], 1)
                    if qb + 1 < TPB:
                        exponentials(qb + 1)

            batches(act, body)


def finish_layers(nc, m, g, out):
    norm, gather = Norm(m, g["x"]), Gather(nc, m, g)
    att = m.sb("att", [P, 2, TPC, P])
    later_turned, den_whole = m.sem("later_turned"), m.sem("den_whole")
    xT = [m.sb(f"xT{u}", [P, 1 + CH]) for u in range(2)]
    omm = m.sb("omm", [P, 2])
    prev = m.sb("prev", [P, 2, 2, CH])
    mix = m.sb("mix", [P, 2, 2, CH])
    krelu = m.sb("krelu", [P, 2, CH])
    kact = m.sb("kact", [P, 2, CH])
    gate = m.sb("gate", [P, 2, CH])
    gated = m.sb("gated", [P, 2, CH])
    res = m.sb("res", [P, 2, TPC, D])
    psA = m.ps("psA", [P, TPC, D])
    psT = [m.ps(f"psT{u}", [P, CH]) for u in range(2)]
    psK = m.ps("psK", [P, CH])
    psR = [m.ps(f"psR{u}", [P, CH]) for u in range(2)]
    psV = [m.ps(f"psV{u}", [P, CH]) for u in range(2)]
    names = ["att_turned", "added", "transposed", "xT_ready", "edge_ready", "mu_ready", "prev_ready", "mix_ready", "keys_done",
             "relu_done", "kact_ready", "gates_done", "gate_ready", "wide_done", "gated_ready", "out_ready"]
    (att_turned, added, transposed, xT_ready, edge_ready, mu_ready, prev_ready, mix_ready, keys_done,
     relu_done, kact_ready, gates_done, gate_ready, wide_done, gated_ready, out_ready) = (m.sem(n) for n in names)
    out_stored = [m.sem(f"out_stored{u}") for u in range(2)]

    with nc.Block() as block:

        @block.sync
        def _(sp):
            gather.load(sp)
            for c in range(NCH):
                sp.wait_ge(out_ready, c + 1)
                dst = bass.AP(out.tensor, c * (CH * D), [[D, P], [P * D, TPC], [1, D]])
                sp.dma_start(dst, res[:, c % 2, :, :]).then_inc(out_stored[c % 2], 16)
            for u in range(2):
                sp.wait_ge(out_stored[u], 16 * NCH // 2)

        @block.gpsimd
        def _(pool):
            def divide(c, u):
                if u == 0:
                    pool.wait_ge(gather.loaded[c // CPB], 32)
                if c >= 2:
                    pool.wait_ge(att_turned, c - 1)
                gather.divide(pool, c, u, att)

            def squares(c, u):
                pool.wait_ge(relu_done, c + 1)
                if c >= 2:
                    pool.wait_ge(wide_done, c - 1)
                pool.tensor_tensor(kact[:, u, :], krelu[:, u, :], krelu[:, u, :], ALU.mult).then_inc(kact_ready, 1)

            def result(c, u):
                pool.wait_ge(gated_ready, c + 1)
                if c >= 2:
                    pool.wait_ge(out_stored[u], (c // 2) * 16)
                pool.tensor_tensor(res[:, u, :, :], gated[:, u, :].rearrange("p (t d) -> p t d", d=D), g["x"][:, c * TPC:(c + 1) * TPC, :],
                                   ALU.add).then_inc(out_ready, 1)

            for n in range(NCH + 5):
                if n < NCH:
                    divide(n, n % 2)
                if 0 <= n - 4 < NCH:
                    squares(n - 4, n % 2)
                if 0 <= n - 5 < NCH:
                    result(n - 5, (n - 5) % 2)

        @block.vector
        def _(dve):
            dve.tensor_scalar(omm[:, :], g["mu"][:, :], -1.0, 1.0, ALU.mult, ALU.add).then_inc(mu_ready, 1)
            dve.wait_ge(later_turned, 1)
            dve.wait_ge(gather.den_loaded, 16)
            dve.tensor_tensor(gather.den[:, :], gather.den[:, :], psK[:, :], ALU.add).then_inc(den_whole, 1)
            dve.wait_ge(den_whole, 1)
            gather.reciprocals(dve)
            dve.wait_ge(mu_ready, 1)

            def add(c, u):
                xs = g["x"][:, c * TPC:(c + 1) * TPC, :]
                dve.wait_ge(att_turned, c + 1)
                dve.tensor_tensor(xs, psA[:, :, :], xs, ALU.add).then_inc(added, 1)
                dve.wait_ge(added, c + 1)
                norm.statistics(dve, c, u)

            def edge(c, u):
                dve.wait_ge(xT_ready, c + 1)
                if u == 0:
                    if c >= 2:
                        dve.wait_ge(mix_ready, c - 1)
                    dve.memset(xT[0][:, 0:1], 0.0).then_inc(edge_ready, 1)
                else:
                    dve.tensor_copy(xT[1][:, 0:1], xT[0][:, CH:CH + 1]).then_inc(edge_ready, 1)

            def mixes(c, u):
                dve.wait_ge(prev_ready, c + 1)
                if c >= 2:
                    dve.wait_ge(gates_done, c - 1)
                for i in range(2):
                    last = dve.scalar_tensor_tensor(mix[:, u, i, :], xT[u][:, 1:CH + 1], g["mu"][:, i:i + 1], prev[:, u, i, :], ALU.mult, ALU.add)
                last.then_inc(mix_ready, 1)

            def gated_values(c, u):
                dve.wait_ge(gate_ready, c + 1)
                dve.wait_ge(wide_done, c + 1)
                if c >= 2:
                    dve.wait_ge(out_ready, c - 1)
                dve.tensor_tensor(gated[:, u, :], psV[u][:, :], gate[:, u, :], ALU.mult).then_inc(gated_ready, 1)

            for n in range(NCH + 5):
                if 0 <= n - 4 < NCH:
                    mixes(n - 4, n % 2)
                if 0 <= n - 3 < NCH:
                    edge(n - 3, (n - 3) % 2)
                if 0 <= n - 5 < NCH:
                    gated_values(n - 5, (n - 5) % 2)
                if 0 <= n - 2 < NCH:
                    norm.scale(dve, n - 2, n % 2, transposed, n - 2 < 2)
                if 0 <= n - 1 < NCH:
                    add(n - 1, (n - 1) % 2)

        @block.scalar
        def _(act):
            def root(c, u, early):
                norm.take_root(act, c, u)

            def turned(c, u, early):
                act.wait_ge(transposed, c + 1)
                if not early:
                    act.wait_ge(mix_ready, c - 1)
                    act.wait_ge(edge_ready, c)
                act.activation(xT[u][:, 1:1 + CH], psT[u][:, :], ACT.Copy).then_inc(xT_ready, 1)

            def earlier(c, u, early):
                act.wait_ge(edge_ready, c + 1)
                if not early:
                    act.wait_ge(mix_ready, c - 1)
                for i in range(2):
                    last = act.activation(prev[:, u, i, :], xT[u][:, 0:CH], ACT.Copy, scale=omm[:, i:i + 1])
                last.then_inc(prev_ready, 1)

            def gates(c, u, early):
                act.wait_ge(keys_done, c + 1)
                if not early:
                    act.wait_ge(kact_ready, c - 1)
                act.activation(krelu[:, u, :], psK[:, :], ACT.Relu).then_inc(relu_done, 1)
                act.wait_ge(gates_done, c + 1)
                if not early:
                    act.wait_ge(gated_ready, c - 1)
                act.activation(gate[:, u, :], psR[u][:, :], ACT.Sigmoid).then_inc(gate_ready, 1)

            pipeline(act, [(earlier, 3), (gates, 4), (turned, 2), (root, 1)])

        @block.tensor
        def _(pe):
            later = g["later"][:, :, :, :].rearrange("p n t o -> p (n t o)").rearrange("p (r s) -> p s r", s=TPC)
            for s in range(TPC):
                last = pe.transpose(psK[:, s * P:(s + 1) * P], later[:, s, :], g["identf"][:, :])
            last.then_inc(later_turned, 1)

            def untransposed(c, u, early):
                pe.wait_ge(gather.att_ready, c + 1)
                if not (isinstance(c, int) and c == 0):
                    pe.wait_ge(added, c)
                for t in range(TPC):
                    last = pe.transpose(psA[:, t, :], att[:, u, t, :], g["identf"][:, :])
                last.then_inc(att_turned, 1)

            def turn(c, u, early):
                pe.wait_ge(norm.xn_ready, c + 1)
                if not early:
                    pe.wait_ge(xT_ready, c - 1)
                for t in range(TPC):
                    last = pe.transpose(psT[u][:, t * P:(t + 1) * P], norm.xn[:, u, t, :], g["identf"][:, :])
                last.then_inc(transposed, 1)

            def keys(c, u, early):
                pe.wait_ge(mix_ready, c + 1)
                if not (isinstance(c, int) and c == 0):
                    pe.wait_ge(relu_done, c)
                pe.matmul(psK[:, :], g["w_d"][:, 1, :], mix[:, u, 1, :], start=True, stop=True).then_inc(keys_done, 1)
                if not early:
                    pe.wait_ge(gate_ready, c - 1)
                for t in range(TPC):
                    last = pe.matmul(psR[u][:, t * P:(t + 1) * P], mix[:, u, 0, t * P:(t + 1) * P], g["w_d"][:, 0, :], start=True, stop=True)
                last.then_inc(gates_done, 1)

            def wide(c, u, early):
                pe.wait_ge(kact_ready, c + 1)
                if not early:
                    pe.wait_ge(gated_ready, c - 1)
                for t in range(TPC):
                    last = pe.matmul(psV[u][:, t * P:(t + 1) * P], kact[:, u, t * P:(t + 1) * P], g["w_d"][:, 2, :], start=True, stop=True)
                last.then_inc(wide_done, 1)

            pipeline(pe, [(untransposed, 0), (keys, 4), (turn, 2), (wide, 4)])


def build(nc, ins, out, phases=99):
    ctx = ExitStack()
    with ctx:
        gm = Mem(nc, ctx, "g")
        g = {
            "x": gm.sb("x", [P, NT, D]),
            "identf": gm.sb("identf", [P, P]), "identb": gm.sb("identb", [P, P], BF16),
            "w_a": gm.sb("w_a", [P, 4, D]), "w_c": gm.sb("w_c", [P, 3, D]), "w_d": gm.sb("w_d", [P, 3, D]),
            "node_wT": gm.sb("node_wT", [P, FF * NODES]), "node_b": gm.sb("node_b", [P, FF * NODES]),
            "bias_qk": gm.sb("bias_qk", [P, 2]), "bv": gm.sb("bv", [P, D]), "bo": gm.sb("bo", [P, D]),
            "mu": gm.sb("mu", [P, 2]), "b1": gm.sb("b1", [P, FF, HID]),
            "tri": gm.sb("tri", [P, NEAR]), "maskneg": gm.sb("maskneg", [P, P], BF16),
            "masknegT": gm.sb("masknegT", [P, P], BF16),
            "q_dram": nc.dram_tensor("q_parts", [HEADS, B, PARTS, HD, T], BF16, kind="Internal").ap(),
            "k_dram": nc.dram_tensor("k_parts", [HEADS, B, HD, PARTS, T], BF16, kind="Internal").ap(),
            "o_dram": nc.dram_tensor("head_outputs", [HEADS, B, VW, T], F32, kind="Internal").ap(),
            "r_dram": nc.dram_tensor("reciprocals", [HEADS, B, T], F32, kind="Internal").ap(),
            "erow_dram": nc.dram_tensor("bias_rows", [HEADS, ERW], F32, kind="Internal").ap(),
        }

        def phase(tag, f, *args):
            with nc.cleanup_on_exit(), ExitStack() as own:
                f(nc, Mem(nc, own, tag), g, *args)

        g["w1"], g["w2"] = gm.sb("w1", [P, FF, LEAVES * LW]), gm.sb("w2", [P, FF, HID, D])
        g["b2p"] = gm.sb("b2p", [P, PARTS, FF, D], BF16)
        g["leafx"] = gm.sb("leafx", [P, FF * LEAVES * LW], BF16)
        g["selT"] = gm.sb("selT", [P, B * T], BF16)

        with ExitStack() as one:
            m1 = Mem(nc, one, "one")
            g["ebias"] = m1.sb("ebias", [P, HEADS, NEAR])
            g["v_all"] = m1.sb("v_all", [P, HEADS, B * TPB, HD])
            phase("setup", load_weights, ins)
            phase("proj1", project_heads, g["w_a"], True)
            phase("heads1", attend_heads, True)
        if phases < 3:
            return
        with ExitStack() as two:
            m2 = Mem(nc, two, "two")
            g["x_hi"], g["x_lo"] = m2.sb("x_hi", [P, B * T], F32R), m2.sb("x_lo", [P, B * T], F32R)
            g["qkT"], g["v_tok"] = m2.sb("qkT", [P, 2, B * T]), m2.sb("v_tok", [P, NT, D])
            phase("route", add_projected)
            phase("trees", trees)
            phase("wide", attend_wide)
        with ExitStack() as three:
            m3 = Mem(nc, three, "three")
            g["v_all"] = m3.sb("v_all", [P, HEADS, B * TPB, HD])
            g["later"] = m3.sb("later", [P, HEADS * B, TPB // 2, 2])
            phase("proj3", project_heads, g["w_c"], False)
            phase("heads3", attend_heads, False)
            phase("finish", finish_layers, out)


def bucket_onehot():
    import numpy as np

    n = np.arange(P + NEAR) - (P - 1)
    near = np.maximum(n, 0)
    exact = BUCKETS // 2
    ratio = np.log(np.maximum(near, 1).astype(np.float32) / np.float32(exact)) / np.float32(np.log(MAX_DIST / exact))
    large = np.minimum(exact + (ratio * np.float32(BUCKETS - exact)).astype(np.int32), BUCKETS - 1)
    bucket = np.where(near < exact, near, large)
    table = (np.arange(BUCKETS)[:, None] == bucket[None, :]).astype(np.float32)
    table[BUCKETS - 1] -= 1.0
    return table


_INS = ['L0_attn_x', 'L0_attn_Wq', 'L0_attn_bq', 'L0_attn_Wk', 'L0_attn_bk', 'L0_attn_Wv', 'L0_attn_bv', 'L0_attn_Wo',
        'L0_attn_bo', 'L0_attn_rel_emb', 'L0_ffn_q_node_w', 'L0_ffn_q_node_b', 'L0_ffn_q_w1', 'L0_ffn_q_b1',
        'L0_ffn_q_w2', 'L0_ffn_q_b2', 'L0_ffn_k_node_w', 'L0_ffn_k_node_b', 'L0_ffn_k_w1', 'L0_ffn_k_b1',
        'L0_ffn_k_w2', 'L0_ffn_k_b2', 'L0_ffn_v_node_w', 'L0_ffn_v_node_b', 'L0_ffn_v_w1', 'L0_ffn_v_b1',
        'L0_ffn_v_w2', 'L0_ffn_v_b2', 'L1_attn_Wq', 'L1_attn_Wk', 'L1_attn_Wv', 'L1_ffn_W_r', 'L1_ffn_W_k',
        'L1_ffn_W_v', 'L1_ffn_mu_r', 'L1_ffn_mu_k']


def kernel(**inputs):
    import numpy as _np
    import concourse.bacc as _bacc
    from concourse import mybir as _mybir
    from concourse.bass_utils import run_bass_kernel_spmd as _run

    nc = _bacc.Bacc("TRN2", target_bir_lowering=False, num_devices=1)
    arrays, ins = {}, {}
    for name in [*_INS, "bucket_onehot"]:
        a = bucket_onehot() if name == "bucket_onehot" else _np.ascontiguousarray(inputs[name])
        arrays[f"in_{name}"] = a
        ins[name] = nc.dram_tensor(f"in_{name}", a.shape, _mybir.dt.from_np(a.dtype), kind="ExternalInput").ap()
    out = nc.dram_tensor("out_x", (B, T, D), F32, kind="ExternalOutput").ap()
    build(nc, ins, out)
    r = _run(nc, [arrays], core_ids=[0])
    return r.results[0]["out_x"]
```
